# Optimizing a Trainium2 kernel written in Bass

```python
import numpy as np
import jax
import jax.numpy as jnp

def _softmax(x, axis=-1):
    return jax.nn.softmax(x, axis=axis)

def _gelu(x):
    return jax.nn.gelu(x, approximate=True)

def _silu(x):
    return jax.nn.silu(x)

def _sigmoid(x):
    return jax.nn.sigmoid(x)

def _layernorm(x, axis=-1, eps=1e-05):
    m = jnp.mean(x, axis=axis, keepdims=True)
    v = jnp.var(x, axis=axis, keepdims=True)
    return (x - m) / jnp.sqrt(v + eps)

def _scatter_add(tgt, idx, src, axis=0):
    return tgt.at[idx].add(src)

def _segment_sum(src, seg, n):
    return jax.ops.segment_sum(src, seg, n)
kernel_name = 'mk_gps_d1_gnn_r8_c3a2b9'

def setup_inputs(seed: int=0):
    np.random.seed(seed)
    _w = jnp.asarray

    def _rec_inputs():
        import jax
        import jax.numpy as jnp
        _gk = jax.random.key(seed)
        x = -0.0005963 + 1.001 * jax.random.normal(jax.random.fold_in(_gk, 1), (384, 1024), jnp.float32)
        src = jax.random.randint(jax.random.fold_in(_gk, 2), (6144,), 0, 384, jnp.int32)
        dst = jax.random.randint(jax.random.fold_in(_gk, 3), (6144,), 0, 384, jnp.int32)
        _o = jnp.argsort(dst, stable=True)
        src = src[_o]
        dst = dst[_o]
        edge_type_5 = jax.random.randint(jax.random.fold_in(_gk, 12), (6144,), 0, 5, jnp.int32)
        return (x, src, dst, edge_type_5)
    x, src, dst, edge_type_5 = _rec_inputs()

    def _L0_gnn_setup():
        import jax, jax.numpy as jnp
        import numpy as np
        N = 384
        E = 12288
        IN_F = 1024
        OUT_F = 1024
        H = 16
        D = OUT_F // H
        NUM_ETYPES = 4

        def _build_mask(edge_index, edge_type, edge_type_weights, dtype):
            src, dst = (edge_index[0], edge_index[1])
            w = jax.nn.softplus(edge_type_weights)
            mask = jnp.full((N, N), -jnp.inf, dtype=dtype)
            mask = mask.at[src, dst].set(w[edge_type - 1])
            diag = jnp.diagonal(mask)
            idx = jnp.arange(N)
            mask = mask.at[idx, idx].set(jnp.where(jnp.isneginf(diag), w[3], diag))
            return mask
        key = jax.random.key(seed)
        ks = jax.random.split(key, 20)
        p = lambda k, shape: jax.random.normal(k, shape, dtype=jnp.float32) * 0.02
        return {'x': jax.random.normal(ks[0], (N, IN_F), dtype=jnp.float32), 'edge_index': jax.random.randint(ks[1], (2, E), 0, N), 'edge_type': jax.random.randint(ks[2], (E,), 1, NUM_ETYPES + 1), 'edge_type_weights': jnp.ones((NUM_ETYPES,), jnp.float32) + 0.1 * jax.random.normal(ks[3], (NUM_ETYPES,), dtype=jnp.float32), 'wq': p(ks[4], (OUT_F, IN_F)), 'bq': p(ks[5], (OUT_F,)), 'wk': p(ks[6], (OUT_F, IN_F)), 'bk': p(ks[7], (OUT_F,)), 'wv': p(ks[8], (OUT_F, IN_F)), 'bv': p(ks[9], (OUT_F,)), 'wiq': p(ks[10], (OUT_F, OUT_F)), 'biq': p(ks[11], (OUT_F,)), 'wik': p(ks[12], (OUT_F, OUT_F)), 'bik': p(ks[13], (OUT_F,)), 'wiv': p(ks[14], (OUT_F, OUT_F)), 'biv': p(ks[15], (OUT_F,)), 'wo': p(ks[16], (OUT_F, OUT_F)), 'bo': p(ks[17], (OUT_F,))}
    _L0_gnn_all = _L0_gnn_setup()
    _L0_gnn_in = {k: v for k, v in _L0_gnn_all.items() if k in ('edge_type_weights', 'wq', 'bq', 'wk', 'bk', 'wv', 'bv', 'wiq', 'biq', 'wik', 'bik', 'wiv', 'biv', 'wo', 'bo')}
    del _L0_gnn_all

    def _L0_mix_setup():
        import jax, jax.numpy as jnp
        import numpy as np
        B, S, D = (2, 1024, 1024)
        H, HD, FD = (16, 64, 256)
        key = jax.random.key(seed)
        ks = jax.random.split(key, 6)
        sc = 1.0 / np.sqrt(D)
        return {'hidden_states': jax.random.normal(ks[0], (B, S, D), jnp.float32), 'Wq': jax.random.normal(ks[1], (D, D), jnp.float32) * sc, 'Wk': jax.random.normal(ks[2], (D, D), jnp.float32) * sc, 'Wv': jax.random.normal(ks[3], (D, D), jnp.float32) * sc, 'Wo': jax.random.normal(ks[4], (D, D), jnp.float32) * sc, 'Wf': jax.random.normal(ks[5], (FD, HD), jnp.float32) * (1.0 / np.sqrt(HD))}
    _L0_mix_all = _L0_mix_setup()
    _L0_mix_in = {k: v for k, v in _L0_mix_all.items() if k in ('Wq', 'Wk', 'Wv', 'Wo', 'Wf')}
    del _L0_mix_all

    def _L0_ffn_setup():
        import jax, jax.numpy as jnp
        import numpy as np
        B, S, H, E, K = (2, 1024, 1024, 8, 2)
        D = 2 * H
        key = jax.random.key(seed)
        ks = jax.random.split(key, 7)
        x = jax.random.normal(ks[0], (B, S, H), dtype=jnp.float32)
        Wr = jax.random.normal(ks[1], (H, E), dtype=jnp.float32) / np.sqrt(H)
        br = jnp.zeros((E,), dtype=jnp.float32)
        W1 = jax.random.normal(ks[2], (E, H, D), dtype=jnp.float32) / np.sqrt(H)
        b1 = jnp.zeros((E, D), dtype=jnp.float32)
        W2 = jax.random.normal(ks[3], (E, D, H), dtype=jnp.float32) / np.sqrt(D)
        b2 = jnp.zeros((E, H), dtype=jnp.float32)
        return {'x': x, 'Wr': Wr, 'br': br, 'W1': W1, 'b1': b1, 'W2': W2, 'b2': b2}
    _L0_ffn_all = _L0_ffn_setup()
    _L0_ffn_in = {k: v for k, v in _L0_ffn_all.items() if k in ('Wr', 'br', 'W1', 'b1', 'W2', 'b2')}
    del _L0_ffn_all
    return {'x': x, 'src': src, 'dst': dst, 'edge_type_5': edge_type_5, 'L0_gnn_edge_type_weights': _L0_gnn_in['edge_type_weights'], 'L0_gnn_wq': _L0_gnn_in['wq'], 'L0_gnn_bq': _L0_gnn_in['bq'], 'L0_gnn_wk': _L0_gnn_in['wk'], 'L0_gnn_bk': _L0_gnn_in['bk'], 'L0_gnn_wv': _L0_gnn_in['wv'], 'L0_gnn_bv': _L0_gnn_in['bv'], 'L0_gnn_wiq': _L0_gnn_in['wiq'], 'L0_gnn_biq': _L0_gnn_in['biq'], 'L0_gnn_wik': _L0_gnn_in['wik'], 'L0_gnn_bik': _L0_gnn_in['bik'], 'L0_gnn_wiv': _L0_gnn_in['wiv'], 'L0_gnn_biv': _L0_gnn_in['biv'], 'L0_gnn_wo': _L0_gnn_in['wo'], 'L0_gnn_bo': _L0_gnn_in['bo'], 'L0_mix_Wq': _L0_mix_in['Wq'], 'L0_mix_Wk': _L0_mix_in['Wk'], 'L0_mix_Wv': _L0_mix_in['Wv'], 'L0_mix_Wo': _L0_mix_in['Wo'], 'L0_mix_Wf': _L0_mix_in['Wf'], 'L0_ffn_Wr': _L0_ffn_in['Wr'], 'L0_ffn_br': _L0_ffn_in['br'], 'L0_ffn_W1': _L0_ffn_in['W1'], 'L0_ffn_b1': _L0_ffn_in['b1'], 'L0_ffn_W2': _L0_ffn_in['W2'], 'L0_ffn_b2': _L0_ffn_in['b2']}

def reference(x, src, dst, edge_type_5, L0_gnn_edge_type_weights, L0_gnn_wq, L0_gnn_bq, L0_gnn_wk, L0_gnn_bk, L0_gnn_wv, L0_gnn_bv, L0_gnn_wiq, L0_gnn_biq, L0_gnn_wik, L0_gnn_bik, L0_gnn_wiv, L0_gnn_biv, L0_gnn_wo, L0_gnn_bo, L0_mix_Wq, L0_mix_Wk, L0_mix_Wv, L0_mix_Wo, L0_mix_Wf, L0_ffn_Wr, L0_ffn_br, L0_ffn_W1, L0_ffn_b1, L0_ffn_W2, L0_ffn_b2):
    import jax
    import jax.numpy as jnp

    def _L0_gnn_ref(x, edge_index, edge_type, edge_type_weights, wq, bq, wk, bk, wv, bv, wiq, biq, wik, bik, wiv, biv, wo, bo):
        import jax, jax.numpy as jnp
        import numpy as np
        N = 384
        E = 12288
        IN_F = 1024
        OUT_F = 1024
        H = 16
        D = OUT_F // H
        NUM_ETYPES = 4

        def _build_mask(edge_index, edge_type, edge_type_weights, dtype):
            src, dst = (edge_index[0], edge_index[1])
            w = jax.nn.softplus(edge_type_weights)
            mask = jnp.full((N, N), -jnp.inf, dtype=dtype)
            mask = mask.at[src, dst].set(w[edge_type - 1])
            diag = jnp.diagonal(mask)
            idx = jnp.arange(N)
            mask = mask.at[idx, idx].set(jnp.where(jnp.isneginf(diag), w[3], diag))
            return mask
        q = x @ wq.T + bq
        k = x @ wk.T + bk
        v = x @ wv.T + bv
        q2 = (q @ wiq.T + biq).reshape(N, H, D).transpose(1, 0, 2)
        k2 = (k @ wik.T + bik).reshape(N, H, D).transpose(1, 0, 2)
        v2 = (v @ wiv.T + biv).reshape(N, H, D).transpose(1, 0, 2)
        mask = _build_mask(edge_index, edge_type, edge_type_weights, x.dtype)
        scale = 1.0 / np.sqrt(D).astype(np.float32)
        scores = jnp.einsum('hnd,hmd->hnm', q2, k2) * scale + mask[None]
        attn = jax.nn.softmax(scores, axis=-1)
        out = jnp.einsum('hnm,hmd->hnd', attn, v2)
        out = out.transpose(1, 0, 2).reshape(N, OUT_F)
        return out @ wo.T + bo

    def _L0_mix_ref(hidden_states, Wq, Wk, Wv, Wo, Wf):
        import jax, jax.numpy as jnp
        import numpy as np
        B, S, D = (2, 1024, 1024)
        H, HD, FD = (16, 64, 256)
        b, s, _ = hidden_states.shape
        q = (hidden_states @ Wq.T).reshape(b, s, H, HD)
        k = (hidden_states @ Wk.T).reshape(b, s, H, HD)
        v = (hidden_states @ Wv.T).reshape(b, s, H, HD)
        qf = jax.nn.elu(q @ Wf.T) + 1.0
        kf = jax.nn.elu(k @ Wf.T) + 1.0
        kv = jnp.einsum('bshf,bshd->bhfd', kf, v)
        out = jnp.einsum('bshf,bhfd->bshd', qf, kv)
        k_sum = kf.sum(axis=1)
        norm = jnp.einsum('bshf,bhf->bsh', qf, k_sum)[..., None] + 1e-06
        out = (out / norm).reshape(b, s, D)
        return out @ Wo.T

    def _L0_ffn_ref(x, Wr, br, W1, b1, W2, b2):
        import jax, jax.numpy as jnp
        import numpy as np
        B, S, H, E, K = (2, 1024, 1024, 8, 2)
        D = 2 * H
        logits = jnp.einsum('bsh,he->bse', x, Wr) + br
        probs = jax.nn.softmax(logits, axis=-1)
        top_p, top_i = jax.lax.top_k(probs, K)
        cw = jnp.sum(jax.nn.one_hot(top_i, E, dtype=x.dtype) * top_p[..., None], axis=-2)
        h = jax.nn.relu(jnp.einsum('bsh,ehd->bsed', x, W1) + b1)
        y = jnp.einsum('bsed,edh->bseh', h, W2) + b2
        out = jnp.einsum('bseh,bse->bsh', y, cw)
        return out
    edge_index = jnp.stack([src, dst])
    xn = _layernorm(x, axis=-1)
    x = x + _L0_gnn_ref(xn, edge_index, edge_type_5, L0_gnn_edge_type_weights, L0_gnn_wq, L0_gnn_bq, L0_gnn_wk, L0_gnn_bk, L0_gnn_wv, L0_gnn_bv, L0_gnn_wiq, L0_gnn_biq, L0_gnn_wik, L0_gnn_bik, L0_gnn_wiv, L0_gnn_biv, L0_gnn_wo, L0_gnn_bo) + _L0_mix_ref(xn[None], L0_mix_Wq, L0_mix_Wk, L0_mix_Wv, L0_mix_Wo, L0_mix_Wf)[0]
    x = x + _L0_ffn_ref(_layernorm(x, axis=-1)[None], L0_ffn_Wr, L0_ffn_br, L0_ffn_W1, L0_ffn_b1, L0_ffn_W2, L0_ffn_b2)[0]
    return x

_drawn_inputs = setup_inputs


def setup_inputs(seed=0):
    import zlib

    import numpy as np

    out = dict(_drawn_inputs(seed))
    spreads = {'L0_ffn_br': (0.0, 0.1), 'L0_ffn_b1': (0.0, 0.279), 'L0_ffn_b2': (0.0, 0.1)}
    factors = {'L0_gnn_edge_type_weights': 3.919,
     'L0_gnn_bq': 64.0,
     'L0_gnn_bk': 64.0,
     'L0_gnn_bv': 4.33,
     'L0_gnn_biq': 41.579,
     'L0_gnn_bik': 64.0,
     'L0_mix_Wq': 23.874,
     'L0_mix_Wk': 3.578,
     'L0_mix_Wf': 30.423,
     'L0_gnn_wq': 2.705}
    for name, (base, spread) in spreads.items():
        noise = np.random.default_rng([zlib.crc32(name.encode()), seed]).standard_normal(out[name].shape)
        drawn = base * np.exp(spread * noise) if base else spread * noise
        out[name] = jnp.asarray(drawn.astype(out[name].dtype))
    for name, factor in factors.items():
        out[name] = (out[name] * factor).astype(out[name].dtype)
    return out
```

```python
from contextlib import ExitStack

import concourse.bass as bass
from concourse import mybir

F32 = mybir.dt.float32
F32R = mybir.dt.float32r
BF16 = mybir.dt.bfloat16
I32 = mybir.dt.int32
U32 = mybir.dt.uint32
ALU = mybir.AluOpType
ACT = mybir.ActivationFunctionType
AX = mybir.AxisListType

P = 128
N = 384
NT = N // P
DM = 1024
KT = DM // P
H = 16
HD = DM // H
FD = 256
E = 6144
EB = 3
ET = E // P // EB
NE = 8
DF = 2048
FT = DF // P
C = 144
ROUNDS = -(-N // C)
EPS = 1e-5
NEG = -1e30
SCALE = HD ** -0.5

PIECE = KT * P
UNIT = 2 * PIECE
RAW = 4
TURN = 2 * RAW
SPLIT = 4
AHEAD = 3
BANKS = 4
TURNS = 11
LAYER_PIECES = TURNS * TURN
PROJ_PIECES = 9 * TURN
F_TURNS = 2 * FT * KT * P // PIECE // TURN
F_PIECES = F_TURNS * TURN
F_GROUPS = FT + KT
COMBINE_STEPS = 9
EDGE_STEPS = 26
F_BANKS = 12


def build(nc, x, edges, etw, bias, wall, wf, wr, br, wffn, bffn, yrows, out):
    with ExitStack() as ctx:
        def sb(name, shape, dt=F32):
            return ctx.enter_context(nc.sbuf_tensor(name, shape, dt))

        def sem(name):
            return ctx.enter_context(nc.semaphore(name))

        bank = [ctx.enter_context(nc.psum_tensor(f"bank{i}", [P, 512], F32)) for i in range(2 * BANKS)]

        raw = sb("raw", [P, RAW, UNIT])
        whi = sb("whi", [P, SPLIT, PIECE], F32R)
        wlo = sb("wlo", [P, SPLIT, PIECE], F32R)
        x_tok = sb("x_tok", [P, NT, DM])
        a_hi = sb("a_hi", [P, KT * N], F32R)
        a_lo = sb("a_lo", [P, KT * N], F32R)
        t_hi = sb("t_hi", [P, KT * N], F32R)
        t_lo = sb("t_lo", [P, KT * N], F32R)
        dense = sb("dense", [P, 3 * KT, N])
        v_tok = sb("v_tok", [P, NT, H, HD + 1])
        mo = sb("mo", [P, NT * DM])
        mask8 = sb("mask8", [P, NT, N])
        xg = sb("xg", [P, KT, 2, C], F32R)
        pick = sb("pick", [P, NT, C], F32R)
        ident = sb("ident", [P, P])
        later = sb("later", [P, P])
        later16 = sb("later16", [P, P], BF16)
        ones16 = sb("ones16", [P, P], BF16)
        biases = sb("biases", [P, 7 * KT])
        wf_sb = sb("wf_sb", [P, FD])
        wr_sb = sb("wr_sb", [P, KT, NE])
        br_sb = sb("br_sb", [P, NE])
        etw_sb = sb("etw_sb", [P, 4])
        bffn_sb = sb("bffn_sb", [P, NE, F_GROUPS])
        bcur = sb("bcur", [P, F_GROUPS])
        small = sb("small", [P, 160])
        slot_iota = sb("slot_iota", [P, C])
        base_e = sb("base_e", [P, NE])
        eid = sb("eid", [P, NE])
        rt = sb("rt", [P, 12, NT, NE])
        top_i = sb("top_i", [P, NT, 8], U32)
        sel16 = sb("sel16", [P, NT, NE], BF16)
        posi = sb("posi", [P, 2, NT], I32)
        over = sb("over", [P, 1], I32)

        A_hi, A_lo = (a[:, :].rearrange("p (k n) -> p k n", k=KT) for a in (a_hi, a_lo))
        T_hi, T_lo = (a[:, :].rearrange("p (k n) -> p k n", k=KT) for a in (t_hi, t_lo))
        X_hi, X_lo = (a[:, :].rearrange("p (t d) -> p t d", t=NT) for a in (a_hi, a_lo))
        h_hi, h_lo = (a[:, 0:FT * C].rearrange("p (k c) -> p k c", k=FT) for a in (t_hi, t_lo))
        mo_t = mo[:, :].rearrange("p (t d) -> p t d", t=NT)
        dflat = dense[:, :, :].rearrange("p k n -> p (k n)")
        free_d = dflat[:, 2 * KT * N:3 * KT * N]
        qf = [free_d[:, i * 2 * N:(i + 1) * 2 * N].rearrange("p (f n) -> p f n", f=2) for i in range(2)]
        kf = [free_d[:, (2 + i) * 2 * N:(3 + i) * 2 * N].rearrange("p (t f) -> p t f", t=NT) for i in range(2)]
        prob = [free_d[:, i * NT * N:(i + 1) * NT * N].rearrange("p (t n) -> p t n", t=NT) for i in range(2)]
        probT = [mo[:, i * NT * N:(i + 1) * NT * N].rearrange("p (t n) -> p t n", t=NT) for i in range(2)]
        ecol = mo[:, 0:3 * ET]
        ekey = mo[:, 48:48 + ET]
        eval_ = mo[:, 64:64 + ET]
        edup = mo[:, 80:80 + ET]
        epow = mo[:, 96:96 + ET]
        escale = mo[:, 112:113]
        ejunk = mo[:, 128:256]
        kb = mo[:, 256:768].rearrange("p (b n) -> p b n", b=4)
        node_iota = mo[:, 768:768 + N]
        hot_s = mo[:, 1152:1152 + 2 * N].bitcast(BF16).rearrange("p (b n) -> p b n", b=4)
        hot_d = mo[:, 1920:1920 + 2 * N].bitcast(BF16).rearrange("p (b n) -> p b n", b=4)
        ecol_i = mo[:, 2688:2688 + EB * 3 * ET].bitcast(I32).rearrange("p (b c) -> p b c", b=EB)
        zero16 = mo[:, 2832:2832 + N // 2].bitcast(BF16)
        diag = mo[:, 2 * NT * N:2 * NT * N + P]
        kv = [sb(f"kv{i}", [P, 2, HD + 1]) for i in range(2)]
        h_raw = dflat[:, 0:4 * C].rearrange("p (b c) -> p b c", b=4)
        yT = dflat[:, 1024:1024 + KT * C].rearrange("p (k c) -> p k c", k=KT)
        pick_a = dflat[:, 2304:2304 + NT * C].rearrange("p (t c) -> p t c", t=NT)
        y_main = dflat[:, 3072:4096]
        y_rest = dflat[:, 4096:5120]
        yg = [dflat[:, 5120:6144], dflat[:, 6144:7168], dflat[:, 7168:8192],
              dflat[:, 8192:9216], dflat[:, 0:1024], dflat[:, 1024:2048]]

        in_x = sem("in_x")
        in_small = sem("in_small")
        in_edges = sem("in_edges")
        raw_in = [sem(f"raw_in{i}") for i in range(RAW)]
        consts = sem("consts")
        hi_done = sem("hi_done")
        lo_done = sem("lo_done")
        used = sem("used")
        evicted = sem("evicted")
        t_hi_done = sem("t_hi_done")
        t_free = sem("t_free")
        dve_seq = sem("dve_seq")
        act_seq = sem("act_seq")
        var_ready = sem("var_ready")
        std_ready = sem("std_ready")
        xn_ready = sem("xn_ready")
        gp_full = sem("gp_full")
        gp_act = sem("gp_act")
        gp_dve = sem("gp_dve")
        hi_copy = sem("hi_copy")
        a_ready = sem("a_ready")
        ekey_ready = sem("ekey_ready")
        ekey_turned = sem("ekey_turned")
        edup_done = sem("edup_done")
        hots_ready = sem("hots_ready")
        hots_used = sem("hots_used")
        mask_zero = sem("mask_zero")
        mask_read = sem("mask_read")
        sp_abs = sem("sp_abs")
        sp_ln = sem("sp_ln")
        v_ready = sem("v_ready")
        feat_relu = sem("feat_relu")
        feat_exp = sem("feat_exp")
        feat_done = sem("feat_done")
        kv_full = sem("kv_full")
        kv_ready = sem("kv_ready")
        mix_full = sem("mix_full")
        mix_done = sem("mix_done")
        neg_ready = sem("neg_ready")
        exp_done = sem("exp_done")
        prob_ready = sem("prob_ready")
        turned = sem("turned")
        probT_ready = sem("probT_ready")
        av_full = sem("av_full")
        av_hi = sem("av_hi")
        av_done = sem("av_done")
        x2T_ready = sem("x2T_ready")
        xl_ready = sem("xl_ready")
        xl_hi = sem("xl_hi")
        xlT_ready = sem("xlT_ready")
        logits = sem("logits")
        cent = sem("cent")
        rexp = sem("rexp")
        sel_ready = sem("sel_ready")
        ranks = sem("ranks")
        routed = sem("routed")
        b_ready = sem("b_ready")
        pick_ready = sem("pick_ready")
        pick_steps = sem("pick_steps")
        h_split = sem("h_split")
        f_full = sem("f_full")
        f_free = sem("f_free")
        f_evicted = sem("f_evicted")
        hraw_free = sem("hraw_free")
        y_in = sem("y_in")
        y_all = sem("y_all")
        rows_ready = sem("rows_ready")
        combine_steps = sem("combine_steps")
        fetching = sem("fetching")
        got = [sem(f"got{i}") for i in range(2 * NT)]
        fin = sem("fin")
        stored = sem("stored")

        gp_order = [("xnT", i, "act+dve") for i in range(KT)]
        gp_order += [("vT", i, "act") for i in range(2 * NT)]
        gp_order += [("feat", 4 * h + i, "dve") for h in range(H) for i in range(4)]
        gp_order += [("v2T", i, "act") for i in range(2 * NT)]
        gp_order += [("moT", i, "act+dve") for i in range(KT)]
        for h in range(H + 1):
            gp_order += [("score", NT * h + i, "dve") for i in range(NT)] if h < H else []
            gp_order += [("probT", NT * (h - 1) + i, "act") for i in range(NT)] if h else []
        gp_order += [("x2", i, "dve") for i in range(2 * NT)]
        gp_order += [("xlT", i, "act") for i in range(KT)]
        gp_order += [("logit", 0, "dve"), ("rank", 0, "dve")]
        gp = {(name, i): n for n, (name, i, _) in enumerate(gp_order)}
        gp_by = [e.split("+")[-1] for _, _, e in gp_order]

        def gp_bank(name, i):
            return bank[BANKS + gp[name, i] % BANKS]

        def gp_take(eng, name, i):
            n = gp[name, i] - BANKS
            if n >= 0:
                eng.wait_ge(gp_act if gp_by[n] == "act" else gp_dve, gp_by[:n + 1].count(gp_by[n]))

        def gp_wait(eng, name, i):
            eng.wait_ge(gp_full, gp[name, i] + 1)

        def halves(k):
            return raw[:, (k // 2) % RAW, (k % 2) * PIECE:(k % 2 + 1) * PIECE]

        def feature(h, i):
            b = gp_bank("feat", 4 * h + i)
            if i < 2:
                return qf[h % 2][:, i, :], b[:, 0:N]
            if i == 2:
                return kf[h % 2][:, 0:2, :], b[:, :].rearrange("p (t f) -> p t f", t=2)
            return kf[h % 2][:, 2, :], b[:, 0:FD]

        block = ctx.enter_context(nc.Block())

        @block.sync
        def _(sp):
            for t in range(NT):
                sp.dma_start(x_tok[:, t, :], x[t]).then_inc(in_x, 16)
            for dst, src in ((biases[:, :], bias), (wr_sb[:, :, :], wr), (br_sb[:, :], br), (etw_sb[:, :], etw),
                             (wf_sb[0:HD, :], wf), (wf_sb[HD:P, :], wf), (bffn_sb[:, :, :], bffn)):
                sp.dma_start(dst, src).then_inc(in_small, 16)
            with sp.Fori(0, TURNS) as turn:
                for s in range(RAW):
                    sp.wait_ge(lo_done, turn * TURN + 2 * s + 2)
                    sp.dma_start(raw[:, s, :], wall[bass.ds(turn * RAW + s, 1)].rearrange("a p n -> (a p) n")).then_inc(raw_in[s], 16)

            def expert(g, e):
                for q in range(F_TURNS):
                    for s in range(RAW):
                        sp.wait_ge(lo_done, g * F_PIECES + LAYER_PIECES + q * TURN + 2 * s + 2)
                        sp.dma_start(raw[:, s, :], wffn[bass.ds(e * (F_TURNS * RAW) + q * RAW + s, 1)].rearrange("a p n -> (a p) n")).then_inc(raw_in[s], 16)

            with sp.Fori(0, NE) as g:
                expert(g, g)
            sp.wait_ge(routed, 1)
            more = sp.value_load(over[0:1, 0:1])
            with sp.If(more > 0):
                with sp.Fori(1, ROUNDS) as r:
                    with sp.Fori(0, NE) as e:
                        expert(r * NE + e, e)
                sp.wait_ge(fin, NT * ROUNDS)
            for t in range(NT):
                sp.wait_ge(fin, t + 1)
                sp.dma_start(out[t], x_tok[:, t, :]).then_inc(stored, 16)
            sp.wait_ge(stored, 16 * NT)

        @block.gpsimd
        def _(pool):
            pool.memset(ident[:, :], 0.0).then_inc(consts, 1)
            pool.memset(later[:, :], 1.0).then_inc(consts, 1)
            pool.memset(ones16[:, :], 1.0).then_inc(consts, 1)
            pool.wait_ge(consts, 3)
            pool.affine_select(out=ident[:, :], in_=ident[:, :], compare_op=ALU.not_equal, fill=1.0, base=0,
                               pattern=[[-1, P]], channel_multiplier=1).then_inc(consts, 1)
            pool.affine_select(out=later[:, :], in_=later[:, :], compare_op=ALU.is_gt, fill=0.0, base=0,
                               pattern=[[1, P]], channel_multiplier=-1).then_inc(consts, 1)
            pool.wait_ge(consts, 5)
            pool.tensor_copy(later16[:, :], later[:, :]).then_inc(consts, 1)
            pool.iota(slot_iota[:, :], pattern=[[1, C]], base=0, channel_multiplier=0,
                      allow_small_or_imprecise_dtypes=True).then_inc(consts, 1)
            pool.iota(base_e[:, :], pattern=[[C, NE]], base=0, channel_multiplier=0,
                      allow_small_or_imprecise_dtypes=True).then_inc(consts, 1)
            pool.iota(eid[:, :], pattern=[[1, NE]], base=0, channel_multiplier=0,
                      allow_small_or_imprecise_dtypes=True).then_inc(consts, 1)
            pool.memset(v_tok[:, :, :, HD:HD + 1], 1.0).then_inc(consts, 1)
            pool.wait_ge(gp_full, KT)
            pool.iota(node_iota, pattern=[[1, N]], base=0, channel_multiplier=0,
                      allow_small_or_imprecise_dtypes=True).then_inc(consts, 1)
            pool.memset(zero16, 0.0).then_inc(consts, 1)
            for i in range(ET):
                last = pool.memset(epow[:, i:i + 1], 2.0 ** (4 * i - 38))
            last.then_inc(consts, 1)
            pool.memset(escale, 2.0 ** -120).then_inc(consts, 1)
            pool.dma_start(ecol_i, edges).then_inc(in_edges, 16)

            def expert(g, e):
                pool.wait_ge(f_evicted, g * F_GROUPS + BANKS)
                pool.tensor_copy(bcur[:, :], bffn_sb[:, bass.ds(e, 1), :].rearrange("p a g -> p (a g)")).then_inc(b_ready, 1)

            def fetch(r):
                pool.wait_ge(y_all, r + 1)
                pool.wait_ge(rows_ready, r + 1)
                pool.sem_inc(fetching, 1)
                for t in range(NT):
                    for c in range(2):
                        pool.indirect_dma_start(out=yg[2 * t + c], out_offset=None, in_=yrows,
                                                in_offset=bass.IndirectOffsetOnAxis(ap=posi[:, c, t:t + 1].bitcast(U32), axis=0)).then_inc(got[2 * t + c], 16)

            pool.wait_ge(in_small, 16 * 7)
            pool.wait_ge(routed, 1)
            with pool.Fori(0, NE) as g:
                expert(g, g)
            more = pool.value_load(over[0:1, 0:1])
            fetch(0)
            with pool.If(more > 0):
                with pool.Fori(1, ROUNDS) as r:
                    with pool.Fori(0, NE) as e:
                        expert(r * NE + e, e)
                    fetch(r)
        @block.scalar
        def _(act):
            seq = [0]

            def link(ins):
                seq[0] += 1
                ins.then_inc(act_seq, 1)
                act.wait_ge(act_seq, seq[0])

            act.sem_inc(f_evicted, BANKS)

            def hi(turn, k, first):
                if k % 2 == 0:
                    act.wait_ge(raw_in[(k // 2) % RAW], (turn + k // TURN + 1) * 16)
                act.wait_ge(used, first + k + 1)
                act.activation(whi[:, k % SPLIT, :], halves(k), ACT.Copy).then_inc(hi_done, 1)

            act.wait_ge(var_ready, 1)
            act.activation(small[:, 8:8 + NT], small[:, 4:4 + NT], ACT.Sqrt).then_inc(std_ready, 1)
            for k in range(AHEAD):
                hi(0, k, 0)
            for i in range(KT):
                gp_wait(act, "xnT", i)
                act.activation(A_hi[:, i, :], gp_bank("xnT", i)[:, 0:N], ACT.Copy).then_inc(hi_copy, 1)
            with act.Fori(0, EB) as m:
                for j in range(TURN):
                    hi(m, j + AHEAD, m * TURN)
            act.wait_ge(sp_abs, 1)
            link(act.activation(small[:, 40:44], small[:, 36:40], ACT.Exp, scale=-1.0))
            act.activation(small[:, 44:48], small[:, 40:44], ACT.Ln, bias=1.0).then_inc(sp_ln, 1)
            act.wait_ge(consts, 14)
            for i in range(2 * NT):
                gp_wait(act, "vT", i)
                act.activation(v_tok[:, i // 2, H // 2 * (i % 2):H // 2 * (i % 2 + 1), 0:HD],
                               gp_bank("vT", i)[:, :].rearrange("p (h d) -> p h d", d=HD), ACT.Copy).then_inc(gp_act, 1)
            relus = 0
            for h in range(H):
                if h >= 2:
                    act.wait_ge(mix_full, h - 1)
                elif h == 0:
                    act.wait_ge(gp_full, gp["vT", 2 * NT - 1] + 1)
                for i in range(4):
                    dst, src = feature(h, i)
                    gp_wait(act, "feat", 4 * h + i)
                    act.activation(dst, src, ACT.Relu, scale=-1.0).then_inc(feat_relu, 1)
                    relus += 1
                    act.wait_ge(feat_relu, relus)
                    act.activation(dst, dst, ACT.Exp, scale=-1.0).then_inc(feat_exp, 1)
            with act.Fori(0, 3) as m:
                for j in range(TURN):
                    if j == 0:
                        act.wait_ge(t_free, m + 1)
                    act.wait_ge(used, m * (2 * TURN) + EB * TURN + j + 1 + SPLIT)
                    act.activation(T_hi[:, j, :], bank[j % BANKS][:, 0:N], ACT.Identity,
                                   bias=bcur[:, j:j + 1]).then_inc(t_hi_done, 1)
                    hi(m * 2 + EB, j + AHEAD, m * (2 * TURN) + EB * TURN)
                for j in range(TURN):
                    hi(m * 2 + EB + 1, j + AHEAD, m * (2 * TURN) + (EB + 1) * TURN)
            for i in range(2 * NT):
                gp_wait(act, "v2T", i)
                act.activation(v_tok[:, i // 2, H // 2 * (i % 2):H // 2 * (i % 2 + 1), 0:HD],
                               gp_bank("v2T", i)[:, :].rearrange("p (h d) -> p h d", d=HD), ACT.Copy).then_inc(gp_act, 1)
            for i in range(KT):
                gp_wait(act, "moT", i)
                act.activation(A_hi[:, i, :], gp_bank("moT", i)[:, 0:N], ACT.Copy).then_inc(hi_copy, 1)
            for h in range(H + 2):
                if h < H:
                    act.wait_ge(neg_ready, h + 1)
                    for t in range(NT):
                        act.activation(prob[h % 2][:, t, :], prob[h % 2][:, t, :], ACT.Exp,
                                       bias=small[:, 64 + 16 * (h % 2) + t:65 + 16 * (h % 2) + t],
                                       accum_out=small[:, 68 + 16 * (h % 2) + t:69 + 16 * (h % 2) + t]).then_inc(exp_done, 1)
                if 1 <= h <= H:
                    g = h - 1
                    if g >= 2:
                        act.wait_ge(av_full, g - 1)
                    elif g == 0:
                        act.wait_ge(gp_full, gp["moT", KT - 1] + 1)
                    for t in range(NT):
                        gp_wait(act, "probT", NT * g + t)
                        act.activation(probT[g % 2][:, t, :], gp_bank("probT", NT * g + t)[:, 0:N], ACT.Copy).then_inc(gp_act, 1)
                if h >= 2 and h % 2 == 1:
                    c = (h - 2) // 2
                    act.wait_ge(av_full, 2 * c + 2)
                    act.activation(T_hi[:, c, :], bank[c % 2][:, 0:N], ACT.Copy).then_inc(av_hi, 1)
            for i in range(2 * TURN - AHEAD):
                hi(9, i + AHEAD, PROJ_PIECES)
            act.wait_ge(var_ready, 2)
            act.activation(small[:, 8:8 + NT], small[:, 4:4 + NT], ACT.Sqrt).then_inc(std_ready, 1)
            act.wait_ge(xl_ready, 1)
            for i in range(KT):
                gp_wait(act, "xlT", i)
                act.activation(dense[:, i, :], gp_bank("xlT", i)[:, 0:N], ACT.Copy).then_inc(gp_act, 1)
            act.activation(a_hi[:, :], mo[:, :], ACT.Copy).then_inc(xl_hi, 1)
            act.wait_ge(cent, 1)
            act.activation(rt[:, 1], rt[:, 0], ACT.Exp).then_inc(rexp, 1)

            def expert(g, e):
                turn0 = g * F_TURNS + TURNS
                first = g * F_PIECES + LAYER_PIECES
                for k in range(AHEAD):
                    hi_f(turn0, k, first)
                for i in range(KT):
                    act.wait_ge(f_full, g * F_BANKS + i + 1 + BANKS)
                    act.activation(xg[:, i, :, :], bank[BANKS + i % BANKS][:, 0:2 * C].rearrange("p (a c) -> p a c", a=2),
                                   ACT.Copy).then_inc(f_free, 1)
                act.wait_ge(b_ready, g + 1)
                for i in range(FT):
                    act.wait_ge(used, first + i + 1 + SPLIT)
                    act.wait_ge(hraw_free, g * FT + i + 1)
                    act.activation(h_raw[:, i % 4, :], bank[i % BANKS][:, 0:C], ACT.Relu,
                                   bias=bcur[:, i:i + 1]).then_inc(f_evicted, 1)
                    hi_f(turn0, i + AHEAD, first)
                for i in range(KT):
                    act.wait_ge(used, first + FT + 2 * i + 2 + SPLIT)
                    act.activation(yT[:, i, :], bank[i % BANKS][:, 0:C], ACT.Identity,
                                   bias=bcur[:, FT + i:FT + i + 1]).then_inc(f_evicted, 1)
                    for k in range(FT + 2 * i + AHEAD, FT + 2 * i + AHEAD + 2):
                        if k < F_PIECES:
                            hi_f(turn0, k, first)
                act.wait_ge(y_in, g * 32 + 32)
                for i in range(2):
                    act.wait_ge(f_full, g * F_BANKS + KT + 1 + i + BANKS)
                    act.activation(y_main[:, i * 512:(i + 1) * 512], bank[BANKS + i][:, :], ACT.Copy).then_inc(f_free, 1)
                for i in range(2):
                    act.wait_ge(f_full, g * F_BANKS + KT + 3 + i + BANKS)
                    act.activation(y_rest[0:C - P, i * 512:(i + 1) * 512], bank[BANKS + 2 + i][0:C - P, :], ACT.Copy).then_inc(f_free, 1)
                act.wait_ge(f_free, g * F_BANKS + F_BANKS + BANKS)
                act.dma_start(yrows[bass.ds(e * C, P), :], y_main).then_inc(y_in, 16)
                act.dma_start(yrows[bass.ds(e * C + P, C - P), :], y_rest[0:C - P, :]).then_inc(y_in, 16)

            def hi_f(turn0, k, first):
                if k % 2 == 0:
                    act.wait_ge(raw_in[(k // 2) % RAW], (turn0 + k // TURN + 1) * 16)
                act.wait_ge(used, first + k + 1)
                act.activation(whi[:, k % SPLIT, :], halves(k), ACT.Copy).then_inc(hi_done, 1)

            act.sem_inc(f_free, BANKS)
            act.sem_inc(y_in, 32)
            with act.Fori(0, NE) as g:
                expert(g, g)
            act.wait_ge(y_in, NE * 32 + 32)
            act.sem_inc(y_all, 1)
            act.wait_ge(routed, 1)
            more = act.value_load(over[0:1, 0:1])
            with act.If(more > 0):
                with act.Fori(1, ROUNDS) as r:
                    act.wait_ge(fin, NT * r)
                    with act.Fori(0, NE) as e:
                        expert(r * NE + e, e)
                    act.wait_ge(y_in, (r + 1) * (NE * 32) + 32)
                    act.sem_inc(y_all, 1)

        @block.tensor
        def _(pe):
            def piece(k, dst, rhs_hi, rhs_lo, start, stop, n=KT):
                w_hi = whi[:, k % SPLIT, :].rearrange("p (c o) -> p c o", c=n)
                w_lo = wlo[:, k % SPLIT, :].rearrange("p (c o) -> p c o", c=n)
                for c in range(n):
                    pe.matmul(dst, w_hi[:, c, :], rhs_hi[:, c, :], start=(start and c == 0), stop=False)
                    pe.matmul(dst, w_hi[:, c, :], rhs_lo[:, c, :], start=False, stop=False)
                    last = pe.matmul(dst, w_lo[:, c, :], rhs_hi[:, c, :], start=False, stop=(stop and c == n - 1))
                return last

            pe.sem_inc(used, SPLIT)
            pe.wait_ge(consts, 4)
            pe.wait_ge(xn_ready, NT)
            for i in range(KT):
                gp_take(pe, "xnT", i)
                for t in range(NT):
                    last = pe.transpose(gp_bank("xnT", i)[:, t * P:(t + 1) * P], mo_t[:, t, i * P:(i + 1) * P], ident[:, :])
                last.then_inc(gp_full, 1)
            pe.wait_ge(consts, 14)
            pe.wait_ge(a_ready, KT)
            for t in range(NT):
                last = pe.matmul(bank[BANKS + t][:, 0:N], zero16[:, 0:P], zero16, start=True, stop=True)
            with pe.Fori(0, EB) as m:
                for j in range(TURN):
                    pe.wait_ge(lo_done, m * TURN + j + 1 + TURN)
                    pe.wait_ge(evicted, m * TURN + j + 1)
                    piece(j, bank[j % BANKS][:, 0:N], A_hi, A_lo, True, True).then_inc(used, 1)
                    if j < 4:
                        pe.wait_ge(ekey_ready, m * 4 + j + 1)
                        for i in range(4):
                            last = pe.transpose(bank[7][:, i * P:(i + 1) * P], kb[:, i, :], ident[:, :])
                        last.then_inc(ekey_turned, 1)
                    else:
                        pe.wait_ge(hots_ready, m * 4 + j - 3)
                        for i in range(4):
                            for t in range(NT):
                                last = pe.matmul(bank[BANKS + t][:, 0:N], hot_s[:, i, t * P:(t + 1) * P], hot_d[:, i, :],
                                                 start=False, stop=True, skip_group_check=True)
                        last.then_inc(hots_used, 1)
            pe.wait_ge(evicted, EB * TURN + BANKS)
            pe.wait_ge(mask_read, NT)
            for i in range(2 * NT):
                gp_take(pe, "vT", i)
                for c in range(4):
                    last = pe.transpose(gp_bank("vT", i)[:, c * P:(c + 1) * P],
                                        dense[:, 2 * KT + 4 * (i % 2) + c, i // 2 * P:(i // 2 + 1) * P], ident[:, :])
                last.then_inc(gp_full, 1)
            pe.wait_ge(in_small, 16 * 7)
            for h in range(H + 2):
                if h >= 2:
                    g = h - 2
                    pe.wait_ge(kv_ready, g + 1)
                    if g >= 2:
                        pe.wait_ge(mix_done, g - 1)
                    for t in range(NT):
                        for f in range(2):
                            last = pe.matmul(bank[2 + g % 2][:, t * (HD + 1):(t + 1) * (HD + 1)], qf[g % 2][:, f, t * P:(t + 1) * P],
                                             kv[g % 2][:, f, :], start=(f == 0), stop=(f == 1))
                    last.then_inc(mix_full, 1)
                if h < H:
                    lo = HD * (h % 2)
                    for i in range(4):
                        gp_take(pe, "feat", 4 * h + i)
                        b = gp_bank("feat", 4 * h + i)
                        if i < 2:
                            last = pe.matmul(b[:, 0:N], wf_sb[lo:lo + HD, i * P:(i + 1) * P], dense[lo:lo + HD, h // 2, :],
                                             start=True, stop=True)
                        else:
                            for t in range(0, 2) if i == 2 else range(2, 3):
                                last = pe.matmul(b[:, (t % 2) * FD:(t % 2 + 1) * FD], dense[lo:lo + HD, KT + h // 2, t * P:(t + 1) * P],
                                                 wf_sb[lo:lo + HD, :], start=True, stop=True)
                        last.then_inc(gp_full, 1)
                if 1 <= h <= H:
                    g = h - 1
                    pe.wait_ge(feat_done, 4 * g + 4)
                    if g == 0:
                        pe.wait_ge(gp_act, gp_by[:gp["vT", 2 * NT - 1] + 1].count("act"))
                    if g >= 2:
                        pe.wait_ge(kv_ready, g - 1)
                    for f in range(2):
                        for t in range(NT):
                            last = pe.matmul(bank[g % 2][:, f * (HD + 1):(f + 1) * (HD + 1)], kf[g % 2][:, t, f * P:(f + 1) * P],
                                             v_tok[:, t, g, :], start=(t == 0), stop=(t == NT - 1))
                    last.then_inc(kv_full, 1)
            pe.wait_ge(mix_done, H)
            with pe.Fori(0, 3) as m:
                base = m * (2 * TURN) + EB * TURN
                for j in range(2 * TURN):
                    pe.wait_ge(lo_done, base + j + 1 + TURN)
                    pe.wait_ge(evicted, base + (TURN + BANKS if j == TURN else j + 1))
                    src = (A_hi, A_lo) if j < TURN else (T_hi, T_lo)
                    last = piece(j, bank[j % BANKS][:, 0:N], *src, True, True)
                    last.then_inc(used, 1)
            pe.wait_ge(evicted, PROJ_PIECES + BANKS)
            for i in range(2 * NT):
                gp_take(pe, "v2T", i)
                for c in range(4):
                    last = pe.transpose(gp_bank("v2T", i)[:, c * P:(c + 1) * P],
                                        dense[:, 2 * KT + 4 * (i % 2) + c, i // 2 * P:(i // 2 + 1) * P], ident[:, :])
                last.then_inc(gp_full, 1)
            for i in range(KT):
                gp_take(pe, "moT", i)
                for t in range(NT):
                    last = pe.transpose(gp_bank("moT", i)[:, t * P:(t + 1) * P], mo_t[:, t, i * P:(i + 1) * P], ident[:, :])
                last.then_inc(gp_full, 1)
            for h in range(H + 2):
                if h < H:
                    lo = HD * (h % 2)
                    for t in range(NT):
                        gp_take(pe, "score", NT * h + t)
                        pe.matmul(gp_bank("score", NT * h + t)[:, 0:N], dense[lo:lo + HD, h // 2, t * P:(t + 1) * P],
                                  dense[lo:lo + HD, KT + h // 2, :], start=True, stop=True).then_inc(gp_full, 1)
                if h >= 2:
                    g = h - 2
                    c = g // 2
                    lo = HD * (g % 2)
                    pe.wait_ge(gp_act, gp_by[:gp["probT", NT * g + NT - 1] + 1].count("act"))
                    if c >= 2 and g % 2 == 0:
                        pe.wait_ge(av_done, c - 1)
                    for t in range(NT):
                        last = pe.matmul(bank[c % 2][lo:lo + HD, 0:N], v_tok[:, t, g, 0:HD], probT[g % 2][:, t, :],
                                         start=(t == 0), stop=(t == NT - 1))
                    last.then_inc(av_full, 1)
                if 1 <= h <= H:
                    g = h - 1
                    pe.wait_ge(prob_ready, g + 1)
                    for mt in range(NT):
                        gp_take(pe, "probT", NT * g + mt)
                        for t in range(NT):
                            last = pe.transpose(gp_bank("probT", NT * g + mt)[:, t * P:(t + 1) * P],
                                                prob[g % 2][:, t, mt * P:(mt + 1) * P], ident[:, :])
                        last.then_inc(gp_full, 1)
                    last = None
            pe.wait_ge(av_done, KT)
            for i in range(KT):
                k = PROJ_PIECES + 2 * i
                pe.wait_ge(lo_done, k + 1 + TURN)
                pe.wait_ge(evicted, PROJ_PIECES + i + 1)
                piece(2 * i, bank[i % BANKS][:, 0:N], A_hi, A_lo, True, False).then_inc(used, 1)
                pe.wait_ge(lo_done, k + 2 + TURN)
                piece(2 * i + 1, bank[i % BANKS][:, 0:N], T_hi, T_lo, False, True).then_inc(used, 1)
            for i in range(2 * NT):
                gp_take(pe, "x2", i)
                if i == 0:
                    pe.wait_ge(evicted, PROJ_PIECES + KT + BANKS)
                for c in range(4):
                    last = pe.transpose(gp_bank("x2", i)[:, c * P:(c + 1) * P],
                                        dense[:, 4 * (i % 2) + c, i // 2 * P:(i // 2 + 1) * P], ident[:, :])
                last.then_inc(gp_full, 1)
            pe.wait_ge(xl_ready, 1)
            for i in range(KT):
                gp_take(pe, "xlT", i)
                for t in range(NT):
                    last = pe.transpose(gp_bank("xlT", i)[:, t * P:(t + 1) * P], mo_t[:, t, i * P:(i + 1) * P], ident[:, :])
                last.then_inc(gp_full, 1)
            gp_take(pe, "logit", 0)
            pe.wait_ge(gp_act, gp_by[:gp["xlT", KT - 1] + 1].count("act"))
            for t in range(NT):
                for i in range(KT):
                    last = pe.matmul(gp_bank("logit", 0)[:, t * NE:(t + 1) * NE], dense[:, i, t * P:(t + 1) * P], wr_sb[:, i, :],
                                     start=(i == 0), stop=(i == KT - 1))
            last.then_inc(gp_full, 1)
            gp_take(pe, "rank", 0)
            pe.wait_ge(sel_ready, 1)
            for t in range(NT + 1):
                for s in range(min(t + 1, NT)):
                    last = pe.matmul(gp_bank("rank", 0)[:, t * NE:(t + 1) * NE], (later16 if s == t else ones16)[:, :], sel16[:, s, :],
                                     start=(s == 0), stop=(s == min(t, NT - 1)))
            last.then_inc(gp_full, 1)
            pe.wait_ge(xl_hi, 2)
            pe.wait_ge(gp_dve, gp_by.count("dve"))

            def expert(g, e):
                first = g * F_PIECES + LAYER_PIECES
                pe.wait_ge(pick_ready, g + 1)
                for i in range(KT):
                    pe.wait_ge(f_free, g * F_BANKS + i + 1)
                    for a, src in enumerate((X_hi, X_lo)):
                        for t in range(NT):
                            last = pe.matmul(bank[BANKS + i % BANKS][:, a * C:(a + 1) * C], src[:, t, i * P:(i + 1) * P],
                                             pick[:, t, :], start=(t == 0), stop=(t == NT - 1))
                    last.then_inc(f_full, 1)
                pe.wait_ge(f_free, g * F_BANKS + KT + BANKS)
                for i in range(FT):
                    pe.wait_ge(lo_done, first + i + 1 + TURN)
                    pe.wait_ge(f_evicted, g * F_GROUPS + i + 1)
                    piece(i, bank[i % BANKS][:, 0:C], xg[:, :, 0, :], xg[:, :, 1, :], True, True).then_inc(used, 1)
                pe.wait_ge(hraw_free, g * FT + FT + BANKS)
                for i in range(KT):
                    pe.wait_ge(f_evicted, g * F_GROUPS + FT + i + 1)
                    for a in range(2):
                        k = FT + 2 * i + a
                        pe.wait_ge(lo_done, first + k + 1 + TURN)
                        piece(k, bank[i % BANKS][:, 0:C], h_hi[:, a * KT:(a + 1) * KT, :], h_lo[:, a * KT:(a + 1) * KT, :],
                              a == 0, a == 1).then_inc(used, 1)
                for part, cols in enumerate((slice(0, P), slice(P, C))):
                    rows = cols.stop - cols.start
                    for i in range(2):
                        n = KT + 2 * part + i
                        pe.wait_ge(f_evicted, g * F_GROUPS + FT + 4 * i + 4 + BANKS)
                        pe.wait_ge(f_free, g * F_BANKS + n + 1)
                        for c in range(4):
                            last = pe.transpose(bank[BANKS + n % BANKS][0:rows, c * P:(c + 1) * P], yT[:, 4 * i + c, cols], ident[:, :])
                        last.then_inc(f_full, 1)

            pe.sem_inc(f_full, BANKS)
            with pe.Fori(0, NE) as g:
                expert(g, g)
            pe.wait_ge(routed, 1)
            more = pe.value_load(over[0:1, 0:1])
            with pe.If(more > 0):
                with pe.Fori(1, ROUNDS) as r:
                    with pe.Fori(0, NE) as e:
                        expert(r * NE + e, e)

        @block.vector
        def _(dve):
            seq = [0]

            def link(ins):
                seq[0] += 1
                ins.then_inc(dve_seq, 1)
                dve.wait_ge(dve_seq, seq[0])

            dve.sem_inc(lo_done, TURN)
            dve.sem_inc(evicted, BANKS)
            dve.sem_inc(hraw_free, BANKS)

            def lo(k, first):
                dve.wait_ge(hi_done, first + k + 1)
                dve.tensor_tensor(wlo[:, k % SPLIT, :], halves(k), whi[:, k % SPLIT, :].bitcast(F32), ALU.subtract).then_inc(lo_done, 1)

            def normalize(n):
                mv = small[:, 12:12 + 2 * NT].rearrange("p (t a) -> p t a", a=2)
                st = small[:, 96:96 + 12 * NT].rearrange("p (t a b) -> p t a b", a=2, b=6)
                for t in range(NT):
                    if n == 0:
                        dve.wait_ge(in_x, 16 * NT)
                    for a in range(2):
                        last = dve.bn_stats(st[:, t, a, :], x_tok[:, t, a * 512:(a + 1) * 512])
                link(last)
                for t in range(NT):
                    last = dve.bn_aggr(mv[:, t, :], st[:, t, :, :].rearrange("p a b -> p (a b)"))
                link(last)
                dve.tensor_scalar(small[:, 4:4 + NT], mv[:, :, 1], EPS, None, ALU.add).then_inc(var_ready, 1)
                dve.wait_ge(std_ready, n + 1)
                r = small[:, 0:NT]
                v = small[:, 4:4 + NT]
                w = small[:, 8:8 + NT]
                link(dve.reciprocal(r, w))
                link(dve.tensor_tensor(w, r, r, ALU.mult))
                link(dve.tensor_tensor(w, w, v, ALU.mult))
                link(dve.tensor_scalar(w, w, -0.5, 1.5, ALU.mult, ALU.add))
                link(dve.tensor_tensor(r, r, w, ALU.mult))
                for t in range(NT):
                    ins = dve.tensor_scalar(mo_t[:, t, :], x_tok[:, t, :], mv[:, t, 0:1], small[:, t:t + 1], ALU.subtract, ALU.mult)
                    if n == 0:
                        ins.then_inc(xn_ready, 1)
                if n == 1:
                    ins.then_inc(xl_ready, 1)

            normalize(0)
            for i in range(KT):
                dve.wait_ge(hi_copy, i + 1)
                dve.tensor_tensor(A_lo[:, i, :], gp_bank("xnT", i)[:, 0:N], A_hi[:, i, :].bitcast(F32), ALU.subtract)\
                   .then_inc(gp_dve, 1)
            dve.wait_ge(gp_dve, KT)
            dve.sem_inc(a_ready, KT)
            for k in range(AHEAD):
                lo(k, 0)
            dve.wait_ge(consts, 14)
            dve.wait_ge(in_small, 16 * 7)
            dve.wait_ge(in_edges, 16)
            with dve.Fori(0, EB) as m:
                es, ed, ety = ecol[:, 0:ET], ecol[:, ET:2 * ET], ecol[:, 2 * ET:3 * ET]
                steps = [0]

                def step(ins):
                    steps[0] += 1
                    ins.then_inc(edup_done, 1)
                    dve.wait_ge(edup_done, m * EDGE_STEPS + steps[0])

                for j in range(TURN):
                    if j == 0:
                        step(dve.tensor_copy(ecol, ecol_i[:, bass.ds(m, 1), :].rearrange("p a c -> p (a c)")))
                        step(dve.tensor_scalar(ekey, es, float(N), None, ALU.mult))
                        step(dve.tensor_tensor(ekey, ekey, ed, ALU.add))
                        step(dve.tensor_scalar(eval_, ety, 0.0, 4.0, ALU.is_equal, ALU.mult))
                        step(dve.tensor_tensor(eval_, eval_, ety, ALU.add))
                        step(dve.tensor_tensor(eval_, eval_, epow, ALU.mult))
                        step(dve.tensor_scalar(escale, escale, 2.0 ** (4 * ET), None, ALU.mult))
                        step(dve.tensor_scalar(eval_, eval_, escale, None, ALU.mult))
                    if j < 4:
                        for i in range(4):
                            last = dve.tensor_copy(kb[:, i, :], ekey[:, 4 * j + i:4 * j + i + 1].to_broadcast([P, P]))
                        last.then_inc(ekey_ready, 1)
                    else:
                        if j > 4:
                            dve.wait_ge(hots_used, m * 4 + j - 4)
                        for i in range(4):
                            c = 4 * (j - 4) + i
                            dve.tensor_scalar(hot_s[:, i, :], node_iota, es[:, c:c + 1], None, ALU.is_equal)
                            last = dve.tensor_scalar(hot_d[:, i, :], node_iota, ed[:, c:c + 1], eval_[:, c:c + 1], ALU.is_equal, ALU.mult)
                        last.then_inc(hots_ready, 1)
                    dve.wait_ge(used, m * TURN + j + 1 + SPLIT)
                    dve.tensor_copy(dense[:, bass.ds(m * KT + j, 1), :].rearrange("p a n -> p (a n)"), bank[j % BANKS][:, 0:N]).then_inc(evicted, 1)
                    lo(j + AHEAD, m * TURN)
                    if j < 4:
                        dve.wait_ge(ekey_turned, m * 4 + j + 1)
                        for i in range(4):
                            c = 4 * j + i
                            step(dve.scalar_tensor_tensor(out=ejunk, in0=bank[7][:, i * P:(i + 1) * P], scalar=ekey[:, c:c + 1],
                                                          in1=later[:, :], op0=ALU.is_equal, op1=ALU.mult, accum_out=edup[:, c:c + 1]))
                    if j == 3:
                        step(dve.tensor_scalar(edup, edup, 0.0, None, ALU.is_equal))
                        step(dve.tensor_tensor(eval_, eval_, edup, ALU.mult))
                dve.wait_ge(hots_used, m * 4 + 4)
                assert steps[0] == EDGE_STEPS, steps[0]

            neg, ab, ln = small[:, 32:36], small[:, 36:40], small[:, 44:48]
            link(dve.tensor_scalar(neg, etw_sb[:, :], -1.0, None, ALU.mult))
            dve.tensor_tensor(ab, neg, etw_sb[:, :], ALU.max).then_inc(sp_abs, 1)
            pos_w = small[:, 132:136]
            link(dve.tensor_scalar(pos_w, etw_sb[:, :], 0.0, None, ALU.max))
            table = mo[:, 0:NT * N].rearrange("p (t n) -> p t n", t=NT)
            tab = mo[:, 0:NT * N]
            for t in range(NT):
                dve.tensor_copy(table[:, t, :], bank[BANKS + t][:, 0:N]).then_inc(mask_read, 1)
            dve.wait_ge(mask_read, NT)
            tmp = mo[:, NT * N:2 * NT * N]
            link(dve.tensor_scalar(tmp.bitcast(I32), tab.bitcast(I32), 22, 7, ALU.logical_shift_right, ALU.bitwise_and))
            link(dve.tensor_copy(tab, tmp.bitcast(I32)))
            for t in range(NT):
                d = table[:, t, t * P:(t + 1) * P]
                link(dve.tensor_scalar(diag, d, 0.0, 6.0, ALU.is_equal, ALU.mult))
                link(dve.tensor_tensor(diag, diag, ident[:, :], ALU.mult))
                link(dve.tensor_tensor(d, d, diag, ALU.add))
            dve.wait_ge(sp_ln, 1)
            link(dve.tensor_tensor(ln, ln, pos_w, ALU.add))
            link(dve.tensor_scalar(ln, ln, 1.0 / SCALE, None, ALU.mult))
            m8 = mask8[:, :, :].rearrange("p t n -> p (t n)")
            link(dve.tensor_scalar(m8, tab, 0.0, NEG, ALU.is_equal, ALU.mult))
            for code, w in ((2.0, 0), (4.0, 1), (5.0, 2), (6.0, 3)):
                link(dve.tensor_scalar(tmp, tab, code, small[:, 44 + w:45 + w], ALU.is_equal, ALU.mult))
                link(dve.tensor_tensor(m8, m8, tmp, ALU.add))

            for h in range(H + 2):
                if h >= 2:
                    g = h - 2
                    o = bank[2 + g % 2][:, 0:NT * (HD + 1)].rearrange("p (t d) -> p t d", t=NT)
                    rn = small[:, 48:48 + NT].rearrange("p (t a) -> p t a", a=1)
                    dve.wait_ge(mix_full, g + 1)
                    link(dve.tensor_scalar(rn, o[:, :, HD:HD + 1], 1e-6, None, ALU.add))
                    link(dve.reciprocal(rn, rn))
                    dve.tensor_tensor(mo_t[:, :, g * HD:(g + 1) * HD], o[:, :, 0:HD], rn.to_broadcast([P, NT, HD]), ALU.mult)\
                       .then_inc(mix_done, 1)
                if h < H:
                    for i in range(4):
                        dst, src = feature(h, i)
                        dve.wait_ge(feat_exp, 4 * h + i + 1)
                        dve.scalar_tensor_tensor(out=dst, in0=src, scalar=0.0, in1=dst, op0=ALU.max, op1=ALU.add).then_inc(gp_dve, 1)
                    dve.wait_ge(gp_dve, gp_by[:gp["feat", 4 * h + 3] + 1].count("dve"))
                    dve.sem_inc(feat_done, 4)
                if 1 <= h <= H:
                    g = h - 1
                    dve.wait_ge(kv_full, g + 1)
                    if g >= 2:
                        dve.wait_ge(mix_full, g - 1)
                    dve.tensor_copy(kv[g % 2][:, :, :].rearrange("p f d -> p (f d)"), bank[g % 2][:, 0:2 * (HD + 1)]).then_inc(kv_ready, 1)

            with dve.Fori(0, 3) as m:
                base = m * (2 * TURN) + EB * TURN
                dve.wait_ge(evicted, base + BANKS)
                dve.tensor_copy(bcur[:, 0:2 * KT], biases[:, bass.ds(m * (2 * KT), 2 * KT)]).then_inc(t_free, 1)
                dve.wait_ge(t_free, m + 1)
                for j in range(TURN):
                    dve.wait_ge(t_hi_done, m * TURN + j + 1)
                    dve.scalar_tensor_tensor(out=T_lo[:, j, :], in0=bank[j % BANKS][:, 0:N], scalar=bcur[:, j:j + 1],
                                             in1=T_hi[:, j, :].bitcast(F32), op0=ALU.add, op1=ALU.subtract).then_inc(evicted, 1)
                    lo(j + AHEAD, base)
                for j in range(TURN):
                    dve.wait_ge(used, base + TURN + j + 1 + SPLIT)
                    dve.tensor_scalar(dense[:, bass.ds(m * KT + j, 1), :].rearrange("p a n -> p (a n)"), bank[j % BANKS][:, 0:N],
                                      bcur[:, KT + j:KT + j + 1], None, ALU.add).then_inc(evicted, 1)
                    lo(j + AHEAD, base + TURN)
            for i in range(KT):
                dve.wait_ge(hi_copy, KT + i + 1)
                dve.tensor_tensor(A_lo[:, i, :], gp_bank("moT", i)[:, 0:N], A_hi[:, i, :].bitcast(F32), ALU.subtract)\
                   .then_inc(gp_dve, 1)
            for h in range(H + 3):
                if h < H:
                    s = 64 + 16 * (h % 2)
                    if h == 0:
                        dve.wait_ge(gp_full, gp["v2T", 2 * NT - 1] + 1)
                    if h >= 2:
                        dve.wait_ge(gp_full, gp["probT", NT * (h - 2) + NT - 1] + 1)
                    for t in range(NT):
                        gp_wait(dve, "score", NT * h + t)
                        dve.tensor_tensor_reduce(out=prob[h % 2][:, t, :], in0=gp_bank("score", NT * h + t)[:, 0:N], in1=mask8[:, t, :],
                                                 scale=SCALE, scalar=-3e38, op0=ALU.add, op1=ALU.max,
                                                 accum_out=small[:, s + 8 + t:s + 9 + t]).then_inc(gp_dve, 1)
                    dve.wait_ge(gp_dve, gp_by[:gp["score", NT * h + NT - 1] + 1].count("dve"))
                    dve.tensor_scalar(small[:, s:s + NT], small[:, s + 8:s + 8 + NT], -1.0, None, ALU.mult).then_inc(neg_ready, 1)
                if 1 <= h <= H:
                    g = h - 1
                    s = 64 + 16 * (g % 2)
                    dve.wait_ge(exp_done, NT * g + NT)
                    link(dve.reciprocal(small[:, s + 12:s + 12 + NT], small[:, s + 4:s + 4 + NT]))
                    for t in range(NT):
                        last = dve.tensor_scalar(prob[g % 2][:, t, :], prob[g % 2][:, t, :], small[:, s + 12 + t:s + 13 + t], None, ALU.mult)
                    last.then_inc(prob_ready, 1)
                if h >= 3 and h % 2 == 1:
                    c = (h - 3) // 2
                    dve.wait_ge(av_hi, c + 1)
                    dve.tensor_tensor(T_lo[:, c, :], bank[c % 2][:, 0:N], T_hi[:, c, :].bitcast(F32), ALU.subtract).then_inc(av_done, 1)
            for i in range(KT):
                dve.wait_ge(used, PROJ_PIECES + 2 * i + 2 + SPLIT)
                dve.tensor_scalar(dense[:, i, :], bank[i % BANKS][:, 0:N], biases[:, 6 * KT + i:6 * KT + i + 1], None, ALU.add)\
                   .then_inc(evicted, 1)
                for k in range(2 * i + AHEAD, 2 * i + AHEAD + 2):
                    if k < 2 * TURN:
                        lo(k, PROJ_PIECES)
            for i in range(2 * NT):
                gp_wait(dve, "x2", i)
                r = x_tok[:, i // 2, (i % 2) * 512:(i % 2 + 1) * 512]
                dve.tensor_tensor(r, gp_bank("x2", i)[:, :], r, ALU.add).then_inc(gp_dve, 1)
            dve.wait_ge(gp_dve, gp_by[:gp["x2", 2 * NT - 1] + 1].count("dve"))
            normalize(1)
            gp_wait(dve, "logit", 0)
            lg = gp_bank("logit", 0)[:, 0:NT * NE].rearrange("p (t e) -> p t e", t=NT)
            cen, ex, prb, srt, sel0, sel1, pos, tm = (rt[:, i] for i in range(8))
            mx = small[:, 52:52 + NT].rearrange("p (t a) -> p t a", a=1)
            brb = br_sb[:, :].rearrange("p (a e) -> p a e", a=1).to_broadcast([P, NT, NE])
            dve.tensor_tensor(cen, lg, brb, ALU.add).then_inc(gp_dve, 1)
            dve.wait_ge(gp_dve, gp_by[:gp["logit", 0] + 1].count("dve"))
            link(dve.tensor_reduce(mx, cen, AX.X, ALU.max))
            dve.tensor_tensor(cen, cen, mx.to_broadcast([P, NT, NE]), ALU.subtract).then_inc(cent, 1)
            dve.wait_ge(rexp, 1)
            link(dve.tensor_reduce(mx, ex, AX.X, ALU.add))
            link(dve.reciprocal(mx, mx))
            link(dve.tensor_tensor(prb, ex, mx.to_broadcast([P, NT, NE]), ALU.mult))
            for t in range(NT):
                link(dve.max(srt[:, t, :], prb[:, t, :]))
                link(dve.max_index(top_i[:, t, :], srt[:, t, :], prb[:, t, :]))
            ti = rt[:, 8]
            link(dve.tensor_copy(ti, top_i[:, :, :]))
            ide = eid[:, :].rearrange("p (a e) -> p a e", a=1).to_broadcast([P, NT, NE])
            link(dve.tensor_tensor(sel0, ide, ti[:, :, 0:1].to_broadcast([P, NT, NE]), ALU.is_equal))
            link(dve.tensor_tensor(sel1, ide, ti[:, :, 1:2].to_broadcast([P, NT, NE]), ALU.is_equal))
            dve.tensor_tensor(sel16[:, :, :], sel0, sel1, ALU.add).then_inc(sel_ready, 1)
            gp_wait(dve, "rank", 0)
            rk = gp_bank("rank", 0)[:, 0:NT * NE].rearrange("p (t e) -> p t e", t=NT)
            link(dve.tensor_scalar(pos, rk, float(C), float((NE - 1) * C), ALU.is_ge, ALU.mult))
            for r in range(2, ROUNDS):
                link(dve.tensor_scalar(tm, rk, float(C * r), float((NE - 1) * C), ALU.is_ge, ALU.mult))
                link(dve.tensor_tensor(pos, pos, tm, ALU.add))
            link(dve.tensor_tensor(pos, pos, rk, ALU.add))
            link(dve.tensor_tensor(pos, pos, base_e[:, :].rearrange("p (a e) -> p a e", a=1).to_broadcast([P, NT, NE]), ALU.add))
            posf = small[:, 56:56 + 2 * NT].rearrange("p (c t) -> p c t", c=2)
            for c, s in enumerate((sel0, sel1)):
                link(dve.tensor_tensor(tm, pos, s, ALU.mult))
                link(dve.tensor_reduce(posf[:, c, :].rearrange("p (t a) -> p t a", a=1), tm, AX.X, ALU.add))
            link(dve.tensor_copy(small[:, 136:136 + 2 * NT], small[:, 56:56 + 2 * NT]))
            cnt = small[:, 62:63]
            dve.tensor_reduce(cnt, gp_bank("rank", 0)[:, NT * NE:(NT + 1) * NE], AX.X, ALU.max).then_inc(gp_dve, 1)
            dve.wait_ge(gp_dve, gp_by.count("dve"))
            dve.tensor_scalar(over[:, :], cnt, float(C), None, ALU.is_gt).then_inc(routed, 1)
            dve.wait_ge(xl_hi, 1)
            dve.tensor_tensor(a_lo[:, :], mo[:, :], a_hi[:, :].bitcast(F32), ALU.subtract).then_inc(xl_hi, 1)

            def expert(g, e):
                first = g * F_PIECES + LAYER_PIECES
                dve.wait_ge(f_full, g * F_BANKS + BANKS)
                for t in range(NT):
                    dve.tensor_scalar(pick_a[:, t, :], slot_iota[:, :], small[:, 56 + t:57 + t], None, ALU.is_equal).then_inc(pick_steps, 1)
                dve.wait_ge(pick_steps, g * (NT + 1) + NT)
                for t in range(NT):
                    last = dve.scalar_tensor_tensor(out=pick[:, t, :], in0=slot_iota[:, :], scalar=small[:, 59 + t:60 + t],
                                                    in1=pick_a[:, t, :], op0=ALU.is_equal, op1=ALU.add)
                last.then_inc(pick_ready, 1)
                dve.wait_ge(pick_ready, g + 1)
                dve.tensor_scalar(slot_iota[:, :], slot_iota[:, :], float(C), None, ALU.add).then_inc(pick_steps, 1)
                for k in range(AHEAD):
                    lo(k, first)
                for i in range(FT):
                    dve.wait_ge(f_evicted, g * F_GROUPS + i + 1 + BANKS)
                    if i == 0:
                        dve.wait_ge(used, first + SPLIT)
                    dve.tensor_copy(h_hi[:, i, :], h_raw[:, i % 4, :]).then_inc(h_split, 1)
                    dve.wait_ge(h_split, g * FT + i + 1)
                    dve.tensor_tensor(h_lo[:, i, :], h_raw[:, i % 4, :], h_hi[:, i, :].bitcast(F32), ALU.subtract).then_inc(hraw_free, 1)
                    lo(i + AHEAD, first)
                for k in range(FT + AHEAD, F_PIECES):
                    lo(k, first)
                dve.wait_ge(pick_steps, (g + 1) * (NT + 1))

            round_pos = small[:, 136:136 + 2 * NT]
            below = small[:, 142:142 + 2 * NT]
            here = small[:, 148:148 + 2 * NT]
            weight = small[:, 154:154 + 2 * NT]

            def combine(r):
                steps = [0]

                def step(ins):
                    steps[0] += 1
                    ins.then_inc(combine_steps, 1)
                    dve.wait_ge(combine_steps, r * COMBINE_STEPS + steps[0])

                step(dve.tensor_scalar(below, round_pos, float(NE * C), None, ALU.is_lt))
                step(dve.tensor_scalar(here, round_pos, 0.0, None, ALU.is_ge))
                step(dve.tensor_tensor(here, here, below, ALU.mult))
                step(dve.tensor_tensor(below, round_pos, here, ALU.mult))
                dve.tensor_copy(posi[:, :, :], below.rearrange("p (c t) -> p c t", c=2)).then_inc(rows_ready, 1)
                step(dve.tensor_tensor(weight.rearrange("p (c t) -> p c t", c=2), here.rearrange("p (c t) -> p c t", c=2),
                                       rt[:, 3, :, 0:2].rearrange("p t c -> p c t"), ALU.mult))
                step(dve.tensor_scalar(round_pos, round_pos, float(-NE * C), None, ALU.add))
                for t in range(NT):
                    for c in range(2):
                        dve.wait_ge(got[2 * t + c], 16 * r + 16)
                        ins = dve.scalar_tensor_tensor(out=x_tok[:, t, :], in0=yg[2 * t + c], scalar=weight[:, c * NT + t:c * NT + t + 1],
                                                       in1=x_tok[:, t, :], op0=ALU.mult, op1=ALU.add)
                        if c == 0:
                            step(ins)
                    ins.then_inc(fin, 1)
                dve.wait_ge(fin, NT * r + NT)
                assert steps[0] == COMBINE_STEPS, steps[0]

            with dve.Fori(0, NE) as g:
                expert(g, g)
            combine(0)
            more = dve.value_load(over[0:1, 0:1])
            with dve.If(more > 0):
                with dve.Fori(1, ROUNDS) as r:
                    with dve.Fori(0, NE) as e:
                        expert(r * NE + e, e)
                    combine(r)


def kernel(**inputs):
    import numpy as np
    import concourse.bacc as bacc
    from concourse.bass_utils import run_bass_kernel_spmd

    a = {k: np.asarray(v) for k, v in inputs.items()}

    def pieces(w):
        return w.reshape(KT, P, KT, P).transpose(0, 3, 2, 1).reshape(KT, P, PIECE)

    def units(p):
        return p.reshape(-1, 2, P, PIECE).transpose(0, 2, 1, 3).reshape(-1, P, UNIT)

    def columns(v):
        return v.reshape(-1, P).T

    g = {k[7:]: v for k, v in a.items() if k.startswith("L0_gnn_")}
    first = [a["L0_mix_Wq"], a["L0_mix_Wk"], a["L0_mix_Wv"], g["wq"], g["wiq"], g["wk"], g["wik"], g["wv"], g["wiv"]]
    last = np.stack([pieces(a["L0_mix_Wo"]), pieces(g["wo"])], axis=1).reshape(2 * KT, P, PIECE)
    wall = units(np.concatenate([pieces(w) for w in first] + [last]))
    w1 = a["L0_ffn_W1"].reshape(NE, KT, P, FT, P).transpose(0, 3, 2, 1, 4).reshape(NE, FT, P, PIECE)
    w2 = a["L0_ffn_W2"].reshape(NE, 2, KT, P, KT, P).transpose(0, 4, 1, 3, 2, 5).reshape(NE, 2 * KT, P, PIECE)
    wffn = units(np.concatenate([w1, w2], axis=1).reshape(-1, P, PIECE))
    edges = np.stack([v.reshape(EB, ET, P) for v in (a["src"], a["dst"], a["edge_type_5"])], axis=1)
    arrays = {
        "x": a["x"].reshape(NT, P, DM),
        "edges": edges.reshape(EB, 3 * ET, P).transpose(2, 0, 1),
        "etw": np.broadcast_to(g["edge_type_weights"], (P, 4)),
        "bias": np.concatenate([columns(g[n]) for n in ("bq", "biq", "bk", "bik", "bv", "biv", "bo")], axis=1),
        "wall": wall,
        "wf": a["L0_mix_Wf"].T,
        "wr": a["L0_ffn_Wr"].reshape(KT, P, NE).transpose(1, 0, 2),
        "br": np.broadcast_to(a["L0_ffn_br"], (P, NE)),
        "wffn": wffn,
        "bffn": np.concatenate([a["L0_ffn_b1"].reshape(NE, FT, P), a["L0_ffn_b2"].reshape(NE, KT, P)], axis=1).transpose(2, 0, 1),
    }
    arrays = {f"in_{k}": np.ascontiguousarray(v) for k, v in arrays.items()}
    nc = bacc.Bacc("TRN2", target_bir_lowering=False, num_devices=1)
    aps = {k[3:]: nc.dram_tensor(k, v.shape, mybir.dt.from_np(v.dtype), kind="ExternalInput").ap() for k, v in arrays.items()}
    yrows = nc.dram_tensor("yrows", (NE * C, DM), F32, kind="Internal").ap()
    out = nc.dram_tensor("out", (NT, P, DM), F32, kind="ExternalOutput").ap()
    build(nc, **aps, yrows=yrows, out=out)
    r = run_bass_kernel_spmd(nc, [arrays], core_ids=[0])
    return r.results[0]["out"].reshape(N, DM)
```

```python
from contextlib import ExitStack

import concourse.bass as bass
from concourse import mybir

F32 = mybir.dt.float32
F32R = mybir.dt.float32r
BF16 = mybir.dt.bfloat16
I32 = mybir.dt.int32
U32 = mybir.dt.uint32
ALU = mybir.AluOpType
ACT = mybir.ActivationFunctionType
AX = mybir.AxisListType

P = 128
N = 384
NT = N // P
DM = 1024
KT = DM // P
H = 16
HD = DM // H
FD = 256
E = 6144
EB = 3
ET = E // P // EB
NE = 8
DF = 2048
FT = DF // P
C = 136
ROUNDS = -(-N // C)
EPS = 1e-5
NEG = -1e30
SCALE = HD ** -0.5

PIECE = KT * P
UNIT = 2 * PIECE
RAW = 4
TURN = 2 * RAW
SPLIT = 4
AHEAD = 3
BANKS = 4
TURNS = 11
LAYER_PIECES = TURNS * TURN
PROJ_PIECES = 9 * TURN
F_TURNS = 2 * FT * KT * P // PIECE // TURN
F_PIECES = F_TURNS * TURN
F_GROUPS = FT + KT
COMBINE_STEPS = 9
EDGE_STEPS = 26
GK = 3
G_BANKS = -(-KT // GK)
Y_BANKS = 4
Y_BANK = (3, 0, 1, 2)
PRE = 2


def build(nc, x, edges, etw, bias, wall, wf, wr, br, wffn, bffn, yrows, out):
    with ExitStack() as ctx:
        def sb(name, shape, dt=F32):
            return ctx.enter_context(nc.sbuf_tensor(name, shape, dt))

        def sem(name):
            return ctx.enter_context(nc.semaphore(name))

        bank = [ctx.enter_context(nc.psum_tensor(f"bank{i}", [P, 512], F32)) for i in range(2 * BANKS)]

        raw = sb("raw", [P, RAW, UNIT])
        whi = sb("whi", [P, SPLIT, PIECE], F32R)
        wlo = sb("wlo", [P, SPLIT, PIECE], F32R)
        x_tok = sb("x_tok", [P, NT, DM])
        a_all = sb("a_all", [P, 2 * KT * N], F32R)
        t_all = sb("t_all", [P, 2 * KT * N], F32R)
        dense = sb("dense", [P, 3 * KT, N])
        v_tok = sb("v_tok", [P, NT, H, HD + 1])
        mo = sb("mo", [P, NT * DM])
        mask8 = sb("mask8", [P, NT, N])
        xg = sb("xg", [P, KT, 2, C], F32R)
        pick = sb("pick", [P, NT, C], BF16)
        ident = sb("ident", [P, P])
        later = sb("later", [P, P])
        later16 = sb("later16", [P, P], BF16)
        ones16 = sb("ones16", [P, P], BF16)
        biases = sb("biases", [P, 7 * KT])
        wf_sb = sb("wf_sb", [P, FD])
        wr_sb = sb("wr_sb", [P, KT, NE])
        br_sb = sb("br_sb", [P, NE])
        etw_sb = sb("etw_sb", [P, 4])
        bffn_sb = sb("bffn_sb", [P, NE, F_GROUPS])
        bcur = sb("bcur", [P, F_GROUPS])
        small = sb("small", [P, 160])
        slot_iota = sb("slot_iota", [P, C])
        base_e = sb("base_e", [P, NE])
        eid = sb("eid", [P, NE])
        rt = sb("rt", [P, 9, NT, NE])
        top_i = sb("top_i", [P, NT, 8], U32)
        sel16 = sb("sel16", [P, NT, NE], BF16)
        posi = sb("posi", [P, 2, NT], I32)
        over = sb("over", [P, 1], I32)

        A_hi, A_lo = (a_all[:, i * KT * N:(i + 1) * KT * N].rearrange("p (k n) -> p k n", k=KT) for i in range(2))
        T_hi, T_lo = (t_all[:, i * KT * N:(i + 1) * KT * N].rearrange("p (k n) -> p k n", k=KT) for i in range(2))
        hid = t_all[:, 0:FT * 2 * C].rearrange("p (k a c) -> p k a c", k=FT, a=2)
        moT = mo[:, :].rearrange("p (k n) -> p k n", k=KT)
        mo_t = mo[:, :].rearrange("p (t d) -> p t d", t=NT)
        dflat = dense[:, :, :].rearrange("p k n -> p (k n)")
        free_d = dflat[:, 2 * KT * N:3 * KT * N]
        qf = [free_d[:, i * 2 * N:(i + 1) * 2 * N].rearrange("p (f n) -> p f n", f=2) for i in range(2)]
        kf = [free_d[:, (2 + i) * 2 * N:(3 + i) * 2 * N].rearrange("p (t f) -> p t f", t=NT) for i in range(2)]
        prob = [free_d[:, i * NT * N:(i + 1) * NT * N].rearrange("p (t n) -> p t n", t=NT) for i in range(2)]
        probT = [mo[:, i * NT * N:(i + 1) * NT * N].rearrange("p (t n) -> p t n", t=NT) for i in range(2)]
        ecol = mo[:, 0:3 * ET]
        ekey = mo[:, 48:48 + ET]
        eval_ = mo[:, 64:64 + ET]
        edup = mo[:, 80:80 + ET]
        epow = mo[:, 96:96 + ET]
        escale = mo[:, 112:113]
        ejunk = mo[:, 128:256]
        kb = mo[:, 256:768].rearrange("p (b n) -> p b n", b=4)
        node_iota = mo[:, 768:768 + N]
        hot_s = mo[:, 1152:1152 + 2 * N].bitcast(BF16).rearrange("p (b n) -> p b n", b=4)
        hot_d = mo[:, 1920:1920 + 2 * N].bitcast(BF16).rearrange("p (b n) -> p b n", b=4)
        ecol_i = mo[:, 2688:2688 + EB * 3 * ET].bitcast(I32).rearrange("p (b c) -> p b c", b=EB)
        zero16 = mo[:, 2832:2832 + N // 2].bitcast(BF16)
        diag = mo[:, 2 * NT * N:2 * NT * N + P]
        norm = sb("norm", [P, 2, N])
        qk = [t_all[:, i * 4 * N:(i + 1) * 4 * N].rearrange("p (m a n) -> p m a n", m=2, a=2) for i in range(2)]
        qf_s = [t_all[:, (2 + i) * 4 * N:(3 + i) * 4 * N].rearrange("p (a f n) -> p a f n", a=2, f=2) for i in range(2)]
        xg_flat = xg[:, :, :, :].rearrange("p k a c -> p (k a c)")
        wf_s = xg_flat[:, 0:2 * FD].rearrange("p (a f) -> p a f", a=2)
        kv = [xg_flat[:, 2 * FD + i * 4 * P:2 * FD + (i + 1) * 4 * P].rearrange("p (a f d) -> p a f d", a=2, f=2) for i in range(2)]
        x_rest = v_tok[:, :, :, :].rearrange("p t h d -> p (t h d)")[:, 0:NT * DM]
        SH = NT * DM // 2
        x16 = [dflat[:, 4608 + i * NT * DM // 2:4608 + (i + 1) * NT * DM // 2].bitcast(BF16) for i in range(3)]
        X16 = [a.rearrange("p (t d) -> p t d", t=NT) for a in x16]
        h_raw = dflat[:, 0:4 * C].rearrange("p (b c) -> p b c", b=4)
        left = dflat[:, 4 * C:8 * C].rearrange("p (b c) -> p b c", b=4)
        yT = dflat[:, 8 * C:(8 + KT) * C].rearrange("p (k c) -> p k c", k=KT)
        y_main = dflat[:, 2304:3328]
        y_rest = dflat[:, 3328:4352]
        pick_a = mask8[:, :, 0:C]
        yg = [m[:, i * DM:(i + 1) * DM] for m in (mo, dflat) for i in range(3)]

        in_x = sem("in_x")
        in_small = sem("in_small")
        in_edges = sem("in_edges")
        raw_in = [sem(f"raw_in{i}") for i in range(RAW)]
        consts = sem("consts")
        hi_done = sem("hi_done")
        lo_done = sem("lo_done")
        used = sem("used")
        evicted = sem("evicted")
        t_hi_done = sem("t_hi_done")
        t_free = sem("t_free")
        dve_seq = sem("dve_seq")
        act_seq = sem("act_seq")
        var_ready = sem("var_ready")
        std_ready = sem("std_ready")
        xn_ready = sem("xn_ready")
        gp_full = sem("gp_full")
        gp_act = sem("gp_act")
        gp_dve = sem("gp_dve")
        hi_copy = sem("hi_copy")
        a_ready = sem("a_ready")
        wf_split = sem("wf_split")
        qk_hi = sem("qk_hi")
        qk_lo = sem("qk_lo")
        mo_hi = sem("mo_hi")
        mo_lo = sem("mo_lo")
        ekey_ready = sem("ekey_ready")
        ekey_turned = sem("ekey_turned")
        edup_done = sem("edup_done")
        hots_ready = sem("hots_ready")
        hots_used = sem("hots_used")
        mask_zero = sem("mask_zero")
        mask_read = sem("mask_read")
        sp_abs = sem("sp_abs")
        sp_ln = sem("sp_ln")
        v_ready = sem("v_ready")
        feat_relu = sem("feat_relu")
        feat_exp = sem("feat_exp")
        feat_done = sem("feat_done")
        kv_full = sem("kv_full")
        kv_hi = sem("kv_hi")
        qf_hi = sem("qf_hi")
        qf_lo = sem("qf_lo")
        norm_ready = sem("norm_ready")
        norm_inv = sem("norm_inv")
        mix_norm = sem("mix_norm")
        kv_ready = sem("kv_ready")
        mix_full = sem("mix_full")
        mix_done = sem("mix_done")
        neg_ready = sem("neg_ready")
        exp_done = sem("exp_done")
        prob_ready = sem("prob_ready")
        turned = sem("turned")
        probT_ready = sem("probT_ready")
        av_full = sem("av_full")
        av_hi = sem("av_hi")
        av_done = sem("av_done")
        x2T_ready = sem("x2T_ready")
        xl_ready = sem("xl_ready")
        x16_dve = sem("x16_dve")
        x16_act = sem("x16_act")
        x16_pool = sem("x16_pool")
        xlT_ready = sem("xlT_ready")
        logits = sem("logits")
        cent = sem("cent")
        rexp = sem("rexp")
        sel_ready = sem("sel_ready")
        ranks = sem("ranks")
        routed = sem("routed")
        b_ready = sem("b_ready")
        pick_ready = sem("pick_ready")
        pick_steps = sem("pick_steps")
        g_full = sem("g_full")
        g_hi = sem("g_hi")
        g_done = sem("g_done")
        y_full = sem("y_full")
        y_free = sem("y_free")
        f_left = sem("f_left")
        f_evicted = sem("f_evicted")
        h_hi = sem("h_hi")
        h_done = sem("h_done")
        y_in = sem("y_in")
        y_all = sem("y_all")
        rows_ready = sem("rows_ready")
        combine_steps = sem("combine_steps")
        fetching = sem("fetching")
        got = [sem(f"got{i}") for i in range(2 * NT)]
        fin = sem("fin")
        stored = sem("stored")

        gp_order = [("xnT", i, "act+dve") for i in range(KT)]
        gp_order += [("vT", i, "act") for i in range(2 * NT)]
        gp_order += [("feat", 4 * h + i, "dve") for h in range(H) for i in range(4)]
        gp_order += [("v2T", i, "act") for i in range(2 * NT)]
        for h in range(H + 1):
            gp_order += [("score", NT * h + i, "dve") for i in range(NT)] if h < H else []
            gp_order += [("probT", NT * (h - 1) + i, "act") for i in range(NT)] if h else []
        gp_order += [("x2", i, "dve") for i in range(2 * NT)]
        gp_order += [("xlT", i, "act") for i in range(KT)]
        gp_order += [("rank", 0, "dve")]
        gp = {(name, i): n for n, (name, i, _) in enumerate(gp_order)}
        gp_by = [e.split("+")[-1] for _, _, e in gp_order]

        def gp_bank(name, i):
            return bank[BANKS + gp[name, i] % BANKS]

        def gp_take(eng, name, i):
            n = gp[name, i] - BANKS
            if n >= 0:
                eng.wait_ge(gp_act if gp_by[n] == "act" else gp_dve, gp_by[:n + 1].count(gp_by[n]))

        def gp_wait(eng, name, i):
            eng.wait_ge(gp_full, gp[name, i] + 1)

        def halves(k):
            return raw[:, (k // 2) % RAW, (k % 2) * PIECE:(k % 2 + 1) * PIECE]

        def feature(h, i):
            b = gp_bank("feat", 4 * h + i)
            if i < 2:
                return qf[h % 2][:, i, :], b[:, 0:N]
            if i == 2:
                return kf[h % 2][:, 0:2, :], b[:, :].rearrange("p (t f) -> p t f", t=2)
            return kf[h % 2][:, 2, :], b[:, 0:FD]

        block = ctx.enter_context(nc.Block())

        @block.sync
        def _(sp):
            for t in range(NT):
                sp.dma_start(x_tok[:, t, :], x[t]).then_inc(in_x, 16)
            for dst, src in ((biases[:, :], bias), (wr_sb[:, :, :], wr), (br_sb[:, :], br), (etw_sb[:, :], etw),
                             (wf_sb[0:HD, :], wf), (wf_sb[HD:P, :], wf), (bffn_sb[:, :, :], bffn)):
                sp.dma_start(dst, src).then_inc(in_small, 16)
            with sp.Fori(0, TURNS) as turn:
                for s in range(RAW):
                    sp.wait_ge(lo_done, turn * TURN + 2 * s + 2)
                    sp.dma_start(raw[:, s, :], wall[bass.ds(turn * RAW + s, 1)].rearrange("a p n -> (a p) n")).then_inc(raw_in[s], 16)

            def unit(g, u, e):
                sp.wait_ge(lo_done, g * F_PIECES + LAYER_PIECES + 2 * u + 2)
                sp.dma_start(raw[:, u % RAW, :], wffn[bass.ds(e * (F_TURNS * RAW) + u, 1)].rearrange("a p n -> (a p) n"))\
                  .then_inc(raw_in[u % RAW], 16)

            def expert(g, e, e_next):
                for u in range(PRE, F_TURNS * RAW):
                    unit(g, u, e)
                for u in range(PRE):
                    unit(g + 1, u, e_next)

            for u in range(PRE):
                unit(0, u, 0)
            with sp.Fori(0, NE - 1) as g:
                expert(g, g, g + 1)
            expert(NE - 1, NE - 1, 0)
            sp.wait_ge(routed, 1)
            more = sp.value_load(over[0:1, 0:1])
            with sp.If(more > 0):
                with sp.Fori(1, ROUNDS) as r:
                    with sp.Fori(0, NE - 1) as e:
                        expert(r * NE + e, e, e + 1)
                    expert(r * NE + (NE - 1), NE - 1, 0)
                sp.wait_ge(fin, NT * ROUNDS)
            for t in range(NT):
                sp.wait_ge(fin, t + 1)
                sp.dma_start(out[t], x_tok[:, t, :]).then_inc(stored, 16)
            sp.wait_ge(stored, 16 * NT)

        @block.gpsimd
        def _(pool):
            pool.memset(ident[:, :], 0.0).then_inc(consts, 1)
            pool.memset(later[:, :], 1.0).then_inc(consts, 1)
            pool.memset(ones16[:, :], 1.0).then_inc(consts, 1)
            pool.wait_ge(consts, 3)
            pool.affine_select(out=ident[:, :], in_=ident[:, :], compare_op=ALU.not_equal, fill=1.0, base=0,
                               pattern=[[-1, P]], channel_multiplier=1).then_inc(consts, 1)
            pool.affine_select(out=later[:, :], in_=later[:, :], compare_op=ALU.is_gt, fill=0.0, base=0,
                               pattern=[[1, P]], channel_multiplier=-1).then_inc(consts, 1)
            pool.wait_ge(consts, 5)
            pool.tensor_copy(later16[:, :], later[:, :]).then_inc(consts, 1)
            pool.iota(slot_iota[:, :], pattern=[[1, C]], base=0, channel_multiplier=0,
                      allow_small_or_imprecise_dtypes=True).then_inc(consts, 1)
            pool.iota(base_e[:, :], pattern=[[C, NE]], base=0, channel_multiplier=0,
                      allow_small_or_imprecise_dtypes=True).then_inc(consts, 1)
            pool.iota(eid[:, :], pattern=[[1, NE]], base=0, channel_multiplier=0,
                      allow_small_or_imprecise_dtypes=True).then_inc(consts, 1)
            pool.memset(v_tok[:, :, :, HD:HD + 1], 1.0).then_inc(consts, 1)
            pool.wait_ge(gp_full, KT)
            pool.iota(node_iota, pattern=[[1, N]], base=0, channel_multiplier=0,
                      allow_small_or_imprecise_dtypes=True).then_inc(consts, 1)
            pool.memset(zero16, 0.0).then_inc(consts, 1)
            for i in range(ET):
                last = pool.memset(epow[:, i:i + 1], 2.0 ** (4 * i - 38))
            last.then_inc(consts, 1)
            pool.memset(escale, 2.0 ** -120).then_inc(consts, 1)
            pool.dma_start(ecol_i, edges).then_inc(in_edges, 16)

            def expert(g, e):
                pool.wait_ge(f_evicted, g * F_GROUPS + BANKS)
                pool.tensor_copy(bcur[:, :], bffn_sb[:, bass.ds(e, 1), :].rearrange("p a g -> p (a g)")).then_inc(b_ready, 1)

            def fetch(r):
                pool.wait_ge(y_all, r + 1)
                pool.wait_ge(rows_ready, r + 1)
                pool.sem_inc(fetching, 1)
                for t in range(NT):
                    for c in range(2):
                        pool.indirect_dma_start(out=yg[2 * t + c], out_offset=None, in_=yrows,
                                                in_offset=bass.IndirectOffsetOnAxis(ap=posi[:, c, t:t + 1].bitcast(U32), axis=0)).then_inc(got[2 * t + c], 16)

            for c in range(KT):
                pool.wait_ge(mix_done, 2 * c + 2)
                pool.wait_ge(norm_inv, c + 1)
                pool.tensor_tensor(moT[:, c, :], moT[:, c, :], norm[:, c % 2, :], ALU.mult).then_inc(mix_norm, 1)
            for i in range(2):
                pool.wait_ge(mo_hi, i + 1)
                ks = slice(i * KT // 2, (i + 1) * KT // 2)
                pool.tensor_tensor(A_lo[:, ks, :], moT[:, ks, :], A_hi[:, ks, :].bitcast(F32), ALU.subtract).then_inc(mo_lo, 1)
            pool.wait_ge(in_small, 16 * 7)
            pool.wait_ge(x16_dve, 1)
            pool.tensor_tensor(x_rest[:, SH:], mo[:, SH:], x16[0][:, SH:], ALU.subtract).then_inc(x16_pool, 1)
            pool.wait_ge(x16_act, 1)
            pool.tensor_tensor(x16[2][:, SH:], x_rest[:, SH:], x16[1][:, SH:], ALU.subtract).then_inc(x16_pool, 1)
            pool.wait_ge(routed, 1)
            with pool.Fori(0, NE) as g:
                expert(g, g)
            more = pool.value_load(over[0:1, 0:1])
            fetch(0)
            with pool.If(more > 0):
                with pool.Fori(1, ROUNDS) as r:
                    with pool.Fori(0, NE) as e:
                        expert(r * NE + e, e)
                    fetch(r)
        @block.scalar
        def _(act):
            seq = [0]

            def link(ins):
                seq[0] += 1
                ins.then_inc(act_seq, 1)
                act.wait_ge(act_seq, seq[0])


            def hi(turn, k, first):
                if k % 2 == 0:
                    act.wait_ge(raw_in[(k // 2) % RAW], (turn + k // TURN + 1) * 16)
                act.wait_ge(used, first + k + 1)
                act.activation(whi[:, k % SPLIT, :], halves(k), ACT.Copy).then_inc(hi_done, 1)

            act.wait_ge(var_ready, 1)
            act.activation(small[:, 8:8 + NT], small[:, 4:4 + NT], ACT.Sqrt).then_inc(std_ready, 1)
            for k in range(AHEAD):
                hi(0, k, 0)
            for i in range(KT):
                gp_wait(act, "xnT", i)
                act.activation(A_hi[:, i, :], gp_bank("xnT", i)[:, 0:N], ACT.Copy).then_inc(hi_copy, 1)
            with act.Fori(0, EB) as m:
                for j in range(TURN):
                    hi(m, j + AHEAD, m * TURN)
            act.wait_ge(sp_abs, 1)
            link(act.activation(small[:, 40:44], small[:, 36:40], ACT.Exp, scale=-1.0))
            act.activation(small[:, 44:48], small[:, 40:44], ACT.Ln, bias=1.0).then_inc(sp_ln, 1)
            act.wait_ge(consts, 14)
            for i in range(2 * NT):
                gp_wait(act, "vT", i)
                act.activation(v_tok[:, i // 2, H // 2 * (i % 2):H // 2 * (i % 2 + 1), 0:HD],
                               gp_bank("vT", i)[:, :].rearrange("p (h d) -> p h d", d=HD), ACT.Copy).then_inc(gp_act, 1)
            act.wait_ge(in_small, 16 * 7)
            act.activation(wf_s[:, 0, :], wf_sb[:, :], ACT.Copy).then_inc(wf_split, 1)

            def split_hi(c):
                if c >= 2:
                    act.wait_ge(gp_full, gp["feat", 8 * (c - 2) + 7] + 1)
                for m in range(2):
                    act.activation(qk[c % 2][:, m, 0, :], dense[:, m * KT + c, :], ACT.Copy).then_inc(qk_hi, 1)

            def kv_high(g):
                own, other = (slice(HD * (p % 2), HD * (p % 2) + HD) for p in (g, g + 1))
                b = bank[g % 2][:, 0:2 * (HD + 1)].rearrange("p (f d) -> p f d", f=2)
                act.wait_ge(kv_full, g + 1)
                if g >= 2:
                    act.wait_ge(mix_full, g - 1)
                act.activation(kv[g % 2][:, 0, :, own], b[:, :, 0:HD], ACT.Copy)
                act.activation(kv[g % 2][:, 0, :, other], b[:, :, HD:HD + 1].to_broadcast([P, 2, HD]), ACT.Copy).then_inc(kv_hi, 1)

            act.wait_ge(evicted, EB * TURN + BANKS)
            split_hi(0)
            relus = 0
            for h in range(H):
                if h % 2 == 0 and h // 2 + 1 < KT:
                    split_hi(h // 2 + 1)
                if h >= 2:
                    act.wait_ge(mix_full, h - 1)
                elif h == 0:
                    act.wait_ge(gp_full, gp["vT", 2 * NT - 1] + 1)
                for i in range(4):
                    dst, src = feature(h, i)
                    gp_wait(act, "feat", 4 * h + i)
                    act.activation(dst, src, ACT.Relu, scale=-1.0).then_inc(feat_relu, 1)
                    relus += 1
                    act.wait_ge(feat_relu, relus)
                    act.activation(dst, dst, ACT.Exp, scale=-1.0).then_inc(feat_exp, 1)
                act.wait_ge(feat_done, 4 * h + 2)
                act.activation(qf_s[h % 2][:, 0, :, :], qf[h % 2], ACT.Copy).then_inc(qf_hi, 1)
                if h >= 1:
                    kv_high(h - 1)
            kv_high(H - 1)
            with act.Fori(0, 3) as m:
                for j in range(TURN):
                    if j == 0:
                        act.wait_ge(t_free, m + 1)
                    act.wait_ge(used, m * (2 * TURN) + EB * TURN + j + 1 + SPLIT)
                    act.activation(T_hi[:, j, :], bank[j % BANKS][:, 0:N], ACT.Identity,
                                   bias=bcur[:, j:j + 1]).then_inc(t_hi_done, 1)
                    hi(m * 2 + EB, j + AHEAD, m * (2 * TURN) + EB * TURN)
                for j in range(TURN):
                    hi(m * 2 + EB + 1, j + AHEAD, m * (2 * TURN) + (EB + 1) * TURN)
            act.wait_ge(used, PROJ_PIECES - TURN + SPLIT)
            act.wait_ge(mix_norm, KT)
            for i in range(2):
                act.activation(A_hi[:, i * KT // 2:(i + 1) * KT // 2, :], moT[:, i * KT // 2:(i + 1) * KT // 2, :], ACT.Copy).then_inc(mo_hi, 1)
            for i in range(2 * NT):
                gp_wait(act, "v2T", i)
                act.activation(v_tok[:, i // 2, H // 2 * (i % 2):H // 2 * (i % 2 + 1), 0:HD],
                               gp_bank("v2T", i)[:, :].rearrange("p (h d) -> p h d", d=HD), ACT.Copy).then_inc(gp_act, 1)
            for h in range(H + 2):
                if h < H:
                    act.wait_ge(neg_ready, h + 1)
                    for t in range(NT):
                        act.activation(prob[h % 2][:, t, :], prob[h % 2][:, t, :], ACT.Exp,
                                       bias=small[:, 64 + 16 * (h % 2) + t:65 + 16 * (h % 2) + t],
                                       accum_out=small[:, 68 + 16 * (h % 2) + t:69 + 16 * (h % 2) + t]).then_inc(exp_done, 1)
                if 1 <= h <= H:
                    g = h - 1
                    if g >= 2:
                        act.wait_ge(av_full, g - 1)
                    elif g == 0:
                        act.wait_ge(mo_lo, 2)
                    for t in range(NT):
                        gp_wait(act, "probT", NT * g + t)
                        act.activation(probT[g % 2][:, t, :], gp_bank("probT", NT * g + t)[:, 0:N], ACT.Copy).then_inc(gp_act, 1)
                if h >= 2 and h % 2 == 1:
                    c = (h - 2) // 2
                    act.wait_ge(av_full, 2 * c + 2)
                    act.activation(T_hi[:, c, :], bank[c % 2][:, 0:N], ACT.Copy).then_inc(av_hi, 1)
            for i in range(2 * TURN):
                hi(9, i + AHEAD, PROJ_PIECES)
            act.wait_ge(var_ready, 2)
            act.activation(small[:, 8:8 + NT], small[:, 4:4 + NT], ACT.Sqrt).then_inc(std_ready, 1)
            act.wait_ge(xl_ready, 1)
            for i in range(KT):
                gp_wait(act, "xlT", i)
                act.activation(dense[:, i, :], gp_bank("xlT", i)[:, 0:N], ACT.Copy).then_inc(gp_act, 1)
            act.wait_ge(x16_pool, 1)
            act.activation(x16[1][:, SH:], x_rest[:, SH:], ACT.Copy).then_inc(x16_act, 1)
            act.wait_ge(cent, 1)
            act.activation(rt[:, 1], rt[:, 0], ACT.Exp).then_inc(rexp, 1)


            def hi_f(g, k):
                if k % 2 == 0:
                    act.wait_ge(raw_in[(k // 2) % RAW], (g * F_TURNS + (TURNS + k // TURN + 1)) * 16)
                act.wait_ge(used, g * F_PIECES + LAYER_PIECES + k + 1)
                act.activation(whi[:, k % SPLIT, :], halves(k), ACT.Copy).then_inc(hi_done, 1)

            def gathered(g):
                for j in range(G_BANKS):
                    ks = min(GK, KT - j * GK)
                    act.wait_ge(g_full, g * G_BANKS + j + 1)
                    act.activation(xg[:, j * GK:j * GK + ks, 0, :], bank[BANKS + j][:, 0:ks * C].rearrange("p (k c) -> p k c", k=ks),
                                   ACT.Copy).then_inc(g_hi, 1)

            def group(g, i, pieces):
                act.wait_ge(used, g * F_PIECES + LAYER_PIECES + pieces + SPLIT)
                act.wait_ge(f_evicted, g * F_GROUPS + i + 1)
                act.activation(left[:, i % 4, :], bank[i % BANKS][:, 0:C], ACT.Identity, bias=bcur[:, i:i + 1]).then_inc(f_left, 1)

            def hidden(g, i):
                act.wait_ge(f_evicted, g * F_GROUPS + i + 1 + BANKS)
                act.activation(hid[:, i, 0, :], h_raw[:, i % 4, :], ACT.Relu).then_inc(h_hi, 1)

            def expert(g, e):
                act.wait_ge(b_ready, g + 1)
                for i in range(FT):
                    hi_f(g, i + AHEAD)
                    group(g, i, i + 1)
                    if i >= 1:
                        hidden(g, i - 1)
                hidden(g, FT - 1)
                for i in range(KT):
                    for k in range(2):
                        hi_f(g, FT + 2 * i + k + AHEAD)
                    group(g, FT + i, FT + 2 * i + 2)
                gathered(g + 1)
                act.wait_ge(y_in, g * 32 + 32)
                for i in range(2):
                    act.wait_ge(y_full, g * Y_BANKS + i + 1 + Y_BANKS)
                    act.activation(y_main[:, i * 512:(i + 1) * 512], bank[BANKS + Y_BANK[i]][:, :], ACT.Copy).then_inc(y_free, 1)
                for i in range(2):
                    act.wait_ge(y_full, g * Y_BANKS + i + 3 + Y_BANKS)
                    act.activation(y_rest[0:C - P, i * 512:(i + 1) * 512], bank[BANKS + Y_BANK[2 + i]][0:C - P, :], ACT.Copy).then_inc(y_free, 1)
                act.wait_ge(y_free, g * Y_BANKS + 3 * Y_BANKS)
                act.dma_start(yrows[bass.ds(e * C, P), :], y_main).then_inc(y_in, 16)
                act.dma_start(yrows[bass.ds(e * C + P, C - P), :], y_rest[0:C - P, :]).then_inc(y_in, 16)

            act.sem_inc(y_free, 2 * Y_BANKS)
            act.sem_inc(y_in, 32)
            gathered(0)
            with act.Fori(0, NE) as g:
                expert(g, g)
            act.wait_ge(y_in, NE * 32 + 32)
            act.sem_inc(y_all, 1)
            act.wait_ge(routed, 1)
            more = act.value_load(over[0:1, 0:1])
            with act.If(more > 0):
                with act.Fori(1, ROUNDS) as r:
                    act.wait_ge(fin, NT * r)
                    with act.Fori(0, NE) as e:
                        expert(r * NE + e, e)
                    act.wait_ge(y_in, (r + 1) * (NE * 32) + 32)
                    act.sem_inc(y_all, 1)

        @block.tensor
        def _(pe):
            def piece(k, dst, rhs_hi, rhs_lo, start, stop, n=KT):
                w_hi = whi[:, k % SPLIT, :].rearrange("p (c o) -> p c o", c=n)
                w_lo = wlo[:, k % SPLIT, :].rearrange("p (c o) -> p c o", c=n)
                for c in range(n):
                    pe.matmul(dst, w_hi[:, c, :], rhs_hi[:, c, :], start=(start and c == 0), stop=False)
                    pe.matmul(dst, w_hi[:, c, :], rhs_lo[:, c, :], start=False, stop=False)
                    last = pe.matmul(dst, w_lo[:, c, :], rhs_hi[:, c, :], start=False, stop=(stop and c == n - 1))
                return last

            pe.sem_inc(used, SPLIT)
            pe.wait_ge(consts, 4)
            pe.wait_ge(xn_ready, NT)
            for i in range(KT):
                gp_take(pe, "xnT", i)
                for t in range(NT):
                    last = pe.transpose(gp_bank("xnT", i)[:, t * P:(t + 1) * P], mo_t[:, t, i * P:(i + 1) * P], ident[:, :])
                last.then_inc(gp_full, 1)
            pe.wait_ge(consts, 14)
            pe.wait_ge(a_ready, KT)
            for t in range(NT):
                last = pe.matmul(bank[BANKS + t][:, 0:N], zero16[:, 0:P], zero16, start=True, stop=True)
            with pe.Fori(0, EB) as m:
                for j in range(TURN):
                    pe.wait_ge(lo_done, m * TURN + j + 1 + TURN)
                    pe.wait_ge(evicted, m * TURN + j + 1)
                    piece(j, bank[j % BANKS][:, 0:N], A_hi, A_lo, True, True).then_inc(used, 1)
                    if j < 4:
                        pe.wait_ge(ekey_ready, m * 4 + j + 1)
                        for i in range(4):
                            last = pe.transpose(bank[7][:, i * P:(i + 1) * P], kb[:, i, :], ident[:, :])
                        last.then_inc(ekey_turned, 1)
                    else:
                        pe.wait_ge(hots_ready, m * 4 + j - 3)
                        for i in range(4):
                            for t in range(NT):
                                last = pe.matmul(bank[BANKS + t][:, 0:N], hot_s[:, i, t * P:(t + 1) * P], hot_d[:, i, :],
                                                 start=False, stop=True, skip_group_check=True)
                        last.then_inc(hots_used, 1)
            pe.wait_ge(evicted, EB * TURN + BANKS)
            pe.wait_ge(mask_read, NT)
            for i in range(2 * NT):
                gp_take(pe, "vT", i)
                for c in range(4):
                    last = pe.transpose(gp_bank("vT", i)[:, c * P:(c + 1) * P],
                                        dense[:, 2 * KT + 4 * (i % 2) + c, i // 2 * P:(i // 2 + 1) * P], ident[:, :])
                last.then_inc(gp_full, 1)
            pe.wait_ge(wf_split, 2)
            for h in range(H + 2):
                if h < H:
                    lo = HD * (h % 2)
                    pe.wait_ge(qk_lo, 2 * (h // 2) + 2)
                    for i in range(4):
                        gp_take(pe, "feat", 4 * h + i)
                        b = gp_bank("feat", 4 * h + i)
                        q, k = (qk[h // 2 % 2][lo:lo + HD, m] for m in range(2))
                        w = wf_s[lo:lo + HD]
                        for n, (x_part, w_part) in enumerate(((0, 0), (0, 1), (1, 0))):
                            if i < 2:
                                last = pe.matmul(b[:, 0:N], w[:, w_part, i * P:(i + 1) * P], q[:, x_part, :], start=(n == 0), stop=(n == 2))
                        for t in range(0, 2) if i == 2 else range(2, 3) if i == 3 else ():
                            for n, (x_part, w_part) in enumerate(((0, 0), (0, 1), (1, 0))):
                                last = pe.matmul(b[:, (t % 2) * FD:(t % 2 + 1) * FD], k[:, x_part, t * P:(t + 1) * P],
                                                 w[:, w_part, :], start=(n == 0), stop=(n == 2))
                        last.then_inc(gp_full, 1)
                if h >= 2:
                    g = h - 2
                    pe.wait_ge(kv_ready, g + 1)
                    if g >= 2:
                        pe.wait_ge(mix_done, g - 1)
                    pe.wait_ge(qf_lo, g + 1)
                    for n, (kv_part, q_part) in enumerate(((0, 0), (0, 1), (1, 0))):
                        for f in range(2):
                            last = pe.matmul(bank[2 + g % 2][:, 0:N], kv[g % 2][:, kv_part, f, :], qf_s[g % 2][:, q_part, f, :],
                                             start=(n == 0 and f == 0), stop=(n == 2 and f == 1))
                    last.then_inc(mix_full, 1)
                if 1 <= h <= H:
                    g = h - 1
                    pe.wait_ge(feat_done, 4 * g + 4)
                    if g == 0:
                        pe.wait_ge(gp_act, gp_by[:gp["vT", 2 * NT - 1] + 1].count("act"))
                    if g >= 2:
                        pe.wait_ge(kv_ready, g - 1)
                    for f in range(2):
                        for t in range(NT):
                            last = pe.matmul(bank[g % 2][:, f * (HD + 1):(f + 1) * (HD + 1)], kf[g % 2][:, t, f * P:(f + 1) * P],
                                             v_tok[:, t, g, :], start=(t == 0), stop=(t == NT - 1))
                    last.then_inc(kv_full, 1)
            pe.wait_ge(mix_done, H)
            with pe.Fori(0, 3) as m:
                base = m * (2 * TURN) + EB * TURN
                for j in range(2 * TURN):
                    pe.wait_ge(lo_done, base + j + 1 + TURN)
                    pe.wait_ge(evicted, base + (TURN + BANKS if j == TURN else j + 1))
                    src = (A_hi, A_lo) if j < TURN else (T_hi, T_lo)
                    last = piece(j, bank[j % BANKS][:, 0:N], *src, True, True)
                    last.then_inc(used, 1)
            pe.wait_ge(evicted, PROJ_PIECES + BANKS)
            for i in range(2 * NT):
                gp_take(pe, "v2T", i)
                for c in range(4):
                    last = pe.transpose(gp_bank("v2T", i)[:, c * P:(c + 1) * P],
                                        dense[:, 2 * KT + 4 * (i % 2) + c, i // 2 * P:(i // 2 + 1) * P], ident[:, :])
                last.then_inc(gp_full, 1)
            for h in range(H + 2):
                if h < H:
                    lo = HD * (h % 2)
                    for t in range(NT):
                        gp_take(pe, "score", NT * h + t)
                        pe.matmul(gp_bank("score", NT * h + t)[:, 0:N], dense[lo:lo + HD, h // 2, t * P:(t + 1) * P],
                                  dense[lo:lo + HD, KT + h // 2, :], start=True, stop=True).then_inc(gp_full, 1)
                if h >= 2:
                    g = h - 2
                    c = g // 2
                    lo = HD * (g % 2)
                    pe.wait_ge(gp_act, gp_by[:gp["probT", NT * g + NT - 1] + 1].count("act"))
                    if c >= 2 and g % 2 == 0:
                        pe.wait_ge(av_done, c - 1)
                    for t in range(NT):
                        last = pe.matmul(bank[c % 2][lo:lo + HD, 0:N], v_tok[:, t, g, 0:HD], probT[g % 2][:, t, :],
                                         start=(t == 0), stop=(t == NT - 1))
                    last.then_inc(av_full, 1)
                if 1 <= h <= H:
                    g = h - 1
                    pe.wait_ge(prob_ready, g + 1)
                    for mt in range(NT):
                        gp_take(pe, "probT", NT * g + mt)
                        for t in range(NT):
                            last = pe.transpose(gp_bank("probT", NT * g + mt)[:, t * P:(t + 1) * P],
                                                prob[g % 2][:, t, mt * P:(mt + 1) * P], ident[:, :])
                        last.then_inc(gp_full, 1)
                    last = None
            pe.wait_ge(av_done, KT)
            pe.wait_ge(mo_lo, 2)
            for i in range(KT):
                k = PROJ_PIECES + 2 * i
                pe.wait_ge(lo_done, k + 1 + TURN)
                pe.wait_ge(evicted, PROJ_PIECES + i + 1)
                piece(2 * i, bank[i % BANKS][:, 0:N], A_hi, A_lo, True, False).then_inc(used, 1)
                pe.wait_ge(lo_done, k + 2 + TURN)
                piece(2 * i + 1, bank[i % BANKS][:, 0:N], T_hi, T_lo, False, True).then_inc(used, 1)
            for i in range(2 * NT):
                gp_take(pe, "x2", i)
                if i == 0:
                    pe.wait_ge(evicted, PROJ_PIECES + KT + BANKS)
                for c in range(4):
                    last = pe.transpose(gp_bank("x2", i)[:, c * P:(c + 1) * P],
                                        dense[:, 4 * (i % 2) + c, i // 2 * P:(i // 2 + 1) * P], ident[:, :])
                last.then_inc(gp_full, 1)
            pe.wait_ge(xl_ready, 1)
            for i in range(KT + 2):
                if i < KT:
                    gp_take(pe, "xlT", i)
                    for t in range(NT):
                        last = pe.transpose(gp_bank("xlT", i)[:, t * P:(t + 1) * P], mo_t[:, t, i * P:(i + 1) * P], ident[:, :])
                    last.then_inc(gp_full, 1)
                if i >= 2:
                    c = i - 2
                    pe.wait_ge(gp_act, gp_by[:gp["xlT", c] + 1].count("act"))
                    for t in range(NT):
                        last = pe.matmul(bank[t][:, 0:NE], dense[:, c, t * P:(t + 1) * P], wr_sb[:, c, :],
                                         start=(c == 0), stop=(c == KT - 1))
            last.then_inc(logits, 1)
            gp_take(pe, "rank", 0)
            pe.wait_ge(sel_ready, 1)
            for t in range(NT + 1):
                for s in range(min(t + 1, NT)):
                    last = pe.matmul(gp_bank("rank", 0)[:, t * NE:(t + 1) * NE], (later16 if s == t else ones16)[:, :], sel16[:, s, :],
                                     start=(s == 0), stop=(s == min(t, NT - 1)))
            last.then_inc(gp_full, 1)
            pe.wait_ge(x16_pool, 2)
            pe.wait_ge(x16_dve, 5)
            pe.wait_ge(gp_dve, gp_by.count("dve"))

            def gather(g):
                pe.wait_ge(pick_ready, g + 1)
                for j in range(G_BANKS):
                    pe.wait_ge(y_free, g * Y_BANKS + Y_BANK.index(j) + 1)
                    for k in range(j * GK, min(KT, (j + 1) * GK)):
                        o = bank[BANKS + j][:, (k - j * GK) * C:(k - j * GK + 1) * C]
                        for a in range(3):
                            for t in range(NT):
                                last = pe.matmul(o, X16[a][:, t, k * P:(k + 1) * P], pick[:, t, :],
                                                 start=(a == 0 and t == 0), stop=(a == 2 and t == NT - 1))
                    last.then_inc(g_full, 1)

            def piece_f(k, dst, rhs, start, stop):
                w_hi = whi[:, k % SPLIT, :].rearrange("p (c o) -> p c o", c=KT)
                w_lo = wlo[:, k % SPLIT, :].rearrange("p (c o) -> p c o", c=KT)
                for c in range(KT):
                    pe.matmul(dst, w_hi[:, c, :], rhs[:, c, :], start=(start and c == 0), stop=False)
                    last = pe.matmul(dst, w_lo[:, c, :], rhs[:, c, :], start=False, stop=(stop and c == KT - 1))
                return last

            def expert(g, e):
                first = g * F_PIECES + LAYER_PIECES
                pe.wait_ge(g_done, (g + 1) * G_BANKS)
                for i in range(FT):
                    pe.wait_ge(lo_done, first + i + 1 + TURN)
                    pe.wait_ge(f_evicted, g * F_GROUPS + i + 1)
                    piece_f(i, bank[i % BANKS][:, 0:2 * C], xg[:, :, :, :].rearrange("p k a c -> p k (a c)"), True, True).then_inc(used, 1)
                for i in range(KT):
                    pe.wait_ge(f_evicted, g * F_GROUPS + FT + i + 1)
                    for a in range(2):
                        k = FT + 2 * i + a
                        pe.wait_ge(lo_done, first + k + 1 + TURN)
                        if i == 0:
                            pe.wait_ge(h_done, g * FT + (a + 1) * KT + BANKS)
                        piece_f(k, bank[i % BANKS][:, 0:2 * C], hid[:, a * KT:(a + 1) * KT, :, :].rearrange("p k a c -> p k (a c)"),
                                a == 0, a == 1).then_inc(used, 1)
                gather(g + 1)
                for n in range(Y_BANKS):
                    part, i = divmod(n, 2)
                    cols = (slice(0, P), slice(P, C))[part]
                    rows = cols.stop - cols.start
                    pe.wait_ge(f_evicted, g * F_GROUPS + FT + 4 * i + 4 + BANKS)
                    if n == 0:
                        pe.wait_ge(y_free, g * Y_BANKS + Y_BANKS + 1)
                    else:
                        pe.wait_ge(g_done, (g + 1) * G_BANKS + Y_BANK[n] + 1)
                    for c in range(4):
                        last = pe.transpose(bank[BANKS + Y_BANK[n]][0:rows, c * P:(c + 1) * P], yT[:, 4 * i + c, cols], ident[:, :])
                    last.then_inc(y_full, 1)

            pe.sem_inc(y_full, Y_BANKS)
            gather(0)
            with pe.Fori(0, NE) as g:
                expert(g, g)
            pe.wait_ge(routed, 1)
            more = pe.value_load(over[0:1, 0:1])
            with pe.If(more > 0):
                with pe.Fori(1, ROUNDS) as r:
                    with pe.Fori(0, NE) as e:
                        expert(r * NE + e, e)

        @block.vector
        def _(dve):
            seq = [0]

            def link(ins):
                seq[0] += 1
                ins.then_inc(dve_seq, 1)
                dve.wait_ge(dve_seq, seq[0])

            dve.sem_inc(lo_done, TURN)
            dve.sem_inc(evicted, BANKS)
            dve.sem_inc(f_evicted, BANKS)
            dve.sem_inc(h_done, BANKS)

            def lo(k, first):
                dve.wait_ge(hi_done, first + k + 1)
                dve.tensor_tensor(wlo[:, k % SPLIT, :], halves(k), whi[:, k % SPLIT, :].bitcast(F32), ALU.subtract).then_inc(lo_done, 1)

            def normalize(n):
                mv = small[:, 12:12 + 2 * NT].rearrange("p (t a) -> p t a", a=2)
                st = small[:, 96:96 + 12 * NT].rearrange("p (t a b) -> p t a b", a=2, b=6)
                for t in range(NT):
                    if n == 0:
                        dve.wait_ge(in_x, 16 * NT)
                    for a in range(2):
                        last = dve.bn_stats(st[:, t, a, :], x_tok[:, t, a * 512:(a + 1) * 512])
                link(last)
                for t in range(NT):
                    last = dve.bn_aggr(mv[:, t, :], st[:, t, :, :].rearrange("p a b -> p (a b)"))
                link(last)
                dve.tensor_scalar(small[:, 4:4 + NT], mv[:, :, 1], EPS, None, ALU.add).then_inc(var_ready, 1)
                dve.wait_ge(std_ready, n + 1)
                r = small[:, 0:NT]
                v = small[:, 4:4 + NT]
                w = small[:, 8:8 + NT]
                link(dve.reciprocal(r, w))
                link(dve.tensor_tensor(w, r, r, ALU.mult))
                link(dve.tensor_tensor(w, w, v, ALU.mult))
                link(dve.tensor_scalar(w, w, -0.5, 1.5, ALU.mult, ALU.add))
                link(dve.tensor_tensor(r, r, w, ALU.mult))
                for t in range(NT):
                    ins = dve.tensor_scalar(mo_t[:, t, :], x_tok[:, t, :], mv[:, t, 0:1], small[:, t:t + 1], ALU.subtract, ALU.mult)
                    if n == 0:
                        ins.then_inc(xn_ready, 1)
                if n == 1:
                    ins.then_inc(xl_ready, 1)

            normalize(0)
            for i in range(KT):
                dve.wait_ge(hi_copy, i + 1)
                dve.tensor_tensor(A_lo[:, i, :], gp_bank("xnT", i)[:, 0:N], A_hi[:, i, :].bitcast(F32), ALU.subtract)\
                   .then_inc(gp_dve, 1)
            dve.wait_ge(gp_dve, KT)
            dve.sem_inc(a_ready, KT)
            for k in range(AHEAD):
                lo(k, 0)
            dve.wait_ge(consts, 14)
            dve.wait_ge(in_small, 16 * 7)
            dve.wait_ge(in_edges, 16)
            with dve.Fori(0, EB) as m:
                es, ed, ety = ecol[:, 0:ET], ecol[:, ET:2 * ET], ecol[:, 2 * ET:3 * ET]
                steps = [0]

                def step(ins):
                    steps[0] += 1
                    ins.then_inc(edup_done, 1)
                    dve.wait_ge(edup_done, m * EDGE_STEPS + steps[0])

                for j in range(TURN):
                    if j == 0:
                        step(dve.tensor_copy(ecol, ecol_i[:, bass.ds(m, 1), :].rearrange("p a c -> p (a c)")))
                        step(dve.tensor_scalar(ekey, es, float(N), None, ALU.mult))
                        step(dve.tensor_tensor(ekey, ekey, ed, ALU.add))
                        step(dve.tensor_scalar(eval_, ety, 0.0, 4.0, ALU.is_equal, ALU.mult))
                        step(dve.tensor_tensor(eval_, eval_, ety, ALU.add))
                        step(dve.tensor_tensor(eval_, eval_, epow, ALU.mult))
                        step(dve.tensor_scalar(escale, escale, 2.0 ** (4 * ET), None, ALU.mult))
                        step(dve.tensor_scalar(eval_, eval_, escale, None, ALU.mult))
                    if j < 4:
                        for i in range(4):
                            last = dve.tensor_copy(kb[:, i, :], ekey[:, 4 * j + i:4 * j + i + 1].to_broadcast([P, P]))
                        last.then_inc(ekey_ready, 1)
                    else:
                        if j > 4:
                            dve.wait_ge(hots_used, m * 4 + j - 4)
                        for i in range(4):
                            c = 4 * (j - 4) + i
                            dve.tensor_scalar(hot_s[:, i, :], node_iota, es[:, c:c + 1], None, ALU.is_equal)
                            last = dve.tensor_scalar(hot_d[:, i, :], node_iota, ed[:, c:c + 1], eval_[:, c:c + 1], ALU.is_equal, ALU.mult)
                        last.then_inc(hots_ready, 1)
                    dve.wait_ge(used, m * TURN + j + 1 + SPLIT)
                    dve.tensor_copy(dense[:, bass.ds(m * KT + j, 1), :].rearrange("p a n -> p (a n)"), bank[j % BANKS][:, 0:N]).then_inc(evicted, 1)
                    lo(j + AHEAD, m * TURN)
                    if j < 4:
                        dve.wait_ge(ekey_turned, m * 4 + j + 1)
                        for i in range(4):
                            c = 4 * j + i
                            step(dve.scalar_tensor_tensor(out=ejunk, in0=bank[7][:, i * P:(i + 1) * P], scalar=ekey[:, c:c + 1],
                                                          in1=later[:, :], op0=ALU.is_equal, op1=ALU.mult, accum_out=edup[:, c:c + 1]))
                    if j == 3:
                        step(dve.tensor_scalar(edup, edup, 0.0, None, ALU.is_equal))
                        step(dve.tensor_tensor(eval_, eval_, edup, ALU.mult))
                dve.wait_ge(hots_used, m * 4 + 4)
                assert steps[0] == EDGE_STEPS, steps[0]

            neg, ab, ln = small[:, 32:36], small[:, 36:40], small[:, 44:48]
            link(dve.tensor_scalar(neg, etw_sb[:, :], -1.0, None, ALU.mult))
            dve.tensor_tensor(ab, neg, etw_sb[:, :], ALU.max).then_inc(sp_abs, 1)
            pos_w = small[:, 132:136]
            link(dve.tensor_scalar(pos_w, etw_sb[:, :], 0.0, None, ALU.max))
            table = mo[:, 0:NT * N].rearrange("p (t n) -> p t n", t=NT)
            tab = mo[:, 0:NT * N]
            for t in range(NT):
                dve.tensor_copy(table[:, t, :], bank[BANKS + t][:, 0:N]).then_inc(mask_read, 1)
            dve.wait_ge(mask_read, NT)
            tmp = mo[:, NT * N:2 * NT * N]
            link(dve.tensor_scalar(tmp.bitcast(I32), tab.bitcast(I32), 22, 7, ALU.logical_shift_right, ALU.bitwise_and))
            link(dve.tensor_copy(tab, tmp.bitcast(I32)))
            for t in range(NT):
                d = table[:, t, t * P:(t + 1) * P]
                link(dve.tensor_scalar(diag, d, 0.0, 6.0, ALU.is_equal, ALU.mult))
                link(dve.tensor_tensor(diag, diag, ident[:, :], ALU.mult))
                link(dve.tensor_tensor(d, d, diag, ALU.add))
            dve.wait_ge(sp_ln, 1)
            link(dve.tensor_tensor(ln, ln, pos_w, ALU.add))
            link(dve.tensor_scalar(ln, ln, 1.0 / SCALE, None, ALU.mult))
            m8 = mask8[:, :, :].rearrange("p t n -> p (t n)")
            link(dve.tensor_scalar(m8, tab, 0.0, NEG, ALU.is_equal, ALU.mult))
            for code, w in ((2.0, 0), (4.0, 1), (5.0, 2), (6.0, 3)):
                link(dve.tensor_scalar(tmp, tab, code, small[:, 44 + w:45 + w], ALU.is_equal, ALU.mult))
                link(dve.tensor_tensor(m8, m8, tmp, ALU.add))

            def split_lo(c):
                for m in range(2):
                    dve.wait_ge(qk_hi, 2 * c + m + 1)
                    dve.tensor_tensor(qk[c % 2][:, m, 1, :], dense[:, m * KT + c, :], qk[c % 2][:, m, 0, :].bitcast(F32), ALU.subtract)\
                       .then_inc(qk_lo, 1)

            dve.wait_ge(wf_split, 1)
            dve.tensor_tensor(wf_s[:, 1, :], wf_sb[:, :], wf_s[:, 0, :].bitcast(F32), ALU.subtract).then_inc(wf_split, 1)
            split_lo(0)
            for h in range(H + 2):
                if h % 2 == 0 and h // 2 + 1 < KT:
                    split_lo(h // 2 + 1)
                if h < H:
                    for i in range(4):
                        dst, src = feature(h, i)
                        dve.wait_ge(feat_exp, 4 * h + i + 1)
                        dve.scalar_tensor_tensor(out=dst, in0=src, scalar=0.0, in1=dst, op0=ALU.max, op1=ALU.add).then_inc(gp_dve, 1)
                        if i == 1 or i == 3:
                            dve.wait_ge(gp_dve, gp_by[:gp["feat", 4 * h + i] + 1].count("dve"))
                            dve.sem_inc(feat_done, 2)
                if h >= 2:
                    g = h - 2
                    own, other = (slice(HD * (p % 2), HD * (p % 2) + HD) for p in (g, g + 1))
                    o = bank[2 + g % 2]
                    dve.wait_ge(mix_full, g + 1)
                    if g >= 4:
                        dve.wait_ge(mix_norm, (g - 4) // 2 + 1)
                    dve.tensor_scalar(norm[own, g // 2 % 2, :], o[other, 0:N], 1e-6, None, ALU.add).then_inc(norm_ready, 1)
                    dve.tensor_copy(moT[own, g // 2, :], o[own, 0:N]).then_inc(mix_done, 1)
                if 1 <= h <= H:
                    g = h - 1
                    own, other = (slice(HD * (p % 2), HD * (p % 2) + HD) for p in (g, g + 1))
                    b = bank[g % 2][:, 0:2 * (HD + 1)].rearrange("p (f d) -> p f d", f=2)
                    dve.wait_ge(kv_hi, g + 1)
                    dve.tensor_tensor(kv[g % 2][:, 1, :, own], b[:, :, 0:HD], kv[g % 2][:, 0, :, own].bitcast(F32), ALU.subtract)
                    dve.tensor_tensor(kv[g % 2][:, 1, :, other], b[:, :, HD:HD + 1].to_broadcast([P, 2, HD]),
                                      kv[g % 2][:, 0, :, other].bitcast(F32), ALU.subtract).then_inc(kv_ready, 1)
                if h < H:
                    dve.wait_ge(qf_hi, h + 1)
                    dve.tensor_tensor(qf_s[h % 2][:, 1, :, :], qf[h % 2], qf_s[h % 2][:, 0, :, :].bitcast(F32), ALU.subtract).then_inc(qf_lo, 1)
                if h >= 3 and h % 2 == 1:
                    c = (h - 3) // 2
                    dve.wait_ge(norm_ready, 2 * c + 2)
                    dve.reciprocal(norm[:, c % 2, :], norm[:, c % 2, :]).then_inc(norm_inv, 1)

            with dve.Fori(0, 3) as m:
                base = m * (2 * TURN) + EB * TURN
                dve.wait_ge(evicted, base + BANKS)
                dve.tensor_copy(bcur[:, 0:2 * KT], biases[:, bass.ds(m * (2 * KT), 2 * KT)]).then_inc(t_free, 1)
                dve.wait_ge(t_free, m + 1)
                for j in range(TURN):
                    dve.wait_ge(t_hi_done, m * TURN + j + 1)
                    dve.scalar_tensor_tensor(out=T_lo[:, j, :], in0=bank[j % BANKS][:, 0:N], scalar=bcur[:, j:j + 1],
                                             in1=T_hi[:, j, :].bitcast(F32), op0=ALU.add, op1=ALU.subtract).then_inc(evicted, 1)
                    lo(j + AHEAD, base)
                for j in range(TURN):
                    dve.wait_ge(used, base + TURN + j + 1 + SPLIT)
                    dve.tensor_scalar(dense[:, bass.ds(m * KT + j, 1), :].rearrange("p a n -> p (a n)"), bank[j % BANKS][:, 0:N],
                                      bcur[:, KT + j:KT + j + 1], None, ALU.add).then_inc(evicted, 1)
                    lo(j + AHEAD, base + TURN)
            for h in range(H + 3):
                if h < H:
                    s = 64 + 16 * (h % 2)
                    if h == 0:
                        dve.wait_ge(gp_full, gp["v2T", 2 * NT - 1] + 1)
                    if h >= 2:
                        dve.wait_ge(gp_full, gp["probT", NT * (h - 2) + NT - 1] + 1)
                    for t in range(NT):
                        gp_wait(dve, "score", NT * h + t)
                        dve.tensor_tensor_reduce(out=prob[h % 2][:, t, :], in0=gp_bank("score", NT * h + t)[:, 0:N], in1=mask8[:, t, :],
                                                 scale=SCALE, scalar=-3e38, op0=ALU.add, op1=ALU.max,
                                                 accum_out=small[:, s + 8 + t:s + 9 + t]).then_inc(gp_dve, 1)
                    dve.wait_ge(gp_dve, gp_by[:gp["score", NT * h + NT - 1] + 1].count("dve"))
                    dve.tensor_scalar(small[:, s:s + NT], small[:, s + 8:s + 8 + NT], -1.0, None, ALU.mult).then_inc(neg_ready, 1)
                if 1 <= h <= H:
                    g = h - 1
                    s = 64 + 16 * (g % 2)
                    dve.wait_ge(exp_done, NT * g + NT)
                    link(dve.reciprocal(small[:, s + 12:s + 12 + NT], small[:, s + 4:s + 4 + NT]))
                    for t in range(NT):
                        last = dve.tensor_scalar(prob[g % 2][:, t, :], prob[g % 2][:, t, :], small[:, s + 12 + t:s + 13 + t], None, ALU.mult)
                    last.then_inc(prob_ready, 1)
                if h >= 3 and h % 2 == 1:
                    c = (h - 3) // 2
                    dve.wait_ge(av_hi, c + 1)
                    dve.tensor_tensor(T_lo[:, c, :], bank[c % 2][:, 0:N], T_hi[:, c, :].bitcast(F32), ALU.subtract).then_inc(av_done, 1)
            for i in range(KT):
                dve.wait_ge(used, PROJ_PIECES + 2 * i + 2 + SPLIT)
                dve.tensor_scalar(dense[:, i, :], bank[i % BANKS][:, 0:N], biases[:, 6 * KT + i:6 * KT + i + 1], None, ALU.add)\
                   .then_inc(evicted, 1)
                for k in range(2 * i + AHEAD, 2 * i + AHEAD + 2):
                    lo(k, PROJ_PIECES)
            for i in range(2 * NT):
                gp_wait(dve, "x2", i)
                r = x_tok[:, i // 2, (i % 2) * 512:(i % 2 + 1) * 512]
                dve.tensor_tensor(r, gp_bank("x2", i)[:, :], r, ALU.add).then_inc(gp_dve, 1)
            dve.wait_ge(gp_dve, gp_by[:gp["x2", 2 * NT - 1] + 1].count("dve"))
            normalize(1)
            dve.wait_ge(xl_ready, 1)
            dve.tensor_copy(x16[0][:, SH:], mo[:, SH:]).then_inc(x16_dve, 1)
            for n, ins in enumerate((
                    lambda: dve.tensor_copy(x16[0][:, 0:SH], mo[:, 0:SH]),
                    lambda: dve.tensor_tensor(x_rest[:, 0:SH], mo[:, 0:SH], x16[0][:, 0:SH], ALU.subtract),
                    lambda: dve.tensor_copy(x16[1][:, 0:SH], x_rest[:, 0:SH]),
                    lambda: dve.tensor_tensor(x16[2][:, 0:SH], x_rest[:, 0:SH], x16[1][:, 0:SH], ALU.subtract))):
                ins().then_inc(x16_dve, 1)
                dve.wait_ge(x16_dve, n + 2)
            dve.wait_ge(logits, 1)
            cen, ex, prb, srt, sel0, sel1, pos, tm = (rt[:, i] for i in range(8))
            mx = small[:, 52:52 + NT].rearrange("p (t a) -> p t a", a=1)
            for t in range(NT):
                last = dve.tensor_tensor(cen[:, t, :], bank[t][:, 0:NE], br_sb[:, :], ALU.add)
            link(last)
            link(dve.tensor_reduce(mx, cen, AX.X, ALU.max))
            dve.tensor_tensor(cen, cen, mx.to_broadcast([P, NT, NE]), ALU.subtract).then_inc(cent, 1)
            dve.wait_ge(rexp, 1)
            link(dve.tensor_reduce(mx, ex, AX.X, ALU.add))
            link(dve.reciprocal(mx, mx))
            link(dve.tensor_tensor(prb, ex, mx.to_broadcast([P, NT, NE]), ALU.mult))
            for t in range(NT):
                link(dve.max(srt[:, t, :], prb[:, t, :]))
                link(dve.max_index(top_i[:, t, :], srt[:, t, :], prb[:, t, :]))
            ti = rt[:, 8]
            link(dve.tensor_copy(ti, top_i[:, :, :]))
            ide = eid[:, :].rearrange("p (a e) -> p a e", a=1).to_broadcast([P, NT, NE])
            link(dve.tensor_tensor(sel0, ide, ti[:, :, 0:1].to_broadcast([P, NT, NE]), ALU.is_equal))
            link(dve.tensor_tensor(sel1, ide, ti[:, :, 1:2].to_broadcast([P, NT, NE]), ALU.is_equal))
            dve.tensor_tensor(sel16[:, :, :], sel0, sel1, ALU.add).then_inc(sel_ready, 1)
            gp_wait(dve, "rank", 0)
            rk = gp_bank("rank", 0)[:, 0:NT * NE].rearrange("p (t e) -> p t e", t=NT)
            link(dve.tensor_scalar(pos, rk, float(C), float((NE - 1) * C), ALU.is_ge, ALU.mult))
            for r in range(2, ROUNDS):
                link(dve.tensor_scalar(tm, rk, float(C * r), float((NE - 1) * C), ALU.is_ge, ALU.mult))
                link(dve.tensor_tensor(pos, pos, tm, ALU.add))
            link(dve.tensor_tensor(pos, pos, rk, ALU.add))
            link(dve.tensor_tensor(pos, pos, base_e[:, :].rearrange("p (a e) -> p a e", a=1).to_broadcast([P, NT, NE]), ALU.add))
            posf = small[:, 56:56 + 2 * NT].rearrange("p (c t) -> p c t", c=2)
            for c, s in enumerate((sel0, sel1)):
                link(dve.tensor_tensor(tm, pos, s, ALU.mult))
                link(dve.tensor_reduce(posf[:, c, :].rearrange("p (t a) -> p t a", a=1), tm, AX.X, ALU.add))
            link(dve.tensor_copy(small[:, 136:136 + 2 * NT], small[:, 56:56 + 2 * NT]))
            cnt = small[:, 62:63]
            dve.tensor_reduce(cnt, gp_bank("rank", 0)[:, NT * NE:(NT + 1) * NE], AX.X, ALU.max).then_inc(gp_dve, 1)
            dve.wait_ge(gp_dve, gp_by.count("dve"))
            dve.tensor_scalar(over[:, :], cnt, float(C), None, ALU.is_gt).then_inc(routed, 1)

            def choose(g):
                for t in range(NT):
                    dve.tensor_scalar(pick_a[:, t, :], slot_iota[:, :], small[:, 56 + t:57 + t], None, ALU.is_equal).then_inc(pick_steps, 1)
                dve.wait_ge(pick_steps, g * (NT + 1) + NT)
                for t in range(NT):
                    last = dve.scalar_tensor_tensor(out=pick[:, t, :], in0=slot_iota[:, :], scalar=small[:, 59 + t:60 + t],
                                                    in1=pick_a[:, t, :], op0=ALU.is_equal, op1=ALU.add)
                last.then_inc(pick_ready, 1)
                dve.wait_ge(pick_ready, g + 1)
                dve.tensor_scalar(slot_iota[:, :], slot_iota[:, :], float(C), None, ALU.add).then_inc(pick_steps, 1)
                dve.wait_ge(pick_steps, (g + 1) * (NT + 1))

            def gathered(g):
                for j in range(G_BANKS):
                    ks = min(GK, KT - j * GK)
                    dve.wait_ge(g_hi, g * G_BANKS + j + 1)
                    dve.tensor_tensor(xg[:, j * GK:j * GK + ks, 1, :], bank[BANKS + j][:, 0:ks * C].rearrange("p (k c) -> p k c", k=ks),
                                      xg[:, j * GK:j * GK + ks, 0, :].bitcast(F32), ALU.subtract).then_inc(g_done, 1)

            def group(g, i, dst):
                dve.wait_ge(f_left, g * F_GROUPS + i + 1)
                dve.tensor_tensor(dst, bank[i % BANKS][:, C:2 * C], left[:, i % 4, :], ALU.add).then_inc(f_evicted, 1)

            def h_low(g, i):
                dve.wait_ge(h_hi, g * FT + i + 1)
                dve.scalar_tensor_tensor(out=hid[:, i, 1, :], in0=h_raw[:, i % 4, :], scalar=0.0, in1=hid[:, i, 0, :].bitcast(F32),
                                         op0=ALU.max, op1=ALU.subtract).then_inc(h_done, 1)

            def expert(g, e):
                first = g * F_PIECES + LAYER_PIECES
                for i in range(FT):
                    dve.wait_ge(h_done, g * FT + i + 1)
                    group(g, i, h_raw[:, i % 4, :])
                    if i >= 1:
                        h_low(g, i - 1)
                    lo(i + AHEAD, first)
                h_low(g, FT - 1)
                for i in range(KT):
                    if i == 1:
                        choose(g + 1)
                    if i == 0:
                        dve.wait_ge(y_full, g * Y_BANKS + Y_BANKS)
                    group(g, FT + i, yT[:, i, :])
                    for k in range(2):
                        lo(FT + 2 * i + k + AHEAD, first)
                gathered(g + 1)

            round_pos = small[:, 136:136 + 2 * NT]
            below = small[:, 142:142 + 2 * NT]
            here = small[:, 148:148 + 2 * NT]
            weight = small[:, 154:154 + 2 * NT]

            def combine(r):
                steps = [0]

                def step(ins):
                    steps[0] += 1
                    ins.then_inc(combine_steps, 1)
                    dve.wait_ge(combine_steps, r * COMBINE_STEPS + steps[0])

                step(dve.tensor_scalar(below, round_pos, float(NE * C), None, ALU.is_lt))
                step(dve.tensor_scalar(here, round_pos, 0.0, None, ALU.is_ge))
                step(dve.tensor_tensor(here, here, below, ALU.mult))
                step(dve.tensor_tensor(below, round_pos, here, ALU.mult))
                dve.tensor_copy(posi[:, :, :], below.rearrange("p (c t) -> p c t", c=2)).then_inc(rows_ready, 1)
                step(dve.tensor_tensor(weight.rearrange("p (c t) -> p c t", c=2), here.rearrange("p (c t) -> p c t", c=2),
                                       rt[:, 3, :, 0:2].rearrange("p t c -> p c t"), ALU.mult))
                step(dve.tensor_scalar(round_pos, round_pos, float(-NE * C), None, ALU.add))
                for t in range(NT):
                    for c in range(2):
                        dve.wait_ge(got[2 * t + c], 16 * r + 16)
                        ins = dve.scalar_tensor_tensor(out=x_tok[:, t, :], in0=yg[2 * t + c], scalar=weight[:, c * NT + t:c * NT + t + 1],
                                                       in1=x_tok[:, t, :], op0=ALU.mult, op1=ALU.add)
                        if c == 0:
                            step(ins)
                    ins.then_inc(fin, 1)
                dve.wait_ge(fin, NT * r + NT)
                assert steps[0] == COMBINE_STEPS, steps[0]

            choose(0)
            gathered(0)
            with dve.Fori(0, NE) as g:
                expert(g, g)
            combine(0)
            more = dve.value_load(over[0:1, 0:1])
            with dve.If(more > 0):
                with dve.Fori(1, ROUNDS) as r:
                    with dve.Fori(0, NE) as e:
                        expert(r * NE + e, e)
                    combine(r)


def kernel(**inputs):
    import numpy as np
    import concourse.bacc as bacc
    from concourse.bass_utils import run_bass_kernel_spmd

    a = {k: np.asarray(v) for k, v in inputs.items()}

    def pieces(w):
        return w.reshape(KT, P, KT, P).transpose(0, 3, 2, 1).reshape(KT, P, PIECE)

    def units(p):
        return p.reshape(-1, 2, P, PIECE).transpose(0, 2, 1, 3).reshape(-1, P, UNIT)

    def columns(v):
        return v.reshape(-1, P).T

    g = {k[7:]: v for k, v in a.items() if k.startswith("L0_gnn_")}
    first = [a["L0_mix_Wq"], a["L0_mix_Wk"], a["L0_mix_Wv"], g["wq"], g["wiq"], g["wk"], g["wik"], g["wv"], g["wiv"]]
    last = np.stack([pieces(a["L0_mix_Wo"]), pieces(g["wo"])], axis=1).reshape(2 * KT, P, PIECE)
    wall = units(np.concatenate([pieces(w) for w in first] + [last]))
    w1 = a["L0_ffn_W1"].reshape(NE, KT, P, FT, P).transpose(0, 3, 2, 1, 4).reshape(NE, FT, P, PIECE)
    w2 = a["L0_ffn_W2"].reshape(NE, 2, KT, P, KT, P).transpose(0, 4, 1, 3, 2, 5).reshape(NE, 2 * KT, P, PIECE)
    wffn = units(np.concatenate([w1, w2], axis=1).reshape(-1, P, PIECE))
    edges = np.stack([v.reshape(EB, ET, P) for v in (a["src"], a["dst"], a["edge_type_5"])], axis=1)
    arrays = {
        "x": a["x"].reshape(NT, P, DM),
        "edges": edges.reshape(EB, 3 * ET, P).transpose(2, 0, 1),
        "etw": np.broadcast_to(g["edge_type_weights"], (P, 4)),
        "bias": np.concatenate([columns(g[n]) for n in ("bq", "biq", "bk", "bik", "bv", "biv", "bo")], axis=1),
        "wall": wall,
        "wf": a["L0_mix_Wf"].T,
        "wr": a["L0_ffn_Wr"].reshape(KT, P, NE).transpose(1, 0, 2),
        "br": np.broadcast_to(a["L0_ffn_br"], (P, NE)),
        "wffn": wffn,
        "bffn": np.concatenate([a["L0_ffn_b1"].reshape(NE, FT, P), a["L0_ffn_b2"].reshape(NE, KT, P)], axis=1).transpose(2, 0, 1),
    }
    arrays = {f"in_{k}": np.ascontiguousarray(v) for k, v in arrays.items()}
    nc = bacc.Bacc("TRN2", target_bir_lowering=False, num_devices=1)
    aps = {k[3:]: nc.dram_tensor(k, v.shape, mybir.dt.from_np(v.dtype), kind="ExternalInput").ap() for k, v in arrays.items()}
    yrows = nc.dram_tensor("yrows", (NE * C, DM), F32, kind="Internal").ap()
    out = nc.dram_tensor("out", (NT, P, DM), F32, kind="ExternalOutput").ap()
    build(nc, **aps, yrows=yrows, out=out)
    r = run_bass_kernel_spmd(nc, [arrays], core_ids=[0])
    return r.results[0]["out"].reshape(N, DM)
```

```python
from contextlib import ExitStack

import concourse.bass as bass
from concourse import mybir

F32 = mybir.dt.float32
F32R = mybir.dt.float32r
BF16 = mybir.dt.bfloat16
I32 = mybir.dt.int32
U32 = mybir.dt.uint32
ALU = mybir.AluOpType
ACT = mybir.ActivationFunctionType
AX = mybir.AxisListType

P = 128
N = 384
NT = N // P
DM = 1024
KT = DM // P
H = 16
HD = DM // H
FD = 256
E = 6144
EB = 3
ET = E // P // EB
NE = 8
DF = 2048
FT = DF // P
C = 136
ROUNDS = -(-N // C)
EPS = 1e-5
NEG = -1e30
SCALE = HD ** -0.5

PIECE = KT * P
UNIT = 2 * PIECE
RAW = 4
TURN = 2 * RAW
SPLIT = 4
AHEAD = 3
BANKS = 4
TURNS = 11
LAYER_PIECES = TURNS * TURN
PROJ_PIECES = 9 * TURN
F_TURNS = 2 * FT * KT * P // PIECE // TURN
F_PIECES = F_TURNS * TURN
F_GROUPS = FT + KT
COMBINE_STEPS = 9
EDGE_STEPS = 26
MASK_STEPS = 14
GK = 3
G_BANKS = -(-KT // GK)
Y_BANKS = 4
Y_BANK = (3, 0, 1, 2)
PRE = 2


def build(nc, x, edges, etw, bias, wall, wf, wr, br, wffn, bffn, yrows, out):
    with ExitStack() as ctx:
        def sb(name, shape, dt=F32):
            return ctx.enter_context(nc.sbuf_tensor(name, shape, dt))

        def sem(name):
            return ctx.enter_context(nc.semaphore(name))

        bank = [ctx.enter_context(nc.psum_tensor(f"bank{i}", [P, 512], F32)) for i in range(2 * BANKS)]

        raw = sb("raw", [P, RAW, UNIT])
        whi = sb("whi", [P, SPLIT, PIECE], F32R)
        wlo = sb("wlo", [P, SPLIT, PIECE], F32R)
        x_tok = sb("x_tok", [P, NT, DM])
        a_all = sb("a_all", [P, 2 * KT * N], F32R)
        t_all = sb("t_all", [P, 2 * KT * N], F32R)
        dense = sb("dense", [P, 3 * KT, N])
        v_tok = sb("v_tok", [P, NT, H, HD + 1])
        mo = sb("mo", [P, NT * DM])
        mask8 = sb("mask8", [P, NT, N])
        xg = sb("xg", [P, KT, 2, C], F32R)
        pick = sb("pick", [P, NT, C], BF16)
        ident = sb("ident", [P, P])
        later = sb("later", [P, P])
        later16 = sb("later16", [P, P], BF16)
        ones16 = sb("ones16", [P, P], BF16)
        biases = sb("biases", [P, 7 * KT])
        wf_sb = sb("wf_sb", [P, FD])
        wr_sb = sb("wr_sb", [P, KT, NE])
        br_sb = sb("br_sb", [P, NE])
        etw_sb = sb("etw_sb", [P, 4])
        bffn_sb = sb("bffn_sb", [P, NE, F_GROUPS])
        bcur = sb("bcur", [P, F_GROUPS])
        small = sb("small", [P, 160])
        slot_iota = sb("slot_iota", [P, C])
        base_e = sb("base_e", [P, NE])
        eid = sb("eid", [P, NE])
        rt = sb("rt", [P, 9, NT, NE])
        top_i = sb("top_i", [P, NT, 8], U32)
        sel16 = sb("sel16", [P, NT, NE], BF16)
        posi = sb("posi", [P, 2, NT], I32)
        over = sb("over", [P, 1], I32)

        A_hi, A_lo = (a_all[:, i * KT * N:(i + 1) * KT * N].rearrange("p (k n) -> p k n", k=KT) for i in range(2))
        T_hi, T_lo = (t_all[:, i * KT * N:(i + 1) * KT * N].rearrange("p (k n) -> p k n", k=KT) for i in range(2))
        hid = t_all[:, 0:FT * 2 * C].rearrange("p (k a c) -> p k a c", k=FT, a=2)
        moT = mo[:, :].rearrange("p (k n) -> p k n", k=KT)
        mo_t = mo[:, :].rearrange("p (t d) -> p t d", t=NT)
        dflat = dense[:, :, :].rearrange("p k n -> p (k n)")
        free_d = dflat[:, 2 * KT * N:3 * KT * N]
        qf = [free_d[:, i * 2 * N:(i + 1) * 2 * N].rearrange("p (f n) -> p f n", f=2) for i in range(2)]
        kf = [free_d[:, (2 + i) * 2 * N:(3 + i) * 2 * N].rearrange("p (t f) -> p t f", t=NT) for i in range(2)]
        prob = [free_d[:, i * NT * N:(i + 1) * NT * N].rearrange("p (t n) -> p t n", t=NT) for i in range(2)]
        ecol = mo[:, 0:3 * ET]
        ekey = mo[:, 48:48 + ET]
        eval_ = mo[:, 64:64 + ET]
        edup = mo[:, 80:80 + ET]
        epow = mo[:, 96:96 + ET]
        escale = mo[:, 112:113]
        ejunk = mo[:, 128:256]
        kb = mo[:, 256:768].rearrange("p (b n) -> p b n", b=4)
        node_iota = mo[:, 768:768 + N]
        hot_s = mo[:, 1152:1152 + 2 * N].bitcast(BF16).rearrange("p (b n) -> p b n", b=4)
        hot_d = mo[:, 1920:1920 + 2 * N].bitcast(BF16).rearrange("p (b n) -> p b n", b=4)
        ecol_i = mo[:, 2688:2688 + EB * 3 * ET].bitcast(I32).rearrange("p (b c) -> p b c", b=EB)
        zero16 = mo[:, 2832:2832 + N // 2].bitcast(BF16)
        v_flat = v_tok[:, :, :, :].rearrange("p t h d -> p (t h d)")
        tab, tmp, diag = v_flat[:, 0:N], v_flat[:, N:2 * N], v_flat[:, 2 * N:2 * N + P]
        norm = sb("norm", [P, 2, N])
        qk = [t_all[:, i * 4 * N:(i + 1) * 4 * N].rearrange("p (m a n) -> p m a n", m=2, a=2) for i in range(2)]
        qf_s = [t_all[:, (2 + i) * 4 * N:(3 + i) * 4 * N].rearrange("p (a f n) -> p a f n", a=2, f=2) for i in range(2)]
        xg_flat = xg[:, :, :, :].rearrange("p k a c -> p (k a c)")
        wf_s = xg_flat[:, 0:2 * FD].rearrange("p (a f) -> p a f", a=2)
        probT = [a_all[:, i * 2 * NT * N:(i + 1) * 2 * NT * N].rearrange("p (a t n) -> p a t n", a=2, t=NT) for i in range(2)]
        qk2 = [m.rearrange("p (m a n) -> p m a n", m=2, a=2) for m in (a_all[:, 4 * NT * N:4 * NT * N + 4 * N], xg_flat[:, 0:4 * N])]
        v_s = xg_flat[:, 4 * N:4 * N + 2 * NT * HD].rearrange("p (t a d) -> p t a d", a=2, t=NT)
        kv = [xg_flat[:, 2 * FD + i * 4 * P:2 * FD + (i + 1) * 4 * P].rearrange("p (a f d) -> p a f d", a=2, f=2) for i in range(2)]
        x_rest = v_flat[:, 0:NT * DM]
        SH = NT * DM // 2
        x16 = [dflat[:, 4608 + i * NT * DM // 2:4608 + (i + 1) * NT * DM // 2].bitcast(BF16) for i in range(3)]
        X16 = [a.rearrange("p (t d) -> p t d", t=NT) for a in x16]
        h_raw = dflat[:, 0:4 * C].rearrange("p (b c) -> p b c", b=4)
        left = dflat[:, 4 * C:8 * C].rearrange("p (b c) -> p b c", b=4)
        yT = dflat[:, 8 * C:(8 + KT) * C].rearrange("p (k c) -> p k c", k=KT)
        y_main = dflat[:, 2304:3328]
        y_rest = dflat[:, 3328:4352]
        pick_a = mask8[:, :, 0:C]
        yg = [m[:, i * DM:(i + 1) * DM] for m in (mo, dflat) for i in range(3)]

        in_x = [sem(f"in_x{t}") for t in range(NT)]
        in_small = sem("in_small")
        in_edges = sem("in_edges")
        raw_in = [sem(f"raw_in{i}") for i in range(RAW)]
        consts = sem("consts")
        hi_done = sem("hi_done")
        lo_done = sem("lo_done")
        used = sem("used")
        evicted = sem("evicted")
        t_hi_done = sem("t_hi_done")
        t_free = sem("t_free")
        dve_seq = sem("dve_seq")
        act_seq = sem("act_seq")
        var_ready = sem("var_ready")
        std_ready = sem("std_ready")
        xn_ready = sem("xn_ready")
        gp_full = sem("gp_full")
        gp_act = sem("gp_act")
        gp_dve = sem("gp_dve")
        hi_copy = sem("hi_copy")
        a_ready = sem("a_ready")
        wf_split = sem("wf_split")
        qk_hi = sem("qk_hi")
        qk_lo = sem("qk_lo")
        mo_hi = sem("mo_hi")
        mo_lo = sem("mo_lo")
        ekey_ready = sem("ekey_ready")
        ekey_turned = sem("ekey_turned")
        edup_done = sem("edup_done")
        hots_ready = sem("hots_ready")
        hots_used = sem("hots_used")
        mask_read = sem("mask_read")
        mask_steps = sem("mask_steps")
        sp_abs = sem("sp_abs")
        sp_ln = sem("sp_ln")
        feat_relu = sem("feat_relu")
        feat_exp = sem("feat_exp")
        feat_done = sem("feat_done")
        kv_full = sem("kv_full")
        kv_hi = sem("kv_hi")
        qf_hi = sem("qf_hi")
        qf_lo = sem("qf_lo")
        norm_ready = sem("norm_ready")
        norm_inv = sem("norm_inv")
        mix_norm = sem("mix_norm")
        kv_ready = sem("kv_ready")
        mix_full = sem("mix_full")
        mix_done = sem("mix_done")
        neg_ready = sem("neg_ready")
        exp_done = sem("exp_done")
        prob_ready = sem("prob_ready")
        sc_full = sem("sc_full")
        sc_done = sem("sc_done")
        pt_full = sem("pt_full")
        pt_lo = sem("pt_lo")
        v_hi = sem("v_hi")
        v_lo = sem("v_lo")
        pt_hi = sem("pt_hi")
        av_full = sem("av_full")
        av_left = sem("av_left")
        av_sum = sem("av_sum")
        av_hi = sem("av_hi")
        av_done = sem("av_done")
        xl_ready = sem("xl_ready")
        x16_dve = sem("x16_dve")
        x16_act = sem("x16_act")
        x16_pool = sem("x16_pool")
        logits = sem("logits")
        cent = sem("cent")
        rexp = sem("rexp")
        sel_ready = sem("sel_ready")
        routed = sem("routed")
        b_ready = sem("b_ready")
        pick_ready = sem("pick_ready")
        pick_steps = sem("pick_steps")
        g_full = sem("g_full")
        g_hi = sem("g_hi")
        g_done = sem("g_done")
        y_full = sem("y_full")
        y_free = sem("y_free")
        f_left = sem("f_left")
        f_evicted = sem("f_evicted")
        h_hi = sem("h_hi")
        h_done = sem("h_done")
        y_in = sem("y_in")
        y_all = sem("y_all")
        rows_ready = sem("rows_ready")
        combine_steps = sem("combine_steps")
        fetching = sem("fetching")
        got = [sem(f"got{i}") for i in range(2 * NT)]
        fin = sem("fin")
        stored = sem("stored")

        gp_order = [("xnT", i, "act+dve") for i in range(KT)]
        gp_order += [("vT", i, "act") for i in range(2 * NT)]
        gp_order += [("feat", 4 * h + i, "dve") for h in range(H) for i in range(4)]
        gp_order += [("v2T", i, "act") for i in range(2 * NT)]
        gp_order += [("x2", i, "dve") for i in range(2 * NT)]
        gp_order += [("xlT", i, "act") for i in range(KT)]
        gp_order += [("rank", 0, "dve")]
        gp = {(name, i): n for n, (name, i, _) in enumerate(gp_order)}
        gp_by = [e.split("+")[-1] for _, _, e in gp_order]

        def gp_bank(name, i):
            return bank[BANKS + gp[name, i] % BANKS]

        def gp_take(eng, name, i):
            n = gp[name, i] - BANKS
            if n >= 0:
                eng.wait_ge(gp_act if gp_by[n] == "act" else gp_dve, gp_by[:n + 1].count(gp_by[n]))

        def gp_wait(eng, name, i):
            eng.wait_ge(gp_full, gp[name, i] + 1)

        sc_bank = bank[4:7]
        pt_bank = [bank[7], bank[2], bank[3]]
        av_bank = bank[0:2]

        def halves(k):
            return raw[:, (k // 2) % RAW, (k % 2) * PIECE:(k % 2 + 1) * PIECE]

        def feature(h, i):
            b = gp_bank("feat", 4 * h + i)
            if i < 2:
                return qf[h % 2][:, i, :], b[:, 0:N]
            if i == 2:
                return kf[h % 2][:, 0:2, :], b[:, :].rearrange("p (t f) -> p t f", t=2)
            return kf[h % 2][:, 2, :], b[:, 0:FD]

        block = ctx.enter_context(nc.Block())

        @block.sync
        def _(sp):
            for t in range(NT):
                sp.dma_start(x_tok[:, t, :], x[t]).then_inc(in_x[t], 16)
            for dst, src in ((biases[:, :], bias), (wr_sb[:, :, :], wr), (br_sb[:, :], br), (etw_sb[:, :], etw),
                             (wf_sb[0:HD, :], wf), (wf_sb[HD:P, :], wf), (bffn_sb[:, :, :], bffn)):
                sp.dma_start(dst, src).then_inc(in_small, 16)
            with sp.Fori(0, TURNS) as turn:
                for s in range(RAW):
                    sp.wait_ge(lo_done, turn * TURN + 2 * s + 2)
                    sp.dma_start(raw[:, s, :], wall[bass.ds(turn * RAW + s, 1)].rearrange("a p n -> (a p) n")).then_inc(raw_in[s], 16)

            def unit(g, u, e):
                sp.wait_ge(lo_done, g * F_PIECES + LAYER_PIECES + 2 * u + 2)
                sp.dma_start(raw[:, u % RAW, :], wffn[bass.ds(e * (F_TURNS * RAW) + u, 1)].rearrange("a p n -> (a p) n"))\
                  .then_inc(raw_in[u % RAW], 16)

            def expert(g, e, e_next):
                for u in range(PRE, F_TURNS * RAW):
                    unit(g, u, e)
                for u in range(PRE):
                    unit(g + 1, u, e_next)

            for u in range(PRE):
                unit(0, u, 0)
            with sp.Fori(0, NE - 1) as g:
                expert(g, g, g + 1)
            expert(NE - 1, NE - 1, 0)
            sp.wait_ge(routed, 1)
            more = sp.value_load(over[0:1, 0:1])
            with sp.If(more > 0):
                with sp.Fori(1, ROUNDS) as r:
                    with sp.Fori(0, NE - 1) as e:
                        expert(r * NE + e, e, e + 1)
                    expert(r * NE + (NE - 1), NE - 1, 0)
                sp.wait_ge(fin, NT * ROUNDS)
            for t in range(NT):
                sp.wait_ge(fin, t + 1)
                sp.dma_start(out[t], x_tok[:, t, :]).then_inc(stored, 16)
            sp.wait_ge(stored, 16 * NT)

        @block.gpsimd
        def _(pool):
            pool.memset(ident[:, :], 0.0).then_inc(consts, 1)
            pool.memset(later[:, :], 1.0).then_inc(consts, 1)
            pool.memset(ones16[:, :], 1.0).then_inc(consts, 1)
            pool.wait_ge(consts, 3)
            pool.affine_select(out=ident[:, :], in_=ident[:, :], compare_op=ALU.not_equal, fill=1.0, base=0,
                               pattern=[[-1, P]], channel_multiplier=1).then_inc(consts, 1)
            pool.affine_select(out=later[:, :], in_=later[:, :], compare_op=ALU.is_gt, fill=0.0, base=0,
                               pattern=[[1, P]], channel_multiplier=-1).then_inc(consts, 1)
            pool.wait_ge(consts, 5)
            pool.tensor_copy(later16[:, :], later[:, :]).then_inc(consts, 1)
            pool.iota(slot_iota[:, :], pattern=[[1, C]], base=0, channel_multiplier=0,
                      allow_small_or_imprecise_dtypes=True).then_inc(consts, 1)
            pool.iota(base_e[:, :], pattern=[[C, NE]], base=0, channel_multiplier=0,
                      allow_small_or_imprecise_dtypes=True).then_inc(consts, 1)
            pool.iota(eid[:, :], pattern=[[1, NE]], base=0, channel_multiplier=0,
                      allow_small_or_imprecise_dtypes=True).then_inc(consts, 1)
            pool.memset(v_tok[:, :, :, HD:HD + 1], 1.0).then_inc(consts, 1)
            pool.wait_ge(gp_full, KT)
            pool.iota(node_iota, pattern=[[1, N]], base=0, channel_multiplier=0,
                      allow_small_or_imprecise_dtypes=True).then_inc(consts, 1)
            pool.memset(zero16, 0.0).then_inc(consts, 1)
            for i in range(ET):
                last = pool.memset(epow[:, i:i + 1], 2.0 ** (4 * i - 38))
            last.then_inc(consts, 1)
            pool.memset(escale, 2.0 ** -120).then_inc(consts, 1)
            pool.dma_start(ecol_i, edges).then_inc(in_edges, 16)

            def expert(g, e):
                pool.wait_ge(f_evicted, g * F_GROUPS + BANKS)
                pool.tensor_copy(bcur[:, :], bffn_sb[:, bass.ds(e, 1), :].rearrange("p a g -> p (a g)")).then_inc(b_ready, 1)

            def fetch(r):
                pool.wait_ge(y_all, r + 1)
                pool.wait_ge(rows_ready, r + 1)
                pool.sem_inc(fetching, 1)
                for t in range(NT):
                    for c in range(2):
                        pool.indirect_dma_start(out=yg[2 * t + c], out_offset=None, in_=yrows,
                                                in_offset=bass.IndirectOffsetOnAxis(ap=posi[:, c, t:t + 1].bitcast(U32), axis=0)).then_inc(got[2 * t + c], 16)

            def split(c):
                if c >= 2:
                    pool.wait_ge(gp_full, gp["feat", 8 * (c - 2) + 7] + 1)
                for m in range(2):
                    pool.tensor_copy(qk[c % 2][:, m, 0, :], dense[:, m * KT + c, :]).then_inc(qk_hi, 1)
                    pool.wait_ge(qk_hi, 2 * c + m + 1)
                    pool.tensor_tensor(qk[c % 2][:, m, 1, :], dense[:, m * KT + c, :], qk[c % 2][:, m, 0, :].bitcast(F32), ALU.subtract)\
                        .then_inc(qk_lo, 1)

            pool.wait_ge(evicted, EB * TURN + BANKS)
            split(0)
            for h in range(H + 4):
                if h % 2 == 0 and h // 2 + 1 < KT:
                    split(h // 2 + 1)
                if h < H:
                    pool.wait_ge(qf_hi, h + 1)
                    pool.tensor_tensor(qf_s[h % 2][:, 1, :, :], qf[h % 2], qf_s[h % 2][:, 0, :, :].bitcast(F32), ALU.subtract).then_inc(qf_lo, 1)
                if h % 2 == 1 and h >= 5:
                    c = (h - 5) // 2
                    pool.wait_ge(mix_done, 2 * c + 2)
                    pool.wait_ge(norm_inv, 2 * c + 2)
                    pool.tensor_tensor(moT[:, c, :], moT[:, c, :], norm[:, c % 2, :], ALU.mult).then_inc(mix_norm, 1)

            def split2_lo(c):
                for m in range(2):
                    pool.wait_ge(qk_hi, 2 * KT + 2 * c + m + 1)
                    pool.tensor_tensor(qk2[c % 2][:, m, 1, :], dense[:, m * KT + c, :], qk2[c % 2][:, m, 0, :].bitcast(F32), ALU.subtract)\
                        .then_inc(qk_lo, 1)

            split2_lo(0)
            for h in range(H + 4):
                if h % 2 == 0 and h // 2 + 1 < KT:
                    split2_lo(h // 2 + 1)
                if h % 2 == 1 and h >= 5:
                    c = (h - 5) // 2
                    pool.wait_ge(av_hi, c + 1)
                    pool.tensor_tensor(T_lo[:, c, :], norm[:, 1, :], T_hi[:, c, :].bitcast(F32), ALU.subtract).then_inc(av_done, 1)
                if 2 <= h < H + 2:
                    g = h - 2
                    pool.wait_ge(v_hi, g + 1)
                    pool.tensor_tensor(v_s[:, :, 1, :], v_tok[:, :, g, 0:HD], v_s[:, :, 0, :].bitcast(F32), ALU.subtract).then_inc(v_lo, 1)
            pool.wait_ge(mo_hi, 1)
            pool.tensor_tensor(A_lo[:, KT // 2:, :], moT[:, KT // 2:, :], A_hi[:, KT // 2:, :].bitcast(F32), ALU.subtract).then_inc(mo_lo, 1)
            pool.wait_ge(in_small, 16 * 7)
            pool.wait_ge(x16_dve, 1)
            pool.tensor_tensor(x_rest[:, SH:], mo[:, SH:], x16[0][:, SH:], ALU.subtract).then_inc(x16_pool, 1)
            pool.wait_ge(x16_act, 1)
            pool.tensor_tensor(x16[2][:, SH:], x_rest[:, SH:], x16[1][:, SH:], ALU.subtract).then_inc(x16_pool, 1)
            pool.wait_ge(routed, 1)
            with pool.Fori(0, NE) as g:
                expert(g, g)
            more = pool.value_load(over[0:1, 0:1])
            fetch(0)
            with pool.If(more > 0):
                with pool.Fori(1, ROUNDS) as r:
                    with pool.Fori(0, NE) as e:
                        expert(r * NE + e, e)
                    fetch(r)
        @block.scalar
        def _(act):
            seq = [0]

            def link(ins):
                seq[0] += 1
                ins.then_inc(act_seq, 1)
                act.wait_ge(act_seq, seq[0])


            def hi(turn, k, first):
                if k % 2 == 0:
                    act.wait_ge(raw_in[(k // 2) % RAW], (turn + k // TURN + 1) * 16)
                act.wait_ge(used, first + k + 1)
                act.activation(whi[:, k % SPLIT, :], halves(k), ACT.Copy).then_inc(hi_done, 1)

            act.wait_ge(var_ready, 1)
            act.activation(small[:, 8:8 + NT], small[:, 4:4 + NT], ACT.Sqrt).then_inc(std_ready, 1)
            for k in range(AHEAD):
                hi(0, k, 0)
            for i in range(KT):
                gp_wait(act, "xnT", i)
                act.activation(A_hi[:, i, :], gp_bank("xnT", i)[:, 0:N], ACT.Copy).then_inc(hi_copy, 1)
            act.wait_ge(in_small, 16 * 7)
            act.activation(wf_s[:, 0, :], wf_sb[:, :], ACT.Copy).then_inc(wf_split, 1)
            with act.Fori(0, EB) as m:
                for j in range(TURN):
                    hi(m, j + AHEAD, m * TURN)
            act.wait_ge(sp_abs, 1)
            link(act.activation(small[:, 40:44], small[:, 36:40], ACT.Exp, scale=-1.0))
            act.activation(small[:, 44:48], small[:, 40:44], ACT.Ln, bias=1.0).then_inc(sp_ln, 1)
            act.wait_ge(consts, 14)
            for i in range(2 * NT):
                gp_wait(act, "vT", i)
                act.activation(v_tok[:, i // 2, H // 2 * (i % 2):H // 2 * (i % 2 + 1), 0:HD],
                               gp_bank("vT", i)[:, :].rearrange("p (h d) -> p h d", d=HD), ACT.Copy).then_inc(gp_act, 1)
            def kv_high(g):
                own, other = (slice(HD * (p % 2), HD * (p % 2) + HD) for p in (g, g + 1))
                b = bank[g % 2][:, 0:2 * (HD + 1)].rearrange("p (f d) -> p f d", f=2)
                act.wait_ge(kv_full, g + 1)
                if g >= 2:
                    act.wait_ge(mix_full, g - 1)
                act.activation(kv[g % 2][:, 0, :, own], b[:, :, 0:HD], ACT.Copy)
                act.activation(kv[g % 2][:, 0, :, other], b[:, :, HD:HD + 1].to_broadcast([P, 2, HD]), ACT.Copy).then_inc(kv_hi, 1)

            relus = 0
            for h in range(H):
                if h >= 2:
                    act.wait_ge(qf_lo, h - 1)
                    act.wait_ge(kv_full, h - 1)
                elif h == 0:
                    act.wait_ge(gp_full, gp["vT", 2 * NT - 1] + 1)
                for i in range(4):
                    dst, src = feature(h, i)
                    gp_wait(act, "feat", 4 * h + i)
                    act.activation(dst, src, ACT.Relu, scale=-1.0).then_inc(feat_relu, 1)
                    relus += 1
                    act.wait_ge(feat_relu, relus)
                    act.activation(dst, dst, ACT.Exp, scale=-1.0).then_inc(feat_exp, 1)
                act.wait_ge(feat_done, 4 * h + 2)
                if h >= 2:
                    act.wait_ge(mix_full, h - 1)
                act.activation(qf_s[h % 2][:, 0, :, :], qf[h % 2], ACT.Copy).then_inc(qf_hi, 1)
                if h >= 1:
                    kv_high(h - 1)
            kv_high(H - 1)
            with act.Fori(0, 3) as m:
                for j in range(TURN):
                    if j == 0:
                        act.wait_ge(t_free, m + 1)
                    act.wait_ge(used, m * (2 * TURN) + EB * TURN + j + 1 + SPLIT)
                    act.activation(T_hi[:, j, :], bank[j % BANKS][:, 0:N], ACT.Identity,
                                   bias=bcur[:, j:j + 1]).then_inc(t_hi_done, 1)
                    hi(m * 2 + EB, j + AHEAD, m * (2 * TURN) + EB * TURN)
                for j in range(TURN):
                    hi(m * 2 + EB + 1, j + AHEAD, m * (2 * TURN) + (EB + 1) * TURN)
            def split2_hi(c):
                if c >= 2:
                    act.wait_ge(sc_full, NT * (2 * (c - 2) + 2))
                for m in range(2):
                    act.activation(qk2[c % 2][:, m, 0, :], dense[:, m * KT + c, :], ACT.Copy).then_inc(qk_hi, 1)

            act.wait_ge(used, PROJ_PIECES - TURN + SPLIT)
            act.wait_ge(evicted, PROJ_PIECES - 2 * TURN + BANKS)
            act.wait_ge(mix_full, H)
            act.wait_ge(mix_norm, KT)
            split2_hi(0)
            for i in range(2 * NT):
                gp_wait(act, "v2T", i)
                act.activation(v_tok[:, i // 2, H // 2 * (i % 2):H // 2 * (i % 2 + 1), 0:HD],
                               gp_bank("v2T", i)[:, :].rearrange("p (h d) -> p h d", d=HD), ACT.Copy).then_inc(gp_act, 1)
            for h in range(H + 4):
                if h % 2 == 0 and h // 2 + 1 < KT:
                    split2_hi(h // 2 + 1)
                if 2 <= h < H + 2:
                    g = h - 2
                    if g >= 2:
                        act.wait_ge(av_full, g - 1)
                    for t in range(NT):
                        act.wait_ge(pt_full, NT * g + t + 1)
                        act.activation(probT[g % 2][:, 0, t, :], pt_bank[t][:, 0:N], ACT.Copy).then_inc(pt_hi, 1)
                if h % 2 == 1 and h >= 5:
                    c = (h - 5) // 2
                    act.wait_ge(av_sum, 2 * c + 2)
                    act.activation(T_hi[:, c, :], norm[:, 1, :], ACT.Copy).then_inc(av_hi, 1)
                if h < H:
                    act.wait_ge(neg_ready, h + 1)
                    for t in range(NT):
                        act.activation(prob[h % 2][:, t, :], prob[h % 2][:, t, :], ACT.Exp,
                                       bias=small[:, 64 + 16 * (h % 2) + t:65 + 16 * (h % 2) + t],
                                       accum_out=small[:, 68 + 16 * (h % 2) + t:69 + 16 * (h % 2) + t]).then_inc(exp_done, 1)
                if 2 <= h < H + 2:
                    g = h - 2
                    if g >= 1:
                        act.wait_ge(av_full, g)
                    act.activation(v_s[:, :, 0, :], v_tok[:, :, g, 0:HD], ACT.Copy).then_inc(v_hi, 1)
                if 3 <= h < H + 3:
                    g = h - 3
                    act.wait_ge(av_full, g + 1)
                    if g >= 1:
                        act.wait_ge(av_sum, g)
                    act.activation(norm[0:HD, 0, :], av_bank[g % 2][HD:P, 0:N], ACT.Copy).then_inc(av_left, 1)
            act.activation(A_hi[:, KT // 2:, :], moT[:, KT // 2:, :], ACT.Copy).then_inc(mo_hi, 1)
            act.activation(A_hi[:, 0:KT // 2, :], moT[:, 0:KT // 2, :], ACT.Copy).then_inc(mo_hi, 1)
            for i in range(2 * TURN):
                hi(9, i + AHEAD, PROJ_PIECES)
            act.wait_ge(var_ready, 2)
            act.activation(small[:, 8:8 + NT], small[:, 4:4 + NT], ACT.Sqrt).then_inc(std_ready, 1)
            act.wait_ge(xl_ready, 1)
            for i in range(KT):
                gp_wait(act, "xlT", i)
                act.activation(dense[:, i, :], gp_bank("xlT", i)[:, 0:N], ACT.Copy).then_inc(gp_act, 1)
            act.wait_ge(x16_pool, 1)
            act.activation(x16[1][:, SH:], x_rest[:, SH:], ACT.Copy).then_inc(x16_act, 1)
            act.wait_ge(cent, 1)
            act.activation(rt[:, 1], rt[:, 0], ACT.Exp).then_inc(rexp, 1)


            def hi_f(g, k):
                if k % 2 == 0:
                    act.wait_ge(raw_in[(k // 2) % RAW], (g * F_TURNS + (TURNS + k // TURN + 1)) * 16)
                act.wait_ge(used, g * F_PIECES + LAYER_PIECES + k + 1)
                act.activation(whi[:, k % SPLIT, :], halves(k), ACT.Copy).then_inc(hi_done, 1)

            def gathered(g):
                for j in range(G_BANKS):
                    ks = min(GK, KT - j * GK)
                    act.wait_ge(g_full, g * G_BANKS + j + 1)
                    act.activation(xg[:, j * GK:j * GK + ks, 0, :], bank[BANKS + j][:, 0:ks * C].rearrange("p (k c) -> p k c", k=ks),
                                   ACT.Copy).then_inc(g_hi, 1)

            def group(g, i, pieces):
                act.wait_ge(used, g * F_PIECES + LAYER_PIECES + pieces + SPLIT)
                act.wait_ge(f_evicted, g * F_GROUPS + i + 1)
                act.activation(left[:, i % 4, :], bank[i % BANKS][:, 0:C], ACT.Identity, bias=bcur[:, i:i + 1]).then_inc(f_left, 1)

            def hidden(g, i):
                act.wait_ge(f_evicted, g * F_GROUPS + i + 1 + BANKS)
                act.activation(hid[:, i, 0, :], h_raw[:, i % 4, :], ACT.Relu).then_inc(h_hi, 1)

            def expert(g, e):
                act.wait_ge(b_ready, g + 1)
                for i in range(FT):
                    hi_f(g, i + AHEAD)
                    group(g, i, i + 1)
                    if i >= 1:
                        hidden(g, i - 1)
                hidden(g, FT - 1)
                for i in range(KT):
                    for k in range(2):
                        hi_f(g, FT + 2 * i + k + AHEAD)
                    group(g, FT + i, FT + 2 * i + 2)
                gathered(g + 1)
                act.wait_ge(y_in, g * 32 + 32)
                for i in range(2):
                    act.wait_ge(y_full, g * Y_BANKS + i + 1 + Y_BANKS)
                    act.activation(y_main[:, i * 512:(i + 1) * 512], bank[BANKS + Y_BANK[i]][:, :], ACT.Copy).then_inc(y_free, 1)
                for i in range(2):
                    act.wait_ge(y_full, g * Y_BANKS + i + 3 + Y_BANKS)
                    act.activation(y_rest[0:C - P, i * 512:(i + 1) * 512], bank[BANKS + Y_BANK[2 + i]][0:C - P, :], ACT.Copy).then_inc(y_free, 1)
                act.wait_ge(y_free, g * Y_BANKS + 3 * Y_BANKS)
                act.dma_start(yrows[bass.ds(e * C, P), :], y_main).then_inc(y_in, 16)
                act.dma_start(yrows[bass.ds(e * C + P, C - P), :], y_rest[0:C - P, :]).then_inc(y_in, 16)

            act.sem_inc(y_free, 2 * Y_BANKS)
            act.sem_inc(y_in, 32)
            gathered(0)
            with act.Fori(0, NE) as g:
                expert(g, g)
            act.wait_ge(y_in, NE * 32 + 32)
            act.sem_inc(y_all, 1)
            act.wait_ge(routed, 1)
            more = act.value_load(over[0:1, 0:1])
            with act.If(more > 0):
                with act.Fori(1, ROUNDS) as r:
                    act.wait_ge(fin, NT * r)
                    with act.Fori(0, NE) as e:
                        expert(r * NE + e, e)
                    act.wait_ge(y_in, (r + 1) * (NE * 32) + 32)
                    act.sem_inc(y_all, 1)

        @block.tensor
        def _(pe):
            def piece(k, dst, rhs_hi, rhs_lo, start, stop, n=KT):
                w_hi = whi[:, k % SPLIT, :].rearrange("p (c o) -> p c o", c=n)
                w_lo = wlo[:, k % SPLIT, :].rearrange("p (c o) -> p c o", c=n)
                for c in range(n):
                    pe.matmul(dst, w_hi[:, c, :], rhs_hi[:, c, :], start=(start and c == 0), stop=False)
                    pe.matmul(dst, w_hi[:, c, :], rhs_lo[:, c, :], start=False, stop=False)
                    last = pe.matmul(dst, w_lo[:, c, :], rhs_hi[:, c, :], start=False, stop=(stop and c == n - 1))
                return last

            pe.sem_inc(used, SPLIT)
            pe.wait_ge(consts, 4)
            pe.wait_ge(xn_ready, NT)
            for i in range(KT):
                gp_take(pe, "xnT", i)
                for t in range(NT):
                    last = pe.transpose(gp_bank("xnT", i)[:, t * P:(t + 1) * P], mo_t[:, t, i * P:(i + 1) * P], ident[:, :])
                last.then_inc(gp_full, 1)
            pe.wait_ge(consts, 14)
            pe.wait_ge(a_ready, KT)
            for t in range(NT):
                last = pe.matmul(bank[BANKS + t][:, 0:N], zero16[:, 0:P], zero16, start=True, stop=True)
            with pe.Fori(0, EB) as m:
                for j in range(TURN):
                    pe.wait_ge(lo_done, m * TURN + j + 1 + TURN)
                    pe.wait_ge(evicted, m * TURN + j + 1)
                    piece(j, bank[j % BANKS][:, 0:N], A_hi, A_lo, True, True).then_inc(used, 1)
                    if j < 4:
                        pe.wait_ge(ekey_ready, m * 4 + j + 1)
                        for i in range(4):
                            last = pe.transpose(bank[7][:, i * P:(i + 1) * P], kb[:, i, :], ident[:, :])
                        last.then_inc(ekey_turned, 1)
                    else:
                        pe.wait_ge(hots_ready, m * 4 + j - 3)
                        for i in range(4):
                            for t in range(NT):
                                last = pe.matmul(bank[BANKS + t][:, 0:N], hot_s[:, i, t * P:(t + 1) * P], hot_d[:, i, :],
                                                 start=False, stop=True, skip_group_check=True)
                        last.then_inc(hots_used, 1)
            pe.wait_ge(evicted, EB * TURN + BANKS)
            pe.wait_ge(mask_read, NT)
            for i in range(2 * NT):
                gp_take(pe, "vT", i)
                for c in range(4):
                    last = pe.transpose(gp_bank("vT", i)[:, c * P:(c + 1) * P],
                                        dense[:, 2 * KT + 4 * (i % 2) + c, i // 2 * P:(i // 2 + 1) * P], ident[:, :])
                last.then_inc(gp_full, 1)
            pe.wait_ge(wf_split, 2)
            for h in range(H + 2):
                if h < H:
                    lo = HD * (h % 2)
                    pe.wait_ge(qk_lo, 2 * (h // 2) + 2)
                    for i in range(4):
                        gp_take(pe, "feat", 4 * h + i)
                        b = gp_bank("feat", 4 * h + i)
                        q, k = (qk[h // 2 % 2][lo:lo + HD, m] for m in range(2))
                        w = wf_s[lo:lo + HD]
                        for n, (x_part, w_part) in enumerate(((0, 0), (0, 1), (1, 0))):
                            if i < 2:
                                last = pe.matmul(b[:, 0:N], w[:, w_part, i * P:(i + 1) * P], q[:, x_part, :], start=(n == 0), stop=(n == 2))
                        for t in range(0, 2) if i == 2 else range(2, 3) if i == 3 else ():
                            for n, (x_part, w_part) in enumerate(((0, 0), (0, 1), (1, 0))):
                                last = pe.matmul(b[:, (t % 2) * FD:(t % 2 + 1) * FD], k[:, x_part, t * P:(t + 1) * P],
                                                 w[:, w_part, :], start=(n == 0), stop=(n == 2))
                        last.then_inc(gp_full, 1)
                if h >= 2:
                    g = h - 2
                    pe.wait_ge(kv_ready, g + 1)
                    if g >= 2:
                        pe.wait_ge(mix_done, g - 1)
                    pe.wait_ge(qf_lo, g + 1)
                    for n, (kv_part, q_part) in enumerate(((0, 0), (0, 1), (1, 0))):
                        for f in range(2):
                            last = pe.matmul(bank[2 + g % 2][:, 0:N], kv[g % 2][:, kv_part, f, :], qf_s[g % 2][:, q_part, f, :],
                                             start=(n == 0 and f == 0), stop=(n == 2 and f == 1))
                    last.then_inc(mix_full, 1)
                if 1 <= h <= H:
                    g = h - 1
                    pe.wait_ge(feat_done, 4 * g + 4)
                    if g == 0:
                        pe.wait_ge(gp_act, gp_by[:gp["vT", 2 * NT - 1] + 1].count("act"))
                    if g >= 2:
                        pe.wait_ge(kv_ready, g - 1)
                    for f in range(2):
                        for t in range(NT):
                            last = pe.matmul(bank[g % 2][:, f * (HD + 1):(f + 1) * (HD + 1)], kf[g % 2][:, t, f * P:(f + 1) * P],
                                             v_tok[:, t, g, :], start=(t == 0), stop=(t == NT - 1))
                    last.then_inc(kv_full, 1)
            pe.wait_ge(mix_done, H)
            with pe.Fori(0, 3) as m:
                base = m * (2 * TURN) + EB * TURN
                for j in range(2 * TURN):
                    pe.wait_ge(lo_done, base + j + 1 + TURN)
                    pe.wait_ge(evicted, base + (TURN + BANKS if j == TURN else j + 1))
                    src = (A_hi, A_lo) if j < TURN else (T_hi, T_lo)
                    last = piece(j, bank[j % BANKS][:, 0:N], *src, True, True)
                    last.then_inc(used, 1)
            pe.wait_ge(evicted, PROJ_PIECES + BANKS)
            for i in range(2 * NT):
                gp_take(pe, "v2T", i)
                for c in range(4):
                    last = pe.transpose(gp_bank("v2T", i)[:, c * P:(c + 1) * P],
                                        dense[:, 2 * KT + 4 * (i % 2) + c, i // 2 * P:(i // 2 + 1) * P], ident[:, :])
                last.then_inc(gp_full, 1)
            pe.wait_ge(gp_act, gp_by[:gp["v2T", 2 * NT - 1] + 1].count("act"))
            for h in range(H + 3):
                if h < H:
                    lo = HD * (h % 2)
                    q, k = (qk2[h // 2 % 2][lo:lo + HD, m] for m in range(2))
                    pe.wait_ge(qk_lo, 2 * KT + 2 * (h // 2) + 2)
                    for t in range(NT):
                        if h >= 1:
                            pe.wait_ge(sc_done, NT * (h - 1) + t + 1)
                        for n, (q_part, k_part) in enumerate(((0, 0), (0, 1), (1, 0))):
                            last = pe.matmul(sc_bank[t][:, 0:N], q[:, q_part, t * P:(t + 1) * P], k[:, k_part, :],
                                             start=(n == 0), stop=(n == 2))
                        last.then_inc(sc_full, 1)
                if h >= 3:
                    g = h - 3
                    pe.wait_ge(pt_lo, NT * g + NT)
                    pe.wait_ge(v_lo, g + 1)
                    if g >= 2:
                        pe.wait_ge(av_sum, g - 1)
                    for part in range(2):
                        for t in range(NT):
                            last = pe.matmul(av_bank[g % 2][:, 0:N], v_s[:, t, :, :].rearrange("p a d -> p (a d)"), probT[g % 2][:, part, t, :],
                                             start=(part == 0 and t == 0), stop=(part == 1 and t == NT - 1))
                    last.then_inc(av_full, 1)
                if 1 <= h <= H:
                    g = h - 1
                    pe.wait_ge(prob_ready, g + 1)
                    for mt in range(NT):
                        if g >= 1:
                            pe.wait_ge(pt_lo, NT * (g - 1) + mt + 1)
                        for t in range(NT):
                            last = pe.transpose(pt_bank[mt][:, t * P:(t + 1) * P], prob[g % 2][:, t, mt * P:(mt + 1) * P], ident[:, :])
                        last.then_inc(pt_full, 1)
            pe.wait_ge(av_done, KT)
            for i in range(KT):
                k = PROJ_PIECES + 2 * i
                pe.wait_ge(lo_done, k + 1 + TURN)
                pe.wait_ge(evicted, PROJ_PIECES + i + 1)
                piece(2 * i, bank[i % BANKS][:, 0:N], T_hi, T_lo, True, False).then_inc(used, 1)
                pe.wait_ge(lo_done, k + 2 + TURN)
                if i == 0:
                    pe.wait_ge(mo_lo, 2)
                piece(2 * i + 1, bank[i % BANKS][:, 0:N], A_hi, A_lo, False, True).then_inc(used, 1)
            for i in range(2 * NT):
                gp_take(pe, "x2", i)
                if i == 0:
                    pe.wait_ge(evicted, PROJ_PIECES + KT + BANKS)
                for c in range(4):
                    last = pe.transpose(gp_bank("x2", i)[:, c * P:(c + 1) * P],
                                        dense[:, 4 * (i % 2) + c, i // 2 * P:(i // 2 + 1) * P], ident[:, :])
                last.then_inc(gp_full, 1)
            pe.wait_ge(xl_ready, 1)
            for i in range(KT + 2):
                if i < KT:
                    gp_take(pe, "xlT", i)
                    for t in range(NT):
                        last = pe.transpose(gp_bank("xlT", i)[:, t * P:(t + 1) * P], mo_t[:, t, i * P:(i + 1) * P], ident[:, :])
                    last.then_inc(gp_full, 1)
                if i >= 2:
                    c = i - 2
                    pe.wait_ge(gp_act, gp_by[:gp["xlT", c] + 1].count("act"))
                    for t in range(NT):
                        last = pe.matmul(bank[t][:, 0:NE], dense[:, c, t * P:(t + 1) * P], wr_sb[:, c, :],
                                         start=(c == 0), stop=(c == KT - 1))
            last.then_inc(logits, 1)
            gp_take(pe, "rank", 0)
            pe.wait_ge(sel_ready, 1)
            for t in range(NT + 1):
                for s in range(min(t + 1, NT)):
                    last = pe.matmul(gp_bank("rank", 0)[:, t * NE:(t + 1) * NE], (later16 if s == t else ones16)[:, :], sel16[:, s, :],
                                     start=(s == 0), stop=(s == min(t, NT - 1)))
            last.then_inc(gp_full, 1)
            pe.wait_ge(x16_pool, 2)
            pe.wait_ge(x16_dve, 5)
            pe.wait_ge(gp_dve, gp_by.count("dve"))

            def gather(g):
                pe.wait_ge(pick_ready, g + 1)
                for j in range(G_BANKS):
                    pe.wait_ge(y_free, g * Y_BANKS + Y_BANK.index(j) + 1)
                    for k in range(j * GK, min(KT, (j + 1) * GK)):
                        o = bank[BANKS + j][:, (k - j * GK) * C:(k - j * GK + 1) * C]
                        for a in range(3):
                            for t in range(NT):
                                last = pe.matmul(o, X16[a][:, t, k * P:(k + 1) * P], pick[:, t, :],
                                                 start=(a == 0 and t == 0), stop=(a == 2 and t == NT - 1))
                    last.then_inc(g_full, 1)

            def piece_f(k, dst, rhs, start, stop):
                w_hi = whi[:, k % SPLIT, :].rearrange("p (c o) -> p c o", c=KT)
                w_lo = wlo[:, k % SPLIT, :].rearrange("p (c o) -> p c o", c=KT)
                for c in range(KT):
                    pe.matmul(dst, w_hi[:, c, :], rhs[:, c, :], start=(start and c == 0), stop=False)
                    last = pe.matmul(dst, w_lo[:, c, :], rhs[:, c, :], start=False, stop=(stop and c == KT - 1))
                return last

            def expert(g, e):
                first = g * F_PIECES + LAYER_PIECES
                pe.wait_ge(g_done, (g + 1) * G_BANKS)
                for i in range(FT):
                    pe.wait_ge(lo_done, first + i + 1 + TURN)
                    pe.wait_ge(f_evicted, g * F_GROUPS + i + 1)
                    piece_f(i, bank[i % BANKS][:, 0:2 * C], xg[:, :, :, :].rearrange("p k a c -> p k (a c)"), True, True).then_inc(used, 1)
                for i in range(KT):
                    pe.wait_ge(f_evicted, g * F_GROUPS + FT + i + 1)
                    for a in range(2):
                        k = FT + 2 * i + a
                        pe.wait_ge(lo_done, first + k + 1 + TURN)
                        if i == 0:
                            pe.wait_ge(h_done, g * FT + (a + 1) * KT + BANKS)
                        piece_f(k, bank[i % BANKS][:, 0:2 * C], hid[:, a * KT:(a + 1) * KT, :, :].rearrange("p k a c -> p k (a c)"),
                                a == 0, a == 1).then_inc(used, 1)
                gather(g + 1)
                for n in range(Y_BANKS):
                    part, i = divmod(n, 2)
                    cols = (slice(0, P), slice(P, C))[part]
                    rows = cols.stop - cols.start
                    pe.wait_ge(f_evicted, g * F_GROUPS + FT + 4 * i + 4 + BANKS)
                    if n == 0:
                        pe.wait_ge(y_free, g * Y_BANKS + Y_BANKS + 1)
                    else:
                        pe.wait_ge(g_done, (g + 1) * G_BANKS + Y_BANK[n] + 1)
                    for c in range(4):
                        last = pe.transpose(bank[BANKS + Y_BANK[n]][0:rows, c * P:(c + 1) * P], yT[:, 4 * i + c, cols], ident[:, :])
                    last.then_inc(y_full, 1)

            pe.sem_inc(y_full, Y_BANKS)
            gather(0)
            with pe.Fori(0, NE) as g:
                expert(g, g)
            pe.wait_ge(routed, 1)
            more = pe.value_load(over[0:1, 0:1])
            with pe.If(more > 0):
                with pe.Fori(1, ROUNDS) as r:
                    with pe.Fori(0, NE) as e:
                        expert(r * NE + e, e)

        @block.vector
        def _(dve):
            seq = [0]

            def link(ins):
                seq[0] += 1
                ins.then_inc(dve_seq, 1)
                dve.wait_ge(dve_seq, seq[0])

            dve.sem_inc(lo_done, TURN)
            dve.sem_inc(evicted, BANKS)
            dve.sem_inc(f_evicted, BANKS)
            dve.sem_inc(h_done, BANKS)

            def lo(k, first):
                dve.wait_ge(hi_done, first + k + 1)
                dve.tensor_tensor(wlo[:, k % SPLIT, :], halves(k), whi[:, k % SPLIT, :].bitcast(F32), ALU.subtract).then_inc(lo_done, 1)

            def normalize(n):
                mv = small[:, 12:12 + 2 * NT].rearrange("p (t a) -> p t a", a=2)
                st = small[:, 96:96 + 12 * NT].rearrange("p (t a b) -> p t a b", a=2, b=6)
                for t in range(NT):
                    if n == 0:
                        dve.wait_ge(in_x[t], 16)
                    for a in range(2):
                        last = dve.bn_stats(st[:, t, a, :], x_tok[:, t, a * 512:(a + 1) * 512])
                link(last)
                for t in range(NT):
                    last = dve.bn_aggr(mv[:, t, :], st[:, t, :, :].rearrange("p a b -> p (a b)"))
                link(last)
                dve.tensor_scalar(small[:, 4:4 + NT], mv[:, :, 1], EPS, None, ALU.add).then_inc(var_ready, 1)
                dve.wait_ge(std_ready, n + 1)
                r = small[:, 0:NT]
                v = small[:, 4:4 + NT]
                w = small[:, 8:8 + NT]
                link(dve.reciprocal(r, w))
                link(dve.tensor_tensor(w, r, r, ALU.mult))
                link(dve.tensor_tensor(w, w, v, ALU.mult))
                link(dve.tensor_scalar(w, w, -0.5, 1.5, ALU.mult, ALU.add))
                link(dve.tensor_tensor(r, r, w, ALU.mult))
                for t in range(NT):
                    ins = dve.tensor_scalar(mo_t[:, t, :], x_tok[:, t, :], mv[:, t, 0:1], small[:, t:t + 1], ALU.subtract, ALU.mult)
                    if n == 0:
                        ins.then_inc(xn_ready, 1)
                if n == 1:
                    ins.then_inc(xl_ready, 1)

            normalize(0)
            for i in range(KT):
                dve.wait_ge(hi_copy, i + 1)
                dve.tensor_tensor(A_lo[:, i, :], gp_bank("xnT", i)[:, 0:N], A_hi[:, i, :].bitcast(F32), ALU.subtract)\
                   .then_inc(gp_dve, 1)
            dve.wait_ge(gp_dve, KT)
            dve.sem_inc(a_ready, KT)
            for k in range(AHEAD):
                lo(k, 0)
            dve.wait_ge(consts, 14)
            dve.wait_ge(in_small, 16 * 7)
            dve.wait_ge(in_edges, 16)
            dve.wait_ge(wf_split, 1)
            dve.tensor_tensor(wf_s[:, 1, :], wf_sb[:, :], wf_s[:, 0, :].bitcast(F32), ALU.subtract).then_inc(wf_split, 1)
            with dve.Fori(0, EB) as m:
                es, ed, ety = ecol[:, 0:ET], ecol[:, ET:2 * ET], ecol[:, 2 * ET:3 * ET]
                steps = [0]

                def step(ins):
                    steps[0] += 1
                    ins.then_inc(edup_done, 1)
                    dve.wait_ge(edup_done, m * EDGE_STEPS + steps[0])

                for j in range(TURN):
                    if j == 0:
                        step(dve.tensor_copy(ecol, ecol_i[:, bass.ds(m, 1), :].rearrange("p a c -> p (a c)")))
                        step(dve.tensor_scalar(ekey, es, float(N), None, ALU.mult))
                        step(dve.tensor_tensor(ekey, ekey, ed, ALU.add))
                        step(dve.tensor_scalar(eval_, ety, 0.0, 4.0, ALU.is_equal, ALU.mult))
                        step(dve.tensor_tensor(eval_, eval_, ety, ALU.add))
                        step(dve.tensor_tensor(eval_, eval_, epow, ALU.mult))
                        step(dve.tensor_scalar(escale, escale, 2.0 ** (4 * ET), None, ALU.mult))
                        step(dve.tensor_scalar(eval_, eval_, escale, None, ALU.mult))
                    if j < 4:
                        for i in range(4):
                            last = dve.tensor_copy(kb[:, i, :], ekey[:, 4 * j + i:4 * j + i + 1].to_broadcast([P, P]))
                        last.then_inc(ekey_ready, 1)
                    else:
                        if j > 4:
                            dve.wait_ge(hots_used, m * 4 + j - 4)
                        for i in range(4):
                            c = 4 * (j - 4) + i
                            dve.tensor_scalar(hot_s[:, i, :], node_iota, es[:, c:c + 1], None, ALU.is_equal)
                            last = dve.tensor_scalar(hot_d[:, i, :], node_iota, ed[:, c:c + 1], eval_[:, c:c + 1], ALU.is_equal, ALU.mult)
                        last.then_inc(hots_ready, 1)
                    dve.wait_ge(used, m * TURN + j + 1 + SPLIT)
                    dve.tensor_copy(dense[:, bass.ds(m * KT + j, 1), :].rearrange("p a n -> p (a n)"), bank[j % BANKS][:, 0:N]).then_inc(evicted, 1)
                    lo(j + AHEAD, m * TURN)
                    if j < 4:
                        dve.wait_ge(ekey_turned, m * 4 + j + 1)
                        for i in range(4):
                            c = 4 * j + i
                            step(dve.scalar_tensor_tensor(out=ejunk, in0=bank[7][:, i * P:(i + 1) * P], scalar=ekey[:, c:c + 1],
                                                          in1=later[:, :], op0=ALU.is_equal, op1=ALU.mult, accum_out=edup[:, c:c + 1]))
                    if j == 3:
                        step(dve.tensor_scalar(edup, edup, 0.0, None, ALU.is_equal))
                        step(dve.tensor_tensor(eval_, eval_, edup, ALU.mult))
                dve.wait_ge(hots_used, m * 4 + 4)
                assert steps[0] == EDGE_STEPS, steps[0]

            neg, ab, ln = small[:, 32:36], small[:, 36:40], small[:, 44:48]
            link(dve.tensor_scalar(neg, etw_sb[:, :], -1.0, None, ALU.mult))
            dve.tensor_tensor(ab, neg, etw_sb[:, :], ALU.max).then_inc(sp_abs, 1)
            pos_w = small[:, 132:136]
            link(dve.tensor_scalar(pos_w, etw_sb[:, :], 0.0, None, ALU.max))
            for t in range(NT):
                dve.tensor_copy(mask8[:, t, :], bank[BANKS + t][:, 0:N]).then_inc(mask_read, 1)

            def invert(c, half):
                dve.wait_ge(norm_ready, 2 * c + 2)
                n = norm[:, c % 2, half * N // 2:(half + 1) * N // 2]
                dve.reciprocal(n, n).then_inc(norm_inv, 1)

            for h in range(H + 2):
                if h < H:
                    for i in range(4):
                        dst, src = feature(h, i)
                        dve.wait_ge(feat_exp, 4 * h + i + 1)
                        dve.scalar_tensor_tensor(out=dst, in0=src, scalar=0.0, in1=dst, op0=ALU.max, op1=ALU.add).then_inc(gp_dve, 1)
                        if i == 1 or i == 3:
                            dve.wait_ge(gp_dve, gp_by[:gp["feat", 4 * h + i] + 1].count("dve"))
                            dve.sem_inc(feat_done, 2)
                if h >= 2:
                    g = h - 2
                    own, other = (slice(HD * (p % 2), HD * (p % 2) + HD) for p in (g, g + 1))
                    o = bank[2 + g % 2]
                    dve.wait_ge(mix_full, g + 1)
                    if g >= 4:
                        dve.wait_ge(mix_norm, (g - 4) // 2 + 1)
                    dve.tensor_scalar(norm[own, g // 2 % 2, :], o[other, 0:N], 1e-6, None, ALU.add).then_inc(norm_ready, 1)
                    dve.tensor_copy(moT[own, g // 2, :], o[own, 0:N]).then_inc(mix_done, 1)
                if 1 <= h <= H:
                    g = h - 1
                    own, other = (slice(HD * (p % 2), HD * (p % 2) + HD) for p in (g, g + 1))
                    b = bank[g % 2][:, 0:2 * (HD + 1)].rearrange("p (f d) -> p f d", f=2)
                    dve.wait_ge(kv_hi, g + 1)
                    dve.tensor_tensor(kv[g % 2][:, 1, :, own], b[:, :, 0:HD], kv[g % 2][:, 0, :, own].bitcast(F32), ALU.subtract)
                    dve.tensor_tensor(kv[g % 2][:, 1, :, other], b[:, :, HD:HD + 1].to_broadcast([P, 2, HD]),
                                      kv[g % 2][:, 0, :, other].bitcast(F32), ALU.subtract).then_inc(kv_ready, 1)
                if h >= 3:
                    invert((h - 3) // 2, (h - 3) % 2)
            invert(KT - 1, 1)

            dve.wait_ge(sp_ln, 1)
            link(dve.tensor_tensor(ln, ln, pos_w, ALU.add))
            link(dve.tensor_scalar(ln, ln, 1.0 / SCALE, None, ALU.mult))

            def edge_mask(m):
                steps = [0]

                def step(ins):
                    steps[0] += 1
                    ins.then_inc(mask_steps, 1)
                    dve.wait_ge(mask_steps, m * MASK_STEPS + steps[0])

                mask = mask8[:, bass.ds(m, 1), :].rearrange("p a n -> p (a n)")
                step(dve.tensor_scalar(tmp.bitcast(I32), mask.bitcast(I32), 22, 7, ALU.logical_shift_right, ALU.bitwise_and))
                step(dve.tensor_copy(tab, tmp.bitcast(I32)))
                own = tab[:, bass.ds(m * P, P)]
                step(dve.tensor_scalar(diag, own, 0.0, 6.0, ALU.is_equal, ALU.mult))
                step(dve.tensor_tensor(diag, diag, ident[:, :], ALU.mult))
                step(dve.tensor_tensor(own, own, diag, ALU.add))
                step(dve.tensor_scalar(mask, tab, 0.0, NEG, ALU.is_equal, ALU.mult))
                for code, w in ((2.0, 0), (4.0, 1), (5.0, 2), (6.0, 3)):
                    step(dve.tensor_scalar(tmp, tab, code, small[:, 44 + w:45 + w], ALU.is_equal, ALU.mult))
                    step(dve.tensor_tensor(mask, mask, tmp, ALU.add))
                assert steps[0] == MASK_STEPS, steps[0]

            with dve.Fori(0, 3) as m:
                base = m * (2 * TURN) + EB * TURN
                dve.wait_ge(evicted, base + BANKS)
                dve.tensor_copy(bcur[:, 0:2 * KT], biases[:, bass.ds(m * (2 * KT), 2 * KT)]).then_inc(t_free, 1)
                dve.wait_ge(t_free, m + 1)
                for j in range(TURN):
                    dve.wait_ge(t_hi_done, m * TURN + j + 1)
                    dve.scalar_tensor_tensor(out=T_lo[:, j, :], in0=bank[j % BANKS][:, 0:N], scalar=bcur[:, j:j + 1],
                                             in1=T_hi[:, j, :].bitcast(F32), op0=ALU.add, op1=ALU.subtract).then_inc(evicted, 1)
                    lo(j + AHEAD, base)
                for j in range(TURN):
                    dve.wait_ge(used, base + TURN + j + 1 + SPLIT)
                    dve.tensor_scalar(dense[:, bass.ds(m * KT + j, 1), :].rearrange("p a n -> p (a n)"), bank[j % BANKS][:, 0:N],
                                      bcur[:, KT + j:KT + j + 1], None, ALU.add).then_inc(evicted, 1)
                    lo(j + AHEAD, base + TURN)
                    if j == 1:
                        edge_mask(m)
            for h in range(H + 4):
                if 1 <= h <= H:
                    g = h - 1
                    s = 64 + 16 * (g % 2)
                    dve.wait_ge(exp_done, NT * g + NT)
                    link(dve.reciprocal(small[:, s + 12:s + 12 + NT], small[:, s + 4:s + 4 + NT]))
                    for t in range(NT):
                        last = dve.tensor_scalar(prob[g % 2][:, t, :], prob[g % 2][:, t, :], small[:, s + 12 + t:s + 13 + t], None, ALU.mult)
                    last.then_inc(prob_ready, 1)
                if h < H:
                    s = 64 + 16 * (h % 2)
                    if h == 0:
                        dve.wait_ge(gp_full, gp["v2T", 2 * NT - 1] + 1)
                    if h >= 2:
                        dve.wait_ge(pt_full, NT * (h - 2) + NT)
                    for t in range(NT):
                        dve.wait_ge(sc_full, NT * h + t + 1)
                        dve.tensor_tensor_reduce(out=prob[h % 2][:, t, :], in0=sc_bank[t][:, 0:N], in1=mask8[:, t, :],
                                                 scale=SCALE, scalar=-3e38, op0=ALU.add, op1=ALU.max,
                                                 accum_out=small[:, s + 8 + t:s + 9 + t]).then_inc(sc_done, 1)
                    dve.wait_ge(sc_done, NT * h + NT)
                    dve.tensor_scalar(small[:, s:s + NT], small[:, s + 8:s + 8 + NT], -1.0, None, ALU.mult).then_inc(neg_ready, 1)
                if 2 <= h < H + 2:
                    g = h - 2
                    for t in range(NT):
                        dve.wait_ge(pt_hi, NT * g + t + 1)
                        dve.tensor_tensor(probT[g % 2][:, 1, t, :], pt_bank[t][:, 0:N],
                                          probT[g % 2][:, 0, t, :].bitcast(F32), ALU.subtract).then_inc(pt_lo, 1)
                if h % 2 == 1 and h >= 5:
                    dve.wait_ge(av_done, (h - 5) // 2 + 1)
                if 3 <= h < H + 3:
                    g = h - 3
                    dve.wait_ge(av_left, g + 1)
                    dve.tensor_tensor(norm[HD * (g % 2):HD * (g % 2) + HD, 1, :], av_bank[g % 2][0:HD, 0:N], norm[0:HD, 0, :], ALU.add)\
                       .then_inc(av_sum, 1)
            dve.wait_ge(mo_hi, 2)
            dve.tensor_tensor(A_lo[:, 0:KT // 2, :], moT[:, 0:KT // 2, :], A_hi[:, 0:KT // 2, :].bitcast(F32), ALU.subtract).then_inc(mo_lo, 1)
            for i in range(KT):
                dve.wait_ge(used, PROJ_PIECES + 2 * i + 2 + SPLIT)
                dve.tensor_scalar(dense[:, i, :], bank[i % BANKS][:, 0:N], biases[:, 6 * KT + i:6 * KT + i + 1], None, ALU.add)\
                   .then_inc(evicted, 1)
                for k in range(2 * i + AHEAD, 2 * i + AHEAD + 2):
                    lo(k, PROJ_PIECES)
            for i in range(2 * NT):
                gp_wait(dve, "x2", i)
                r = x_tok[:, i // 2, (i % 2) * 512:(i % 2 + 1) * 512]
                dve.tensor_tensor(r, gp_bank("x2", i)[:, :], r, ALU.add).then_inc(gp_dve, 1)
            dve.wait_ge(gp_dve, gp_by[:gp["x2", 2 * NT - 1] + 1].count("dve"))
            normalize(1)
            dve.wait_ge(xl_ready, 1)
            dve.tensor_copy(x16[0][:, SH:], mo[:, SH:]).then_inc(x16_dve, 1)
            dve.tensor_copy(x16[0][:, 0:SH], mo[:, 0:SH]).then_inc(x16_dve, 1)
            dve.wait_ge(x16_dve, 2)
            dve.tensor_tensor(x_rest[:, 0:SH], mo[:, 0:SH], x16[0][:, 0:SH], ALU.subtract).then_inc(x16_dve, 1)
            dve.wait_ge(x16_dve, 3)
            dve.tensor_copy(x16[1][:, 0:SH], x_rest[:, 0:SH]).then_inc(x16_dve, 1)
            dve.wait_ge(x16_dve, 4)
            dve.tensor_tensor(x16[2][:, 0:SH], x_rest[:, 0:SH], x16[1][:, 0:SH], ALU.subtract).then_inc(x16_dve, 1)
            dve.wait_ge(logits, 1)
            cen, ex, prb, srt, sel0, sel1, pos, tm = (rt[:, i] for i in range(8))
            mx = small[:, 52:52 + NT].rearrange("p (t a) -> p t a", a=1)
            for t in range(NT):
                last = dve.tensor_tensor(cen[:, t, :], bank[t][:, 0:NE], br_sb[:, :], ALU.add)
            link(last)
            link(dve.tensor_reduce(mx, cen, AX.X, ALU.max))
            dve.tensor_tensor(cen, cen, mx.to_broadcast([P, NT, NE]), ALU.subtract).then_inc(cent, 1)
            dve.wait_ge(rexp, 1)
            link(dve.tensor_reduce(mx, ex, AX.X, ALU.add))
            link(dve.reciprocal(mx, mx))
            link(dve.tensor_tensor(prb, ex, mx.to_broadcast([P, NT, NE]), ALU.mult))
            for t in range(NT):
                link(dve.max(srt[:, t, :], prb[:, t, :]))
                link(dve.max_index(top_i[:, t, :], srt[:, t, :], prb[:, t, :]))
            ti = rt[:, 8]
            link(dve.tensor_copy(ti, top_i[:, :, :]))
            ide = eid[:, :].rearrange("p (a e) -> p a e", a=1).to_broadcast([P, NT, NE])
            link(dve.tensor_tensor(sel0, ide, ti[:, :, 0:1].to_broadcast([P, NT, NE]), ALU.is_equal))
            link(dve.tensor_tensor(sel1, ide, ti[:, :, 1:2].to_broadcast([P, NT, NE]), ALU.is_equal))
            dve.tensor_tensor(sel16[:, :, :], sel0, sel1, ALU.add).then_inc(sel_ready, 1)
            gp_wait(dve, "rank", 0)
            rk = gp_bank("rank", 0)[:, 0:NT * NE].rearrange("p (t e) -> p t e", t=NT)
            link(dve.tensor_scalar(pos, rk, float(C), float((NE - 1) * C), ALU.is_ge, ALU.mult))
            for r in range(2, ROUNDS):
                link(dve.tensor_scalar(tm, rk, float(C * r), float((NE - 1) * C), ALU.is_ge, ALU.mult))
                link(dve.tensor_tensor(pos, pos, tm, ALU.add))
            link(dve.tensor_tensor(pos, pos, rk, ALU.add))
            link(dve.tensor_tensor(pos, pos, base_e[:, :].rearrange("p (a e) -> p a e", a=1).to_broadcast([P, NT, NE]), ALU.add))
            posf = small[:, 56:56 + 2 * NT].rearrange("p (c t) -> p c t", c=2)
            for c, s in enumerate((sel0, sel1)):
                link(dve.tensor_tensor(tm, pos, s, ALU.mult))
                link(dve.tensor_reduce(posf[:, c, :].rearrange("p (t a) -> p t a", a=1), tm, AX.X, ALU.add))
            link(dve.tensor_copy(small[:, 136:136 + 2 * NT], small[:, 56:56 + 2 * NT]))
            cnt = small[:, 62:63]
            dve.tensor_reduce(cnt, gp_bank("rank", 0)[:, NT * NE:(NT + 1) * NE], AX.X, ALU.max).then_inc(gp_dve, 1)
            dve.wait_ge(gp_dve, gp_by.count("dve"))
            dve.tensor_scalar(over[:, :], cnt, float(C), None, ALU.is_gt).then_inc(routed, 1)

            def choose(g):
                for t in range(NT):
                    dve.tensor_scalar(pick_a[:, t, :], slot_iota[:, :], small[:, 56 + t:57 + t], None, ALU.is_equal).then_inc(pick_steps, 1)
                dve.wait_ge(pick_steps, g * (NT + 1) + NT)
                for t in range(NT):
                    last = dve.scalar_tensor_tensor(out=pick[:, t, :], in0=slot_iota[:, :], scalar=small[:, 59 + t:60 + t],
                                                    in1=pick_a[:, t, :], op0=ALU.is_equal, op1=ALU.add)
                last.then_inc(pick_ready, 1)
                dve.wait_ge(pick_ready, g + 1)
                dve.tensor_scalar(slot_iota[:, :], slot_iota[:, :], float(C), None, ALU.add).then_inc(pick_steps, 1)
                dve.wait_ge(pick_steps, (g + 1) * (NT + 1))

            def gathered(g):
                for j in range(G_BANKS):
                    ks = min(GK, KT - j * GK)
                    dve.wait_ge(g_hi, g * G_BANKS + j + 1)
                    dve.tensor_tensor(xg[:, j * GK:j * GK + ks, 1, :], bank[BANKS + j][:, 0:ks * C].rearrange("p (k c) -> p k c", k=ks),
                                      xg[:, j * GK:j * GK + ks, 0, :].bitcast(F32), ALU.subtract).then_inc(g_done, 1)

            def group(g, i, dst):
                dve.wait_ge(f_left, g * F_GROUPS + i + 1)
                dve.tensor_tensor(dst, bank[i % BANKS][:, C:2 * C], left[:, i % 4, :], ALU.add).then_inc(f_evicted, 1)

            def h_low(g, i):
                dve.wait_ge(h_hi, g * FT + i + 1)
                dve.scalar_tensor_tensor(out=hid[:, i, 1, :], in0=h_raw[:, i % 4, :], scalar=0.0, in1=hid[:, i, 0, :].bitcast(F32),
                                         op0=ALU.max, op1=ALU.subtract).then_inc(h_done, 1)

            def expert(g, e):
                first = g * F_PIECES + LAYER_PIECES
                for i in range(FT):
                    lo(i + AHEAD, first)
                    dve.wait_ge(h_done, g * FT + i + 1)
                    group(g, i, h_raw[:, i % 4, :])
                    if i >= 1:
                        h_low(g, i - 1)
                h_low(g, FT - 1)
                for i in range(KT):
                    for k in range(2):
                        lo(FT + 2 * i + k + AHEAD, first)
                    if i == 0:
                        dve.wait_ge(y_full, g * Y_BANKS + Y_BANKS)
                    group(g, FT + i, yT[:, i, :])
                    if i == 3:
                        choose(g + 1)
                gathered(g + 1)

            round_pos = small[:, 136:136 + 2 * NT]
            below = small[:, 142:142 + 2 * NT]
            here = small[:, 148:148 + 2 * NT]
            weight = small[:, 154:154 + 2 * NT]

            def combine(r):
                steps = [0]

                def step(ins):
                    steps[0] += 1
                    ins.then_inc(combine_steps, 1)
                    dve.wait_ge(combine_steps, r * COMBINE_STEPS + steps[0])

                step(dve.tensor_scalar(below, round_pos, float(NE * C), None, ALU.is_lt))
                step(dve.tensor_scalar(here, round_pos, 0.0, None, ALU.is_ge))
                step(dve.tensor_tensor(here, here, below, ALU.mult))
                step(dve.tensor_tensor(below, round_pos, here, ALU.mult))
                dve.tensor_copy(posi[:, :, :], below.rearrange("p (c t) -> p c t", c=2)).then_inc(rows_ready, 1)
                step(dve.tensor_tensor(weight.rearrange("p (c t) -> p c t", c=2), here.rearrange("p (c t) -> p c t", c=2),
                                       rt[:, 3, :, 0:2].rearrange("p t c -> p c t"), ALU.mult))
                step(dve.tensor_scalar(round_pos, round_pos, float(-NE * C), None, ALU.add))
                for t in range(NT):
                    for c in range(2):
                        dve.wait_ge(got[2 * t + c], 16 * r + 16)
                        ins = dve.scalar_tensor_tensor(out=x_tok[:, t, :], in0=yg[2 * t + c], scalar=weight[:, c * NT + t:c * NT + t + 1],
                                                       in1=x_tok[:, t, :], op0=ALU.mult, op1=ALU.add)
                        if c == 0:
                            step(ins)
                    ins.then_inc(fin, 1)
                dve.wait_ge(fin, NT * r + NT)
                assert steps[0] == COMBINE_STEPS, steps[0]

            choose(0)
            gathered(0)
            with dve.Fori(0, NE) as g:
                expert(g, g)
            combine(0)
            more = dve.value_load(over[0:1, 0:1])
            with dve.If(more > 0):
                with dve.Fori(1, ROUNDS) as r:
                    with dve.Fori(0, NE) as e:
                        expert(r * NE + e, e)
                    combine(r)


def kernel(**inputs):
    import numpy as np
    import concourse.bacc as bacc
    from concourse.bass_utils import run_bass_kernel_spmd

    a = {k: np.asarray(v) for k, v in inputs.items()}

    def pieces(w):
        return w.reshape(KT, P, KT, P).transpose(0, 3, 2, 1).reshape(KT, P, PIECE)

    def units(p):
        return p.reshape(-1, 2, P, PIECE).transpose(0, 2, 1, 3).reshape(-1, P, UNIT)

    def columns(v):
        return v.reshape(-1, P).T

    g = {k[7:]: v for k, v in a.items() if k.startswith("L0_gnn_")}
    first = [a["L0_mix_Wq"], a["L0_mix_Wk"], a["L0_mix_Wv"], g["wq"], g["wiq"], g["wk"], g["wik"], g["wv"], g["wiv"]]
    last = np.stack([pieces(g["wo"]), pieces(a["L0_mix_Wo"])], axis=1).reshape(2 * KT, P, PIECE)
    wall = units(np.concatenate([pieces(w) for w in first] + [last]))
    w1 = a["L0_ffn_W1"].reshape(NE, KT, P, FT, P).transpose(0, 3, 2, 1, 4).reshape(NE, FT, P, PIECE)
    w2 = a["L0_ffn_W2"].reshape(NE, 2, KT, P, KT, P).transpose(0, 4, 1, 3, 2, 5).reshape(NE, 2 * KT, P, PIECE)
    wffn = units(np.concatenate([w1, w2], axis=1).reshape(-1, P, PIECE))
    edges = np.stack([v.reshape(EB, ET, P) for v in (a["src"], a["dst"], a["edge_type_5"])], axis=1)
    arrays = {
        "x": a["x"].reshape(NT, P, DM),
        "edges": edges.reshape(EB, 3 * ET, P).transpose(2, 0, 1),
        "etw": np.broadcast_to(g["edge_type_weights"], (P, 4)),
        "bias": np.concatenate([columns(g[n]) for n in ("bq", "biq", "bk", "bik", "bv", "biv", "bo")], axis=1),
        "wall": wall,
        "wf": a["L0_mix_Wf"].T,
        "wr": a["L0_ffn_Wr"].reshape(KT, P, NE).transpose(1, 0, 2),
        "br": np.broadcast_to(a["L0_ffn_br"], (P, NE)),
        "wffn": wffn,
        "bffn": np.concatenate([a["L0_ffn_b1"].reshape(NE, FT, P), a["L0_ffn_b2"].reshape(NE, KT, P)], axis=1).transpose(2, 0, 1),
    }
    arrays = {f"in_{k}": np.ascontiguousarray(v) for k, v in arrays.items()}
    nc = bacc.Bacc("TRN2", target_bir_lowering=False, num_devices=1)
    aps = {k[3:]: nc.dram_tensor(k, v.shape, mybir.dt.from_np(v.dtype), kind="ExternalInput").ap() for k, v in arrays.items()}
    yrows = nc.dram_tensor("yrows", (NE * C, DM), F32, kind="Internal").ap()
    out = nc.dram_tensor("out", (NT, P, DM), F32, kind="ExternalOutput").ap()
    build(nc, **aps, yrows=yrows, out=out)
    r = run_bass_kernel_spmd(nc, [arrays], core_ids=[0])
    return r.results[0]["out"].reshape(N, DM)
```
